# Optimizing a Trainium2 kernel written in Bass

```python
import numpy as np
import jax
import jax.numpy as jnp

def _softmax(x, axis=-1):
    return jax.nn.softmax(x, axis=axis)

def _gelu(x):
    return jax.nn.gelu(x, approximate=True)

def _silu(x):
    return jax.nn.silu(x)

def _sigmoid(x):
    return jax.nn.sigmoid(x)

def _layernorm(x, axis=-1, eps=1e-05):
    m = jnp.mean(x, axis=axis, keepdims=True)
    v = jnp.var(x, axis=axis, keepdims=True)
    return (x - m) / jnp.sqrt(v + eps)

def _scatter_add(tgt, idx, src, axis=0):
    return tgt.at[idx].add(src)

def _segment_sum(src, seg, n):
    return jax.ops.segment_sum(src, seg, n)
kernel_name = 'mk_gnn_resnorm_d2_gnn_r32_5b5147'

def setup_inputs(seed: int=0):
    np.random.seed(seed)
    _w = jnp.asarray

    def _rec_inputs():
        import jax
        import jax.numpy as jnp
        _gk = jax.random.key(seed)
        x = -0.0006008 + 1.001 * jax.random.normal(jax.random.fold_in(_gk, 1), (50000, 256), jnp.float32)
        src = jax.random.randint(jax.random.fold_in(_gk, 2), (25000,), 0, 50000, jnp.int32)
        dst = jnp.minimum((50000 * jax.random.uniform(jax.random.fold_in(_gk, 3), (25000,)) ** 2.0).astype(jnp.int32), 49999)
        _o = jnp.argsort(dst, stable=True)
        src = src[_o]
        dst = dst[_o]
        edge_attr_256 = -4.21973e-05 + 0.999841 * jax.random.normal(jax.random.fold_in(_gk, 13), (25000, 256), jnp.float32)
        return (x, src, dst, edge_attr_256)
    x, src, dst, edge_attr_256 = _rec_inputs()

    def _L0_gnn_setup():
        import jax, jax.numpy as jnp
        import numpy as np
        N_NODES = 10000
        N_EDGES = 10000
        D = 256
        key = jax.random.key(seed)
        k1, k2, k3, k4, k5 = jax.random.split(key, 5)
        x = jax.random.normal(k1, (N_NODES, D), dtype=jnp.float32)
        src = jax.random.randint(k2, (N_EDGES,), 0, N_NODES, dtype=jnp.int32)
        dst = jax.random.randint(k3, (N_EDGES,), 0, N_NODES, dtype=jnp.int32)
        s = 1.0 / np.sqrt(D)
        theta_w = jax.random.uniform(k4, (D, D), jnp.float32, -s, s)
        theta_b = jnp.zeros((D,), jnp.float32)
        phi_w = jax.random.uniform(k5, (D, D), jnp.float32, -s, s)
        phi_b = jnp.zeros((D,), jnp.float32)
        return {'x': x, 'src': src, 'dst': dst, 'theta_w': theta_w, 'theta_b': theta_b, 'phi_w': phi_w, 'phi_b': phi_b}
    _L0_gnn_all = _L0_gnn_setup()
    _L0_gnn_in = {k: v for k, v in _L0_gnn_all.items() if k in ('theta_w', 'theta_b', 'phi_w', 'phi_b')}
    del _L0_gnn_all

    def _L1_gnn_setup():
        import jax, jax.numpy as jnp
        import numpy as np
        N, E, D_IN, D_OUT = (50000, 9375, 256, 256)
        BN_EPS = 1e-05

        def ccorr(a, b):
            return jnp.fft.irfft(jnp.conj(jnp.fft.rfft(a, axis=-1)) * jnp.fft.rfft(b, axis=-1), n=a.shape[-1], axis=-1)
        key = jax.random.key(seed)
        ks = jax.random.split(key, 8)
        return {'node_ft': jax.random.normal(ks[0], (N, D_IN), dtype=jnp.float32), 'edge_ft': jax.random.normal(ks[1], (E, D_IN), dtype=jnp.float32), 'norm': jax.random.uniform(ks[2], (N, 1), dtype=jnp.float32), 'w_loop': jax.random.normal(ks[3], (D_IN, D_OUT), dtype=jnp.float32) * (1.414 / np.sqrt(D_IN)), 'w_in': jax.random.normal(ks[4], (D_IN, D_OUT), dtype=jnp.float32) * (1.414 / np.sqrt(D_IN)), 'loop_rel': jax.random.normal(ks[5], (1, D_IN), dtype=jnp.float32), 'w_bias': jnp.zeros((D_OUT,), dtype=jnp.float32), 'bn_gamma': jnp.ones((D_OUT,), dtype=jnp.float32), 'bn_beta': jnp.zeros((D_OUT,), dtype=jnp.float32), 'src': jax.random.randint(ks[6], (E,), 0, N, dtype=jnp.int32), 'dst': jax.random.randint(ks[7], (E,), 0, N, dtype=jnp.int32)}
    _L1_gnn_all = _L1_gnn_setup()
    _L1_gnn_in = {k: v for k, v in _L1_gnn_all.items() if k in ('w_loop', 'w_in', 'loop_rel', 'w_bias', 'bn_gamma', 'bn_beta')}
    del _L1_gnn_all
    return {'x': x, 'src': src, 'dst': dst, 'edge_attr_256': edge_attr_256, 'L0_gnn_theta_w': _L0_gnn_in['theta_w'], 'L0_gnn_theta_b': _L0_gnn_in['theta_b'], 'L0_gnn_phi_w': _L0_gnn_in['phi_w'], 'L0_gnn_phi_b': _L0_gnn_in['phi_b'], 'L1_gnn_w_loop': _L1_gnn_in['w_loop'], 'L1_gnn_w_in': _L1_gnn_in['w_in'], 'L1_gnn_loop_rel': _L1_gnn_in['loop_rel'], 'L1_gnn_w_bias': _L1_gnn_in['w_bias'], 'L1_gnn_bn_gamma': _L1_gnn_in['bn_gamma'], 'L1_gnn_bn_beta': _L1_gnn_in['bn_beta']}

def reference(x, src, dst, edge_attr_256, L0_gnn_theta_w, L0_gnn_theta_b, L0_gnn_phi_w, L0_gnn_phi_b, L1_gnn_w_loop, L1_gnn_w_in, L1_gnn_loop_rel, L1_gnn_w_bias, L1_gnn_bn_gamma, L1_gnn_bn_beta):
    import jax
    import jax.numpy as jnp

    def _L0_gnn_ref(x, src, dst, theta_w, theta_b, phi_w, phi_b):
        import jax, jax.numpy as jnp
        import numpy as np
        N_NODES = 10000
        N_EDGES = 10000
        D = 256
        x_src = x[src]
        x_dst = x[dst]
        theta_x = (x_dst - x_src) @ theta_w.T + theta_b
        phi_x = x_src @ phi_w.T + phi_b
        e = jax.nn.relu(theta_x + phi_x)
        out = jax.ops.segment_max(e, dst, num_segments=x.shape[0])
        return jnp.where(jnp.isfinite(out), out, 0.0)

    def _L1_gnn_ref(node_ft, edge_ft, norm, w_loop, w_in, loop_rel, w_bias, bn_gamma, bn_beta, src, dst):
        import jax, jax.numpy as jnp
        import numpy as np
        N, E, D_IN, D_OUT = (50000, 9375, 256, 256)
        BN_EPS = 1e-05

        def ccorr(a, b):
            return jnp.fft.irfft(jnp.conj(jnp.fft.rfft(a, axis=-1)) * jnp.fft.rfft(b, axis=-1), n=a.shape[-1], axis=-1)
        n_nodes = node_ft.shape[0]
        loop_msg = ccorr(node_ft, loop_rel) @ w_loop
        msg = ccorr(node_ft[src], edge_ft) @ w_in
        agg = jax.ops.segment_sum(msg, dst, num_segments=n_nodes) * norm
        h = agg + w_bias + loop_msg
        mean = jnp.mean(h, axis=0)
        var = jnp.var(h, axis=0)
        h = (h - mean) * jax.lax.rsqrt(var + BN_EPS) * bn_gamma + bn_beta
        return jnp.tanh(h)
    deg = jnp.maximum(jax.ops.segment_sum(jnp.ones(dst.shape, jnp.float32), dst, num_segments=50000), 1.0)
    deg_isqrt = deg ** (-0.5)
    x = _layernorm(x + _L0_gnn_ref(x, src, dst, L0_gnn_theta_w, L0_gnn_theta_b, L0_gnn_phi_w, L0_gnn_phi_b), axis=-1)
    x = _layernorm(x + _L1_gnn_ref(x, edge_attr_256, deg_isqrt[:, None], L1_gnn_w_loop, L1_gnn_w_in, L1_gnn_loop_rel, L1_gnn_w_bias, L1_gnn_bn_gamma, L1_gnn_bn_beta, src, dst), axis=-1)
    return x

_drawn_inputs = setup_inputs


def setup_inputs(seed=0):
    import zlib

    import numpy as np

    out = dict(_drawn_inputs(seed))
    spreads = {'L0_gnn_theta_b': (0.0, 0.1),
     'L0_gnn_phi_b': (0.0, 0.1),
     'L1_gnn_w_bias': (0.0, 0.1),
     'L1_gnn_bn_gamma': (1.0, 0.2),
     'L1_gnn_bn_beta': (0.0, 0.1)}
    factors = {}
    for name, (base, spread) in spreads.items():
        noise = np.random.default_rng([zlib.crc32(name.encode()), seed]).standard_normal(out[name].shape)
        drawn = base * np.exp(spread * noise) if base else spread * noise
        out[name] = jnp.asarray(drawn.astype(out[name].dtype))
    for name, factor in factors.items():
        out[name] = (out[name] * factor).astype(out[name].dtype)
    return out
```

```python
import concourse.bass as bass
from concourse import mybir
from concourse.bass import ds
from contextlib import ExitStack

F32 = mybir.dt.float32
BF16 = mybir.dt.bfloat16
I32 = mybir.dt.int32
ALU = mybir.AluOpType
ACT = mybir.ActivationFunctionType
AX = mybir.AxisListType

P = 128
J = 4
TILE = P * J
HUGE = 3.38e38
MISSING = 1 << 20
EPS = 1e-5


def need(eng, sem, value):
    if isinstance(value, int) and value <= 0:
        return
    eng.wait_ge(sem, value)


def pipelined(eng, tiles, stages):
    depth = max(lag for lag, _ in stages)
    first = 2 + depth + depth % 2
    pairs = (tiles - 1 - first) // 2

    def straight(t):
        for lag, step in stages:
            k = t - lag
            if 0 <= k < tiles:
                step(k, k // 2, k % 2, k == tiles - 1)

    for t in range(min(first, tiles + depth)):
        straight(t)
    if pairs > 0:
        with eng.Fori(0, pairs) as i:
            for u in range(2):
                for lag, step in stages:
                    k = first + u - lag
                    step(i * 2 + k, i + k // 2, k % 2, False)
    for t in range(first + 2 * max(pairs, 0), tiles + depth):
        straight(t)


def gnn_kernel(nc, x, src, dst, edge_attr, theta_t, theta_b, phi_t, phi_b, w_loop, w_in, loop_rel2,
               w_bias, bn_gamma, bn_beta, identity, upper, dft, idft_t, sigma, out):
    N, D = x.shape
    E = src.shape[0]
    C = D // P
    assert D == 256 and N % J == 0
    NT = -(-N // TILE)
    TP = (N - (NT - 1) * TILE) // J
    ET = -(-E // TILE)
    EP = ET * TILE
    EC = EP // P
    ER = EP // D
    HC = EC // 2
    assert EC % 2 == 0 and HC <= P and ER <= P
    NQ = NT * J
    PAD_DST = (NT + 16) * TILE

    dst_pad = nc.dram_tensor("dst_pad", (1 + EP,), I32, kind="Internal").ap()
    src_pad = nc.dram_tensor("src_pad", (EP,), I32, kind="Internal").ap()
    edge_pad = nc.dram_tensor("edge_pad", (EP,), I32, kind="Internal").ap()
    cap_row = nc.dram_tensor("cap_row", (EP,), BF16, kind="Internal").ap()
    keep_row = nc.dram_tensor("keep_row", (EP,), BF16, kind="Internal").ap()
    max_rows = nc.dram_tensor("max_rows", (EP, D), F32, kind="Internal").ap()
    agg_rows = nc.dram_tensor("agg_rows", (EP, D), F32, kind="Internal").ap()
    x1 = nc.dram_tensor("x1", (N, D), F32, kind="Internal").ap()
    h_t = nc.dram_tensor("h_t", (NT, P, C * TILE), F32, kind="Internal").ap()

    def node_rows(table, t, last):
        rows = TP * J if last else TILE
        return table[ds(t * TILE, rows), :].rearrange("(p j) c -> p j c", j=J)

    def edge_rows(table, t):
        return table[ds(t * TILE, TILE), :].rearrange("(p j) c -> p j c", j=J)

    ctx = ExitStack()
    with ctx:
        def sb(name, shape, dt=F32, at=ctx):
            return at.enter_context(nc.sbuf_tensor(name, shape, dt))

        def ps(name, shape, at):
            return at.enter_context(nc.psum_tensor(name, shape, F32))

        def sem(name):
            return ctx.enter_context(nc.semaphore(name))

        ident = sb("ident", [P, P])
        up = sb("up", [P, P])
        ones = sb("ones", [P, P])
        sig = sb("sig", [P, 1])
        w_dst = sb("w_dst", [P, C, D])
        w_src = sb("w_src", [P, C, D])
        dft_sb = sb("dft_sb", [P, C, D])
        w_h = sb("w_h", [P, C, D])
        w_msg = sb("w_msg", [P, C, D])
        bias_col = sb("bias_col", [P, C])
        wb_col = sb("wb_col", [P, C])
        gam_col = sb("gam_col", [P, C])
        bet_col = sb("bet_col", [P, C])
        eps_col = sb("eps_col", [P, 1])
        src_cols = sb("src_cols", [P, EC], I32)
        edge_cols = sb("edge_cols", [P, EC], I32)
        dst_p = sb("dst_p", [P, EC])
        dst_q = sb("dst_q", [P, EC])
        deg = sb("deg", [P, NQ])
        ptr = sb("ptr", [P, NQ], I32)
        cap_node = sb("cap_node", [P, NQ])
        norm_node = sb("norm_node", [P, NQ])
        h_stats = sb("h_stats", [P, C, NT * 6])
        bn_scale = sb("bn_scale", [P, C])
        bn_shift = sb("bn_shift", [P, C])
        idx = sb("idx", [P, 2, 2, J], I32)

        loaded = sem("loaded")
        loaded_w = sem("loaded_w")
        dst_written = sem("dst_written")
        idx_loaded = sem("idx_loaded")
        prep_v = sem("prep_v")
        prep_t = sem("prep_t")
        pads_ready = sem("pads_ready")
        masks_ready = sem("masks_ready")
        masks_stored = sem("masks_stored")
        prev_loaded = sem("prev_loaded")
        prep_done = sem("prep_done")
        small = ExitStack()
        with small, nc.Block() as block:
            raw_phi = sb("raw_phi", [P, C, D], at=small)
            hankel = sb("hankel", [P, C, D], at=small)
            wl = sb("wl", [P, C, D], at=small)
            wi = sb("wi", [P, C, D], at=small)
            idft_sb = sb("idft_sb", [P, C, D], at=small)
            b_col = sb("b_col", [P, 2, C], at=small)
            first_d = sb("first_d", [1, 1], I32, at=small)
            pad_d = sb("pad_d", [1, EP - E], I32, at=small)
            pad_s = sb("pad_s", [1, EP - E], I32, at=small)
            e_iota = sb("e_iota", [ER, D], I32, at=small)
            e_idx = sb("e_idx", [ER, D], I32, at=small)
            d_now = sb("d_now", [ER, D], I32, at=small)
            d_before = sb("d_before", [ER, D], I32, at=small)
            keep = sb("keep", [ER, D], BF16, at=small)
            cap = sb("cap", [ER, D], BF16, at=small)
            ints = sb("ints", [HC, 3, 2, P], I32, at=small)
            floats = sb("floats", [HC, 3, 2, P], at=small)
            dst_cols = sb("dst_cols", [P, EC], I32, at=small)
            t_a = sb("t_a", [P, EC], I32, at=small)
            t_b = sb("t_b", [P, EC], I32, at=small)
            ps_w = ps("ps_w", [P, 2, C, D], small)
            ps_i = ps("ps_i", [P, 3, 512], small)

            @block.sync
            def _(sp):
                def chunks(w):
                    return w.rearrange("(c p) n -> p c n", p=P)

                sp.dma_start(dst_pad[1:1 + E], dst).then_inc(dst_written, 16)
                sp.dma_start(src_pad[0:E], src).then_inc(dst_written, 16)
                sp.wait_ge(pads_ready, 1)
                sp.dma_start(dst_pad[0:1], first_d[0:1, 0:1]).then_inc(dst_written, 16)
                sp.dma_start(dst_pad[1 + E:], pad_d[0:1, :]).then_inc(dst_written, 16)
                sp.dma_start(src_pad[E:], pad_s[0:1, :]).then_inc(dst_written, 16)
                sp.dma_start(edge_pad.rearrange("(r c) -> r c", c=D), e_idx[:, :]).then_inc(dst_written, 16)
                for dest, w in ((w_dst, theta_t), (raw_phi, phi_t), (wl, w_loop), (wi, w_in),
                                (dft_sb, dft), (idft_sb, idft_t)):
                    sp.dma_start(dest[:, :, :], chunks(w)).then_inc(loaded_w, 16)
                sp.dma_start(ident[:, :], identity).then_inc(loaded, 16)
                sp.dma_start(up[:, :], upper).then_inc(loaded, 16)
                sp.dma_start(sig[:, :], sigma).then_inc(loaded, 16)
                for dest, v in ((b_col[:, 0, :], theta_b), (b_col[:, 1, :], phi_b), (wb_col[:, :], w_bias),
                                (gam_col[:, :], bn_gamma), (bet_col[:, :], bn_beta)):
                    for c in range(C):
                        sp.dma_start(dest[:, c:c + 1], v[c * P:(c + 1) * P].rearrange("(p o) -> p o", o=1)
                                     ).then_inc(loaded, 16)
                for c in range(C):
                    win = bass.AP(loop_rel2.tensor, c * P, [[1, P], [1, D]])
                    sp.dma_start(hankel[:, c, :], win).then_inc(loaded_w, 16)
                sp.wait_ge(dst_written, 6 * 16)
                sp.dma_start(d_now[:, :], dst_pad[1:1 + EP].rearrange("(r c) -> r c", c=D)).then_inc(prev_loaded, 16)
                sp.dma_start(d_before[:, :], dst_pad[0:EP].rearrange("(r c) -> r c", c=D)).then_inc(prev_loaded, 16)
                for n, v in enumerate((src_pad, edge_pad, dst_pad[1:1 + EP])):
                    sp.dma_start(ints[:, n, :, :], v.rearrange("(h r c) -> r h c", h=2, c=P)).then_inc(idx_loaded, 16)
                sp.wait_ge(masks_ready, 1)
                sp.dma_start(keep_row.rearrange("(r c) -> r c", c=D), keep[:, :]).then_inc(masks_stored, 16)
                sp.dma_start(cap_row.rearrange("(r c) -> r c", c=D), cap[:, :]).then_inc(masks_stored, 16)
                sp.wait_ge(masks_stored, 32)

            @block.gpsimd
            def _(pool):
                nc.gpsimd.iota(e_iota[:, :], [[1, D]], base=0, channel_multiplier=D).then_inc(prep_done, 1)

            @block.vector
            def _(dve):
                v = nc.vector
                v.memset(first_d[:, :], -1)
                v.memset(pad_d[:, :], PAD_DST)
                v.memset(pad_s[:, :], 0)
                dve.wait_ge(prep_done, 1)
                v.tensor_scalar(out=e_idx[:, :], in0=e_iota[:, :], scalar1=float(E - 1), scalar2=None,
                                op0=ALU.min).then_inc(pads_ready, 1)
                v.memset(ones[:, :], 1.0)
                v.memset(eps_col[:, :], EPS)
                v.memset(idx[:, :, :, :], 0)
                dve.wait_ge(loaded_w, 16 * (6 + C))
                v.tensor_tensor(out=w_src[:, :, :], in0=raw_phi[:, :, :], in1=w_dst[:, :, :],
                                op=ALU.subtract)
                dve.wait_ge(loaded, 16 * (3 + 5 * C))
                v.tensor_tensor(out=bias_col[:, :], in0=b_col[:, 0, :], in1=b_col[:, 1, :], op=ALU.add)
                dve.wait_ge(prev_loaded, 32)
                v.tensor_tensor(out=keep[:, :], in0=d_now[:, :], in1=d_before[:, :],
                                op=ALU.is_equal).then_inc(prep_v, 1)
                dve.wait_ge(prep_v, 1)
                v.tensor_scalar(out=cap[:, :], in0=keep[:, :], scalar1=2.0, scalar2=1.0, op0=ALU.mult,
                                op1=ALU.subtract).then_inc(prep_v, 1)
                dve.wait_ge(prep_v, 2)
                v.tensor_scalar(out=cap[:, :], in0=cap[:, :], scalar1=HUGE, scalar2=None,
                                op0=ALU.mult).then_inc(masks_ready, 1)
                dve.wait_ge(idx_loaded, 48)
                v.tensor_copy(out=floats[:, :, :, :], in_=ints[:, :, :, :]).then_inc(prep_v, 1)
                dve.wait_ge(prep_t, 1)
                v.tensor_copy(out=src_cols[:, :], in_=ps_i[:, 0, 0:EC])
                v.tensor_copy(out=edge_cols[:, :], in_=ps_i[:, 1, 0:EC])
                v.tensor_copy(out=dst_cols[:, :], in_=ps_i[:, 2, 0:EC]).then_inc(prep_v, 1)
                dve.wait_ge(prep_v, 4)
                v.tensor_scalar(out=t_a[:, :], in0=dst_cols[:, :], scalar1=2, scalar2=P - 1,
                                op0=ALU.logical_shift_right, op1=ALU.bitwise_and).then_inc(prep_v, 1)
                dve.wait_ge(prep_v, 5)
                v.tensor_copy(out=dst_p[:, :], in_=t_a[:, :]).then_inc(prep_v, 1)
                dve.wait_ge(prep_v, 6)
                v.tensor_scalar(out=t_a[:, :], in0=dst_cols[:, :], scalar1=9, scalar2=2,
                                op0=ALU.logical_shift_right, op1=ALU.logical_shift_left)
                v.tensor_scalar(out=t_b[:, :], in0=dst_cols[:, :], scalar1=J - 1, scalar2=None,
                                op0=ALU.bitwise_and).then_inc(prep_v, 1)
                dve.wait_ge(prep_v, 7)
                v.tensor_tensor(out=t_a[:, :], in0=t_a[:, :], in1=t_b[:, :], op=ALU.bitwise_or).then_inc(prep_v, 1)
                dve.wait_ge(prep_v, 8)
                v.tensor_copy(out=dst_q[:, :], in_=t_a[:, :])
                dve.wait_ge(prep_t, 3)
                v.tensor_copy(out=w_h[:, :, :], in_=ps_w[:, 0, :, :])
                v.tensor_copy(out=w_msg[:, :, :], in_=ps_w[:, 1, :, :])

            @block.tensor
            def _(pe):
                pe.wait_ge(loaded, 16 * (3 + 5 * C))
                pe.wait_ge(prep_v, 3)
                for n in range(3):
                    for half in range(2):
                        last = nc.tensor.transpose(ps_i[:, n, half * HC:(half + 1) * HC],
                                                   floats[:, n, half, :], ident[0:HC, 0:HC])
                last.then_inc(prep_t, 1)
                pe.wait_ge(loaded_w, 16 * (6 + C))
                for n, (left, right) in enumerate(((hankel, wl), (idft_sb, wi))):
                    for m in range(C):
                        for c in range(C):
                            last = nc.tensor.matmul(ps_w[:, n, m, :], left[:, c, m * P:(m + 1) * P],
                                                    right[:, c, :], start=(c == 0), stop=(c == C - 1))
                    last.then_inc(prep_t, 1)

        gathers_begun = sem("gathers_begun")

        def stage_indices(pool, ring, cols, t, s, staged, count):
            nc.gpsimd.tensor_copy(out=idx[:, ring, s, :], in_=cols[:, ds(t * J, J)]).then_inc(staged, 1)
            pool.wait_ge(staged, count)
            pool.sem_inc(gathers_begun, 1)

        def gather(table, bound, dest, ring, s, done):
            for j in range(J):
                nc.gpsimd.indirect_dma_start(
                    out=dest[:, j, :], out_offset=None, in_=table,
                    in_offset=bass.IndirectOffsetOnAxis(ap=idx[:, ring, s, j:j + 1], axis=0),
                    bounds_check=bound, oob_is_err=False).then_inc(done, 16)

        def transpose_rows(rows, dest, c, n):
            for j in range(J):
                last = nc.tensor.transpose(dest[:, c, j * P:j * P + n], rows[0:n, j, c * P:(c + 1) * P],
                                           ident[0:n, 0:n])
            return last

        def transpose_back(cols, dest, c, n):
            for j in range(J):
                last = nc.tensor.transpose(dest[0:n, j, c * P:(c + 1) * P], cols[:, c, j * P:j * P + n],
                                           ident[:, :])
            return last

        def part(cols, c, n):
            if n == P:
                return cols[:, c, :]
            return cols[:, c, :].rearrange("p (j n) -> p j n", j=J)[:, :, 0:n]

        a_idx = sem("a_idx")
        a_src = [sem(f"a_src{s}") for s in range(2)]
        a_cap = [sem(f"a_cap{s}") for s in range(2)]
        a_st = [sem(f"a_st{s}") for s in range(2)]
        a_iota = sem("a_iota")
        a_xt = sem("a_xt")
        a_xtc = sem("a_xtc")
        a_b = sem("a_b")
        a_bc = sem("a_bc")
        a_scan = sem("a_scan")
        a_back = sem("a_back")
        a_rows = sem("a_rows")
        a_hot = sem("a_hot")
        a_cnt = sem("a_cnt")
        a_init = sem("a_init")
        c_v = sem("c_v")
        c_t = sem("c_t")
        c_s = sem("c_s")
        mem = ExitStack()
        with mem, nc.Block() as block:
            iota_q = sb("iota_q", [P, NQ], at=mem)
            iota_p = sb("iota_p", [P, P], at=mem)
            xs = sb("xs", [P, 2, J, D], at=mem)
            xt = sb("xt", [P, 2, C, TILE], at=mem)
            bt = sb("bt", [P, 2, C, TILE], at=mem)
            caps = sb("caps", [P, 2, TILE], BF16, at=mem)
            mx = sb("mx", [P, 2, C, TILE], at=mem)
            rows = sb("rows", [P, 2, J, D], at=mem)
            hot_q = sb("hot_q", [P, 2, NQ], BF16, at=mem)
            hot_p = sb("hot_p", [P, 2, P], BF16, at=mem)
            ps_x = ps("ps_x", [P, C, TILE], mem)
            ps_b = ps("ps_b", [P, C, TILE], mem)
            ps_r = ps("ps_r", [P, J, D], mem)
            ps_n = ps("ps_n", [P, 512], mem)

            @block.gpsimd
            def _(pool):
                nc.gpsimd.iota(iota_q[:, :], [[1, NQ]], base=0, channel_multiplier=0,
                               allow_small_or_imprecise_dtypes=True)
                nc.gpsimd.iota(iota_p[:, :], [[1, P]], base=0, channel_multiplier=0,
                               allow_small_or_imprecise_dtypes=True).then_inc(a_iota, 1)

                b_x = nc.gpsimd.to_reg(x.shape[0] - 1)

                def gather_src(t, h, s, last):
                    need(pool, a_src[s], h * J * 16)
                    need(pool, a_xt, (t - 1) * C)
                    stage_indices(pool, 0, src_cols, t, s, a_idx, t + 1)
                    gather(x, b_x, xs[:, s, :, :], 0, s, a_src[s])

                pipelined(pool, ET, [(0, gather_src)])

            @block.sync
            def _(sp):
                def load_caps(t, h, s, last):
                    need(sp, a_scan, (t - 1) * C)
                    sp.dma_start(caps[:, s, :], cap_row[ds(t * TILE, TILE)].partition_broadcast(P)
                                 ).then_inc(a_cap[s], 16)

                def store_rows(t, h, s, last):
                    sp.wait_ge(a_rows, (t + 1) * 2)
                    sp.dma_start(edge_rows(max_rows, t), rows[:, s, :, :]).then_inc(a_st[s], 16)

                pipelined(sp, ET, [(0, load_caps), (2, store_rows)])
                for s in range(2):
                    sp.wait_ge(a_st[s], ((ET + 1 - s) // 2) * 16)

            @block.tensor
            def _(pe):
                def turn(t, h, s, last):
                    pe.wait_ge(a_src[s], (h + 1) * J * 16)
                    need(pe, a_xtc, t * C)
                    for c in range(C):
                        transpose_rows(xs[:, s, :, :], ps_x, c, P).then_inc(a_xt, 1)

                def count(t, h, s, last):
                    for j in range(J):
                        pe.wait_ge(a_hot, t * J + j + 1)
                        nc.tensor.matmul(ps_n[:, 0:NQ], hot_p[:, j % 2, :], hot_q[:, j % 2, :],
                                         start=(isinstance(t, int) and t == 0 and j == 0),
                                         stop=(last and j == J - 1)).then_inc(a_cnt, 1)

                def project(t, h, s, last):
                    for m in range(C):
                        need(pe, a_bc, (t - 1) * C + m + 1)
                        for c in range(C):
                            if m == 0:
                                pe.wait_ge(a_xtc, t * C + c + 1)
                            mm = nc.tensor.matmul(ps_b[:, m, :], w_src[:, c, m * P:(m + 1) * P],
                                                  xt[:, s, c, :], start=(c == 0), stop=(c == C - 1))
                        mm.then_inc(a_b, 1)

                def back(t, h, s, last):
                    need(pe, a_rows, t * 2)
                    pe.wait_ge(a_scan, (t + 1) * C)
                    for c in range(C):
                        mm = transpose_back(mx[:, s, :, :], ps_r, c, P)
                    mm.then_inc(a_back, 1)

                pipelined(pe, ET, [(0, turn), (1, project), (1, count), (2, back)])
                pe.wait_ge(c_v, 2)
                nc.tensor.matmul(ps_x[:, 0, 0:NT], ones[:, :], mx[:, 0, 0, 0:NT], start=True, stop=True)
                nc.tensor.matmul(ps_x[:, 1, 0:NT], up[:, :], mx[:, 0, 0, 0:NT], start=True,
                                 stop=True).then_inc(c_t, 1)

            @block.scalar
            def _(act):
                def copy_xt(t, h, s, last):
                    need(act, a_b, (t - 1) * C)
                    for c in range(C):
                        act.wait_ge(a_xt, t * C + c + 1)
                        nc.scalar.activation(xt[:, s, c, :], ps_x[:, c, :], ACT.Copy).then_inc(a_xtc, 1)

                def add_bias(t, h, s, last):
                    need(act, a_scan, (t - 1) * C)
                    for m in range(C):
                        act.wait_ge(a_b, t * C + m + 1)
                        nc.scalar.activation(bt[:, s, m, :], ps_b[:, m, :], ACT.Identity,
                                             bias=bias_col[:, m:m + 1]).then_inc(a_bc, 1)

                def copy_rows(t, h, s, last):
                    act.wait_ge(a_back, t + 1)
                    need(act, a_st[s], h * 16)
                    for k in range(2):
                        nc.scalar.activation(rows[:, s, 2 * k:2 * k + 2, :], ps_r[:, 2 * k:2 * k + 2, :],
                                             ACT.Copy).then_inc(a_rows, 1)

                pipelined(act, ET, [(0, copy_xt), (1, add_bias), (2, copy_rows)])
                act.wait_ge(c_v, 4)
                nc.scalar.activation(norm_node[:, :], norm_node[:, :], ACT.Sqrt).then_inc(c_s, 1)

            @block.vector
            def _(dve):
                v = nc.vector
                v.memset(mx[:, 1, :, TILE - 1:TILE], -HUGE).then_inc(a_init, 1)
                dve.wait_ge(a_init, 1)
                dve.wait_ge(a_iota, 1)

                def one_hots(t, h, s, last):
                    for j in range(J):
                        need(dve, a_cnt, t * J + j - 1)
                        col = t * J + j
                        v.tensor_scalar(out=hot_q[:, j % 2, :], in0=iota_q[:, :], scalar1=dst_q[:, ds(col, 1)],
                                        scalar2=None, op0=ALU.is_equal)
                        v.tensor_scalar(out=hot_p[:, j % 2, :], in0=iota_p[:, :], scalar1=dst_p[:, ds(col, 1)],
                                        scalar2=None, op0=ALU.is_equal).then_inc(a_hot, 1)

                def running_max(t, h, s, last):
                    need(dve, a_back, t - 1)
                    need(dve, a_scan, t * C)
                    dve.wait_ge(a_cap[s], (h + 1) * 16)
                    for m in range(C):
                        dve.wait_ge(a_bc, t * C + m + 1)
                        v.tensor_tensor_scan(out=mx[:, s, m, :], data0=caps[:, s, :], data1=bt[:, s, m, :],
                                             initial=mx[:, 1 - s, m, TILE - 1:TILE], op0=ALU.min,
                                             op1=ALU.max).then_inc(a_scan, 1)

                pipelined(dve, ET, [(0, one_hots), (1, running_max)])

                done = [0]

                def link(ins):
                    done[0] += 1
                    ins.then_inc(c_v, 1)
                    dve.wait_ge(c_v, done[0])

                tot = mx[:, 0, 0, 0:NT]
                every = mx[:, 0, 1, 0:NT]
                base = mx[:, 1, 0, 0:NT]
                ends = xt[:, 0, :, :].rearrange("p c n -> p (c n)")[:, 0:NQ]
                e4 = ends.rearrange("p (i j) -> p i j", j=J)
                d4 = deg[:, :].rearrange("p (i j) -> p i j", j=J)
                i_a = bt[:, 0, :, :].rearrange("p c n -> p (c n)")[:, 0:NQ].bitcast(I32)
                i_b = bt[:, 1, :, :].rearrange("p c n -> p (c n)")[:, 0:NQ].bitcast(I32)
                i_c = xs[:, 0, :, :].rearrange("p c n -> p (c n)")[:, 0:NQ].bitcast(I32)
                dve.wait_ge(a_back, ET)
                dve.wait_ge(a_cnt, ET * J)
                link(v.tensor_copy(out=deg[:, :], in_=ps_n[:, 0:NQ]))
                link(v.tensor_reduce(out=tot, in_=d4, axis=AX.X, op=ALU.add))
                link(v.tensor_scalar(out=cap_node[:, :], in0=deg[:, :], scalar1=1.0, scalar2=None, op0=ALU.min))
                link(v.tensor_scalar(out=norm_node[:, :], in0=deg[:, :], scalar1=1.0, scalar2=None, op0=ALU.max))
                dve.wait_ge(c_t, 1)
                link(v.tensor_tensor_scan(out=every, data0=ones[:, 0:NT], data1=ps_x[:, 0, 0:NT], initial=0.0,
                                          op0=ALU.mult, op1=ALU.add))
                link(v.tensor_tensor(out=every, in0=every, in1=ps_x[:, 0, 0:NT], op=ALU.subtract))
                link(v.tensor_tensor(out=base, in0=every, in1=ps_x[:, 1, 0:NT], op=ALU.add))
                link(v.tensor_scalar(out=base, in0=base, scalar1=1.0, scalar2=None, op0=ALU.subtract))
                link(v.tensor_tensor(out=e4[:, :, 0], in0=base, in1=d4[:, :, 0], op=ALU.add))
                for j in range(1, J):
                    link(v.tensor_tensor(out=e4[:, :, j], in0=e4[:, :, j - 1], in1=d4[:, :, j], op=ALU.add))
                link(v.tensor_scalar(out=i_a, in0=ends, scalar1=0.0, scalar2=None, op0=ALU.max))
                link(v.tensor_scalar(out=i_b, in0=i_a, scalar1=9, scalar2=9, op0=ALU.logical_shift_right,
                                     op1=ALU.logical_shift_left))
                link(v.tensor_scalar(out=i_c, in0=i_a, scalar1=P - 1, scalar2=2, op0=ALU.bitwise_and,
                                     op1=ALU.logical_shift_left))
                link(v.tensor_tensor(out=i_b, in0=i_b, in1=i_c, op=ALU.bitwise_or))
                link(v.tensor_scalar(out=i_c, in0=i_a, scalar1=7, scalar2=J - 1, op0=ALU.logical_shift_right,
                                     op1=ALU.bitwise_and))
                link(v.tensor_tensor(out=i_b, in0=i_b, in1=i_c, op=ALU.bitwise_or))
                link(v.tensor_scalar(out=i_c, in0=deg[:, :], scalar1=0.0, scalar2=float(MISSING),
                                     op0=ALU.is_equal, op1=ALU.mult))
                link(v.tensor_tensor(out=ptr[:, :], in0=i_b, in1=i_c, op=ALU.bitwise_or))
                dve.wait_ge(c_s, 1)
                link(v.reciprocal(out=norm_node[:, :], in_=norm_node[:, :]))
                link(v.tensor_tensor(out=norm_node[:, :], in0=norm_node[:, :], in1=cap_node[:, :], op=ALU.mult))
                link(v.tensor_scalar(out=cap_node[:, :], in0=cap_node[:, :], scalar1=2.0, scalar2=1.0,
                                     op0=ALU.mult, op1=ALU.subtract))
                link(v.tensor_scalar(out=cap_node[:, :], in0=cap_node[:, :], scalar1=HUGE, scalar2=None,
                                     op0=ALU.mult))

        def row_variance(dve, y, s6, ms, tmp, n, step, first):
            v = nc.vector
            for j in range(J):
                ins = v.bn_stats(out=s6[0:n, j, :], in_=y[0:n, j, :])
            ins.then_inc(step, 1)
            dve.wait_ge(step, first)
            v.tensor_tensor(out=ms[0:n, 0, :], in0=s6[0:n, :, 1], in1=s6[0:n, :, 4], op=ALU.add)
            v.tensor_tensor(out=tmp[0:n, 0, :], in0=s6[0:n, :, 1], in1=s6[0:n, :, 4], op=ALU.subtract)
            v.tensor_tensor(out=tmp[0:n, 1, :], in0=s6[0:n, :, 2], in1=s6[0:n, :, 5],
                            op=ALU.add).then_inc(step, 1)
            dve.wait_ge(step, first + 1)
            v.scalar_tensor_tensor(out=tmp[0:n, 2, :], in0=tmp[0:n, 0, :], scalar=0.25, in1=tmp[0:n, 0, :],
                                   op0=ALU.mult, op1=ALU.mult).then_inc(step, 1)
            dve.wait_ge(step, first + 2)
            return v.scalar_tensor_tensor(out=ms[0:n, 1, :], in0=tmp[0:n, 1, :], scalar=1.0 / D,
                                          in1=tmp[0:n, 2, :], op0=ALU.mult, op1=ALU.add)

        p_idx = sem("p_idx")
        p_mg = [sem(f"p_mg{s}") for s in range(2)]
        p_x = [sem(f"p_x{s}") for s in range(2)]
        p_st = [sem(f"p_st{s}") for s in range(2)]
        p_xt = sem("p_xt")
        p_xtc = sem("p_xtc")
        p_a = sem("p_a")
        p_sum = sem("p_sum")
        p_res = sem("p_res")
        p_s6 = sem("p_s6")
        p_var = sem("p_var")
        p_sd = sem("p_sd")
        p_rs = sem("p_rs")
        p_nb = sem("p_nb")
        p_y = sem("p_y")
        p_init = sem("p_init")
        mem = ExitStack()
        with mem, nc.Block() as block:
            mg = sb("mg", [P, 2, J, D], at=mem)
            xr = sb("xr", [P, 2, J, D], at=mem)
            xt = sb("p_xt_sb", [P, 2, C, TILE], at=mem)
            act_in = sb("act_in", [P, J, D], at=mem)
            res = sb("res", [P, 2, J, D], at=mem)
            yo = sb("yo", [P, 2, J, D], at=mem)
            s6 = sb("s6", [P, J, 6], at=mem)
            ms = sb("ms", [P, 2, 2, J], at=mem)
            tmp = sb("tmp", [P, 3, J], at=mem)
            sd = sb("sd", [P, 2, J], at=mem)
            rs = sb("rs", [P, 2, J], at=mem)
            nb = sb("nb", [P, 2, J], at=mem)
            ps_x = ps("p_ps_x", [P, C, TILE], mem)
            ps_a = ps("p_ps_a", [P, 2, J, D], mem)

            @block.gpsimd
            def _(pool):
                pool.wait_ge(p_init, 1)

                b_max_rows = nc.gpsimd.to_reg(max_rows.shape[0] - 1)

                def gather_max(t, h, s, last):
                    need(pool, p_mg[s], h * J * 16)
                    need(pool, p_sum, t - 1)
                    stage_indices(pool, 0, ptr, t, s, p_idx, t + 1)
                    gather(max_rows, b_max_rows, mg[:, s, :, :], 0, s, p_mg[s])

                pipelined(pool, NT, [(0, gather_max)])

            @block.sync
            def _(sp):
                def load_x(t, h, s, last):
                    n = TP if last else P
                    need(sp, p_res, t - 1)
                    sp.dma_start(xr[0:n, s, :, :], node_rows(x, t, last)).then_inc(p_x[s], 16)

                def store_x1(t, h, s, last):
                    n = TP if last else P
                    sp.wait_ge(p_y, t + 1)
                    sp.dma_start(node_rows(x1, t, last), yo[0:n, s, :, :]).then_inc(p_st[s], 16)

                pipelined(sp, NT, [(0, load_x), (2, store_x1)])
                for s in range(2):
                    sp.wait_ge(p_st[s], ((NT + 1 - s) // 2) * 16)

            @block.tensor
            def _(pe):
                def turn(t, h, s, last):
                    n = TP if last else P
                    pe.wait_ge(p_x[s], (h + 1) * 16)
                    need(pe, p_xtc, t * C)
                    for c in range(C):
                        transpose_rows(xr[:, s, :, :], ps_x, c, n).then_inc(p_xt, 1)

                def project(t, h, s, last):
                    n = TP if last else P
                    need(pe, p_sum, t - 1)
                    pe.wait_ge(p_xtc, (t + 1) * C)
                    for j in range(J):
                        for c in range(C):
                            mm = nc.tensor.matmul(ps_a[0:n, s, j, :], xt[:, s, c, j * P:j * P + n],
                                                  w_dst[:, c, :], start=(c == 0), stop=(c == C - 1))
                    mm.then_inc(p_a, 1)

                pipelined(pe, NT, [(0, turn), (1, project)])

            @block.scalar
            def _(act):
                def copy_xt(t, h, s, last):
                    n = TP if last else P
                    need(act, p_a, t - 1)
                    for c in range(C):
                        act.wait_ge(p_xt, t * C + c + 1)
                        nc.scalar.activation(part(xt[:, s, :, :], c, n), part(ps_x, c, n),
                                             ACT.Copy).then_inc(p_xtc, 1)

                def root(t, h, s, last):
                    n = TP if last else P
                    act.wait_ge(p_var, t + 1)
                    nc.scalar.activation(sd[0:n, s, :], ms[0:n, s, 1, :], ACT.Sqrt,
                                         bias=eps_col[0:n, :]).then_inc(p_sd, 1)

                def normalise(t, h, s, last):
                    n = TP if last else P
                    act.wait_ge(p_nb, t + 1)
                    need(act, p_st[s], h * 16)
                    for j in range(J):
                        a = nc.scalar.activation(yo[0:n, s, j, :], res[0:n, s, j, :], ACT.Identity,
                                                 bias=nb[0:n, s, j:j + 1], scale=rs[0:n, s, j:j + 1])
                    a.then_inc(p_y, 1)

                pipelined(act, NT, [(0, copy_xt), (1, root), (2, normalise)])

            @block.vector
            def _(dve):
                v = nc.vector
                v.memset(mg[:, :, :, :], 0.0).then_inc(p_init, 1)

                def add_relu(t, h, s, last):
                    n = TP if last else P
                    dve.wait_ge(p_mg[s], (h + 1) * J * 16)
                    dve.wait_ge(p_a, t + 1)
                    for j in range(J):
                        a = v.scalar_tensor_tensor(out=act_in[0:n, j, :], in0=mg[0:n, s, j, :],
                                                   scalar=cap_node[0:n, ds(t * J + j, 1)],
                                                   in1=ps_a[0:n, s, j, :], op0=ALU.min, op1=ALU.add)
                    a.then_inc(p_sum, 1)
                    need(dve, p_y, t - 1)
                    dve.wait_ge(p_sum, t + 1)
                    v.scalar_tensor_tensor(out=res[0:n, s, :, :], in0=act_in[0:n, :, :], scalar=0.0,
                                           in1=xr[0:n, s, :, :], op0=ALU.max, op1=ALU.add).then_inc(p_res, 1)
                    dve.wait_ge(p_res, t + 1)
                    row_variance(dve, res[:, s, :, :], s6, ms[:, s, :, :], tmp, n, p_s6, t * 3 + 1).then_inc(p_var, 1)

                def scales(t, h, s, last):
                    n = TP if last else P
                    dve.wait_ge(p_sd, t + 1)
                    v.reciprocal(out=rs[0:n, s, :], in_=sd[0:n, s, :]).then_inc(p_rs, 1)
                    dve.wait_ge(p_rs, t + 1)
                    v.scalar_tensor_tensor(out=nb[0:n, s, :], in0=ms[0:n, s, 0, :], scalar=-0.5,
                                           in1=rs[0:n, s, :], op0=ALU.mult, op1=ALU.mult).then_inc(p_nb, 1)

                pipelined(dve, NT, [(0, add_relu), (1, scales)])

        b_idx = sem("b_idx")
        b_xs = [sem(f"b_xs{s}") for s in range(2)]
        b_es = [sem(f"b_es{s}") for s in range(2)]
        b_kp = [sem(f"b_kp{s}") for s in range(2)]
        b_st = [sem(f"b_st{s}") for s in range(2)]
        b_xt = sem("b_xt")
        b_xtc = sem("b_xtc")
        b_et = sem("b_et")
        b_etc = sem("b_etc")
        b_fa = sem("b_fa")
        b_fac = sem("b_fac")
        b_fe = sem("b_fe")
        b_prod = sem("b_prod")
        b_z = sem("b_z")
        b_sc = sem("b_sc")
        b_msg = sem("b_msg")
        b_rows = sem("b_rows")
        b_init = sem("b_init")
        mem = ExitStack()
        with mem, nc.Block() as block:
            xs = sb("b_xs_sb", [P, 2, J, D], at=mem)
            es = sb("b_es_sb", [P, 2, J, D], at=mem)
            xt = sb("b_xt_sb", [P, 2, C, TILE], at=mem)
            et = sb("b_et_sb", [P, 2, C, TILE], at=mem)
            fa = sb("fa", [P, 2, C, TILE], at=mem)
            prod = sb("prod", [P, 4, TILE], at=mem)
            z = sb("z", [P, C, TILE], at=mem)
            zs = sb("zs", [P, 2, C, TILE], at=mem)
            keeps = sb("keeps", [P, 2, TILE], BF16, at=mem)
            rows = sb("b_rows_sb", [P, 2, J, D], at=mem)
            ps_t = ps("b_ps_t", [P, C, TILE], mem)
            ps_fa = ps("ps_fa", [P, C, TILE], mem)
            ps_fe = ps("ps_fe", [P, C, TILE], mem)
            ps_m = ps("ps_m", [P, J, D], mem)

            @block.gpsimd
            def _(pool):
                b_x1 = nc.gpsimd.to_reg(x1.shape[0] - 1)
                b_edge_attr = nc.gpsimd.to_reg(edge_attr.shape[0] - 1)

                def gather_both(t, h, s, last):
                    need(pool, b_xs[s], h * J * 16)
                    need(pool, b_xt, (t - 1) * C)
                    stage_indices(pool, 0, src_cols, t, s, b_idx, t * 2 + 1)
                    gather(x1, b_x1, xs[:, s, :, :], 0, s, b_xs[s])
                    need(pool, b_es[s], h * J * 16)
                    need(pool, b_et, (t - 1) * C)
                    stage_indices(pool, 1, edge_cols, t, s, b_idx, t * 2 + 2)
                    gather(edge_attr, b_edge_attr, es[:, s, :, :], 1, s, b_es[s])

                pipelined(pool, ET, [(0, gather_both)])

            @block.sync
            def _(sp):
                def load_keep(t, h, s, last):
                    need(sp, b_sc, (t - 1) * C)
                    sp.dma_start(keeps[:, s, :], keep_row[ds(t * TILE, TILE)].partition_broadcast(P)
                                 ).then_inc(b_kp[s], 16)

                def store_rows(t, h, s, last):
                    sp.wait_ge(b_rows, (t + 1) * 2)
                    sp.dma_start(edge_rows(agg_rows, t), rows[:, s, :, :]).then_inc(b_st[s], 16)

                pipelined(sp, ET, [(0, load_keep), (2, store_rows)])
                for s in range(2):
                    sp.wait_ge(b_st[s], ((ET + 1 - s) // 2) * 16)

            @block.tensor
            def _(pe):
                def turn_x(t, h, s, last):
                    pe.wait_ge(b_xs[s], (h + 1) * J * 16)
                    need(pe, b_etc, t * C)
                    for c in range(C):
                        transpose_rows(xs[:, s, :, :], ps_t, c, P).then_inc(b_xt, 1)

                def turn_e(t, h, s, last):
                    pe.wait_ge(b_es[s], (h + 1) * J * 16)
                    pe.wait_ge(b_xtc, (t + 1) * C)
                    for c in range(C):
                        transpose_rows(es[:, s, :, :], ps_t, c, P).then_inc(b_et, 1)

                def dft_x(t, h, s, last):
                    need(pe, b_fac, t * C)
                    pe.wait_ge(b_xtc, (t + 1) * C)
                    for m in range(C):
                        for c in range(C):
                            mm = nc.tensor.matmul(ps_fa[:, m, :], dft_sb[:, c, m * P:(m + 1) * P],
                                                  xt[:, s, c, :], start=(c == 0), stop=(c == C - 1))
                        mm.then_inc(b_fa, 1)

                def dft_e(t, h, s, last):
                    need(pe, b_prod, t)
                    pe.wait_ge(b_etc, (t + 1) * C)
                    for m in range(C):
                        for c in range(C):
                            mm = nc.tensor.matmul(ps_fe[:, m, :], dft_sb[:, c, m * P:(m + 1) * P],
                                                  et[:, s, c, :], start=(c == 0), stop=(c == C - 1))
                        mm.then_inc(b_fe, 1)

                def message(t, h, s, last):
                    need(pe, b_rows, t * 2)
                    pe.wait_ge(b_sc, (t + 1) * C)
                    for j in range(J):
                        for c in range(C):
                            mm = nc.tensor.matmul(ps_m[:, j, :], zs[:, s, c, j * P:(j + 1) * P],
                                                  w_msg[:, c, :], start=(c == 0), stop=(c == C - 1))
                    mm.then_inc(b_msg, 1)

                pipelined(pe, ET, [(0, turn_x), (1, dft_x), (0, turn_e), (1, dft_e), (2, message)])

            @block.scalar
            def _(act):
                def copy_xt(t, h, s, last):
                    need(act, b_fa, (t - 1) * C)
                    for c in range(C):
                        act.wait_ge(b_xt, t * C + c + 1)
                        nc.scalar.activation(xt[:, s, c, :], ps_t[:, c, :], ACT.Copy).then_inc(b_xtc, 1)

                def copy_et(t, h, s, last):
                    need(act, b_fe, (t - 1) * C)
                    for c in range(C):
                        act.wait_ge(b_et, t * C + c + 1)
                        nc.scalar.activation(et[:, s, c, :], ps_t[:, c, :], ACT.Copy).then_inc(b_etc, 1)

                def copy_fa(t, h, s, last):
                    need(act, b_prod, t - 1)
                    for m in range(C):
                        act.wait_ge(b_fa, t * C + m + 1)
                        nc.scalar.activation(fa[:, s, m, :], ps_fa[:, m, :], ACT.Copy).then_inc(b_fac, 1)

                def copy_rows(t, h, s, last):
                    act.wait_ge(b_msg, t + 1)
                    need(act, b_st[s], h * 16)
                    for k in range(2):
                        nc.scalar.activation(rows[:, s, 2 * k:2 * k + 2, :], ps_m[:, 2 * k:2 * k + 2, :],
                                             ACT.Copy).then_inc(b_rows, 1)

                pipelined(act, ET, [(0, copy_xt), (1, copy_fa), (0, copy_et), (2, copy_rows)])

            @block.vector
            def _(dve):
                v = nc.vector
                v.memset(zs[:, 1, :, TILE - 1:TILE], 0.0).then_inc(b_init, 1)
                dve.wait_ge(b_init, 1)

                def correlate(t, h, s, last):
                    dve.wait_ge(b_fac, (t + 1) * C)
                    dve.wait_ge(b_fe, (t + 1) * C)
                    need(dve, b_z, t * C)
                    v.tensor_tensor(out=prod[:, 0, :], in0=fa[:, s, 0, :], in1=ps_fe[:, 0, :], op=ALU.mult)
                    v.tensor_tensor(out=prod[:, 1, :], in0=fa[:, s, 1, :], in1=ps_fe[:, 1, :], op=ALU.mult)
                    v.tensor_tensor(out=prod[:, 2, :], in0=fa[:, s, 1, :], in1=ps_fe[:, 0, :], op=ALU.mult)
                    v.scalar_tensor_tensor(out=prod[:, 3, :], in0=fa[:, s, 0, :], scalar=sig[:, 0:1],
                                           in1=ps_fe[:, 1, :], op0=ALU.mult, op1=ALU.mult).then_inc(b_prod, 1)
                    dve.wait_ge(b_prod, t + 1)
                    need(dve, b_sc, t * C)
                    v.tensor_tensor(out=z[:, 0, :], in0=prod[:, 0, :], in1=prod[:, 1, :], op=ALU.add).then_inc(b_z, 1)
                    v.tensor_tensor(out=z[:, 1, :], in0=prod[:, 2, :], in1=prod[:, 3, :],
                                    op=ALU.subtract).then_inc(b_z, 1)
                    dve.wait_ge(b_kp[s], (h + 1) * 16)
                    need(dve, b_msg, t - 1)
                    for m in range(C):
                        dve.wait_ge(b_z, t * C + m + 1)
                        v.tensor_tensor_scan(out=zs[:, s, m, :], data0=keeps[:, s, :], data1=z[:, m, :],
                                             initial=zs[:, 1 - s, m, TILE - 1:TILE], op0=ALU.mult,
                                             op1=ALU.add).then_inc(b_sc, 1)

                pipelined(dve, ET, [(0, correlate)])

        q_idx = sem("q_idx")
        q_ag = [sem(f"q_ag{s}") for s in range(2)]
        q_x = [sem(f"q_x{s}") for s in range(2)]
        q_st = [sem(f"q_st{s}") for s in range(2)]
        q_xt = sem("q_xt")
        q_xtc = sem("q_xtc")
        q_nrm = sem("q_nrm")
        q_h = sem("q_h")
        q_hc = sem("q_hc")
        q_bn = sem("q_bn")
        q_init = sem("q_init")
        f_v = sem("f_v")
        f_s = sem("f_s")
        mem = ExitStack()
        with mem, nc.Block() as block:
            ag = sb("ag", [P, 2, J, D], at=mem)
            an = sb("an", [P, 2, J, D], at=mem)
            xr = sb("q_xr", [P, 2, J, D], at=mem)
            xt = sb("q_xt_sb", [P, 2, C, TILE], at=mem)
            hs = sb("hs", [P, 2, C, TILE], at=mem)
            mv = sb("q_mv", [P, C, 2], at=mem)
            ps_x = ps("q_ps_x", [P, C, TILE], mem)
            ps_h = ps("q_ps_h", [P, 2, C, TILE], mem)

            @block.gpsimd
            def _(pool):
                pool.wait_ge(q_init, 1)

                b_agg_rows = nc.gpsimd.to_reg(agg_rows.shape[0] - 1)

                def gather_agg(t, h, s, last):
                    need(pool, q_ag[s], h * J * 16)
                    need(pool, q_nrm, t - 1)
                    stage_indices(pool, 0, ptr, t, s, q_idx, t + 1)
                    gather(agg_rows, b_agg_rows, ag[:, s, :, :], 0, s, q_ag[s])

                pipelined(pool, NT, [(0, gather_agg)])

            @block.sync
            def _(sp):
                def load_x1(t, h, s, last):
                    n = TP if last else P
                    need(sp, q_xt, (t - 1) * C)
                    sp.dma_start(xr[0:n, s, :, :], node_rows(x1, t, last)).then_inc(q_x[s], 16)

                def store_h(t, h, s, last):
                    sp.wait_ge(q_hc, (t + 1) * C)
                    dest = h_t[ds(t, 1), :, :].rearrange("o p n -> (o p) n")
                    if last:
                        for c in range(C):
                            sp.dma_start(part(dest.rearrange("p (c n) -> p c n", c=C), c, TP),
                                         part(hs[:, s, :, :], c, TP)).then_inc(q_st[s], 16)
                    else:
                        sp.dma_start(dest, hs[:, s, :, :].rearrange("p c n -> p (c n)")).then_inc(q_st[s], 16)

                pipelined(sp, NT, [(0, load_x1), (2, store_h)])
                for s in range(2):
                    extra = (C - 1) * 16 if (NT - 1) % 2 == s else 0
                    sp.wait_ge(q_st[s], ((NT + 1 - s) // 2) * 16 + extra)

            @block.tensor
            def _(pe):
                def turn(t, h, s, last):
                    n = TP if last else P
                    pe.wait_ge(q_x[s], (h + 1) * 16)
                    need(pe, q_xtc, t * C)
                    for c in range(C):
                        transpose_rows(xr[:, s, :, :], ps_x, c, n).then_inc(q_xt, 1)

                def project(t, h, s, last):
                    n = TP if last else P
                    need(pe, q_hc, (t - 1) * C)
                    pe.wait_ge(q_xtc, (t + 1) * C)
                    pe.wait_ge(q_nrm, t + 1)
                    for m in range(C):
                        for c in range(C):
                            nc.tensor.matmul(part(ps_h[:, s, :, :], m, n), w_h[:, c, m * P:(m + 1) * P],
                                             part(xt[:, s, :, :], c, n), start=(c == 0), stop=False)
                        for j in range(J):
                            mm = nc.tensor.matmul(ps_h[:, s, m, j * P:j * P + n],
                                                  an[0:n, s, j, m * P:(m + 1) * P], ident[0:n, 0:n],
                                                  is_transpose=True, start=False, stop=(j == J - 1))
                        mm.then_inc(q_h, 1)

                pipelined(pe, NT, [(0, turn), (1, project)])

            @block.scalar
            def _(act):
                def copy_xt(t, h, s, last):
                    n = TP if last else P
                    need(act, q_h, (t - 1) * C)
                    for c in range(C):
                        act.wait_ge(q_xt, t * C + c + 1)
                        nc.scalar.activation(part(xt[:, s, :, :], c, n), part(ps_x, c, n),
                                             ACT.Copy).then_inc(q_xtc, 1)

                def add_bias(t, h, s, last):
                    n = TP if last else P
                    need(act, q_st[s], h * 16)
                    need(act, q_bn, (t - 1) * C)
                    for m in range(C):
                        act.wait_ge(q_h, t * C + m + 1)
                        nc.scalar.activation(part(hs[:, s, :, :], m, n), part(ps_h[:, s, :, :], m, n),
                                             ACT.Identity, bias=wb_col[:, m:m + 1]).then_inc(q_hc, 1)

                pipelined(act, NT, [(0, copy_xt), (1, add_bias)])
                act.wait_ge(f_v, 1)
                nc.scalar.activation(bn_scale[:, :], mv[:, :, 1], ACT.Sqrt, bias=eps_col[:, :]).then_inc(f_s, 1)

            @block.vector
            def _(dve):
                v = nc.vector
                v.memset(ag[:, :, :, :], 0.0).then_inc(q_init, 1)

                def scale_sum(t, h, s, last):
                    n = TP if last else P
                    dve.wait_ge(q_ag[s], (h + 1) * J * 16)
                    need(dve, q_h, (t - 1) * C)
                    for j in range(J):
                        a = v.tensor_scalar(out=an[0:n, s, j, :], in0=ag[0:n, s, j, :],
                                            scalar1=norm_node[0:n, ds(t * J + j, 1)], scalar2=None, op0=ALU.mult)
                    a.then_inc(q_nrm, 1)

                def statistics(t, h, s, last):
                    n = TP if last else P
                    for m in range(C):
                        dve.wait_ge(q_hc, t * C + m + 1)
                        v.bn_stats(out=h_stats[:, m, ds(t * 6, 6)], in_=part(hs[:, s, :, :], m, n)
                                   ).then_inc(q_bn, 1)

                pipelined(dve, NT, [(0, scale_sum), (1, statistics)])
                dve.wait_ge(q_bn, NT * C)
                for m in range(C):
                    a = v.bn_aggr(out=mv[:, m, :], in_=h_stats[:, m, :])
                a.then_inc(f_v, 1)
                dve.wait_ge(f_s, 1)
                v.reciprocal(out=bn_scale[:, :], in_=bn_scale[:, :]).then_inc(f_v, 1)
                dve.wait_ge(f_v, 2)
                v.tensor_tensor(out=bn_scale[:, :], in0=bn_scale[:, :], in1=gam_col[:, :], op=ALU.mult).then_inc(f_v, 1)
                dve.wait_ge(f_v, 3)
                v.tensor_tensor(out=bn_shift[:, :], in0=mv[:, :, 0], in1=bn_scale[:, :], op=ALU.mult).then_inc(f_v, 1)
                dve.wait_ge(f_v, 4)
                v.tensor_tensor(out=bn_shift[:, :], in0=bet_col[:, :], in1=bn_shift[:, :], op=ALU.subtract)

        r_h = [sem(f"r_h{s}") for s in range(2)]
        r_x = [sem(f"r_x{s}") for s in range(2)]
        r_st = [sem(f"r_st{s}") for s in range(2)]
        r_th = sem("r_th")
        r_bk = sem("r_bk")
        r_sum = sem("r_sum")
        r_s6 = sem("r_s6")
        r_var = sem("r_var")
        r_ve = sem("r_ve")
        r_rs = sem("r_rs")
        r_nb = sem("r_nb")
        r_y = sem("r_y")
        r_init = sem("r_init")
        mem = ExitStack()
        with mem, nc.Block() as block:
            ht = sb("ht", [P, 2, C, TILE], at=mem)
            th = sb("th", [P, 2, C, TILE], at=mem)
            xr = sb("r_xr", [P, 2, J, D], at=mem)
            res = sb("r_res", [P, 2, J, D], at=mem)
            yo = sb("r_yo", [P, 2, J, D], at=mem)
            s6 = sb("r_s6_sb", [P, J, 6], at=mem)
            ms = sb("r_ms", [P, 2, 2, J], at=mem)
            tmp = sb("r_tmp", [P, 3, J], at=mem)
            ve = sb("ve", [P, 2, J], at=mem)
            rs = sb("r_rs_sb", [P, 2, J], at=mem)
            nb = sb("r_nb_sb", [P, 2, J], at=mem)
            mhalf = sb("mhalf", [P, J], at=mem)
            eps4 = sb("eps4", [P, J], at=mem)
            ps_y = ps("ps_y", [P, 2, J, D], mem)

            @block.sync
            def _(sp):
                def load(t, h, s, last):
                    n = TP if last else P
                    need(sp, r_th, t - 1)
                    source = h_t[ds(t, 1), :, :].rearrange("o p n -> (o p) n")
                    if last:
                        for c in range(C):
                            sp.dma_start(part(ht[:, s, :, :], c, TP),
                                         part(source.rearrange("p (c n) -> p c n", c=C), c, TP)
                                         ).then_inc(r_h[s], 16)
                    else:
                        sp.dma_start(ht[:, s, :, :].rearrange("p c n -> p (c n)"), source).then_inc(r_h[s], 16)
                    need(sp, r_sum, (t - 1) * 2)
                    sp.dma_start(xr[0:n, s, :, :], node_rows(x1, t, last)).then_inc(r_x[s], 16)

                def store(t, h, s, last):
                    n = TP if last else P
                    sp.wait_ge(r_y, t + 1)
                    sp.dma_start(node_rows(out, t, last), yo[0:n, s, :, :]).then_inc(r_st[s], 16)

                pipelined(sp, NT, [(0, load), (2, store)])
                for s in range(2):
                    sp.wait_ge(r_st[s], ((NT + 1 - s) // 2) * 16)

            @block.scalar
            def _(act):
                def squash(t, h, s, last):
                    n = TP if last else P
                    act.wait_ge(r_h[s], (h + 1) * 16 + (16 * (C - 1) if last else 0))
                    need(act, r_bk, t - 1)
                    for m in range(C):
                        a = nc.scalar.activation(part(th[:, s, :, :], m, n), part(ht[:, s, :, :], m, n),
                                                 ACT.Tanh, bias=bn_shift[:, m:m + 1], scale=bn_scale[:, m:m + 1])
                    a.then_inc(r_th, 1)

                def normalise(t, h, s, last):
                    n = TP if last else P
                    act.wait_ge(r_nb, t + 1)
                    need(act, r_st[s], h * 16)
                    for j in range(J):
                        a = nc.scalar.activation(yo[0:n, s, j, :], res[0:n, s, j, :], ACT.Identity,
                                                 bias=nb[0:n, s, j:j + 1], scale=rs[0:n, s, j:j + 1])
                    a.then_inc(r_y, 1)

                pipelined(act, NT, [(0, squash), (2, normalise)])

            @block.tensor
            def _(pe):
                def back(t, h, s, last):
                    n = TP if last else P
                    pe.wait_ge(r_th, t + 1)
                    need(pe, r_sum, (t - 1) * 2)
                    for c in range(C):
                        mm = transpose_back(th[:, s, :, :], ps_y[:, s, :, :], c, n)
                    mm.then_inc(r_bk, 1)

                pipelined(pe, NT, [(0, back)])

            @block.vector
            def _(dve):
                v = nc.vector
                v.memset(eps4[:, :], EPS)
                v.memset(mhalf[:, :], -0.5).then_inc(r_init, 1)

                def add(t, h, s, last):
                    n = TP if last else P
                    dve.wait_ge(r_bk, t + 1)
                    dve.wait_ge(r_x[s], (h + 1) * 16)
                    need(dve, r_y, t - 1)
                    for k in range(2):
                        v.tensor_tensor(out=res[0:n, s, 2 * k:2 * k + 2, :], in0=xr[0:n, s, 2 * k:2 * k + 2, :],
                                        in1=ps_y[0:n, s, 2 * k:2 * k + 2, :], op=ALU.add).then_inc(r_sum, 1)
                    dve.wait_ge(r_sum, (t + 1) * 2)
                    need(dve, r_nb, t - 1)
                    row_variance(dve, res[:, s, :, :], s6, ms[:, s, :, :], tmp, n, r_s6, t * 3 + 1).then_inc(r_var, 1)

                def shift(t, h, s, last):
                    n = TP if last else P
                    dve.wait_ge(r_rs, t + 1)
                    v.scalar_tensor_tensor(out=nb[0:n, s, :], in0=ms[0:n, s, 0, :], scalar=-0.5,
                                           in1=rs[0:n, s, :], op0=ALU.mult, op1=ALU.mult).then_inc(r_nb, 1)

                pipelined(dve, NT, [(0, add), (1, shift)])

            @block.gpsimd
            def _(pool):
                pool.wait_ge(r_init, 1)

                def rsqrt(t, h, s, last):
                    n = TP if last else P
                    pool.wait_ge(r_var, t + 1)
                    nc.gpsimd.tensor_tensor(out=ve[0:n, s, :], in0=ms[0:n, s, 1, :], in1=eps4[0:n, :],
                                            op=ALU.add).then_inc(r_ve, 1)
                    pool.wait_ge(r_ve, t + 1)
                    need(pool, r_y, t - 1)
                    nc.gpsimd.tensor_tensor(out=rs[0:n, s, :], in0=ve[0:n, s, :], in1=mhalf[0:n, :],
                                            op=ALU.pow).then_inc(r_rs, 1)

                pipelined(pool, NT, [(0, rsqrt)])


def constants(d):
    import numpy as np
    n = np.arange(d)
    k = np.arange(d // 2)
    angle = 2 * np.pi * np.outer(n, k) / d
    fwd = np.concatenate([np.cos(angle), np.sin(angle)], 1)
    inv = np.concatenate([2 * np.cos(angle), -2 * np.sin(angle)], 1) / d
    even, odd = (n % 2 == 0) * 1.0, (n % 2 == 1) * 1.0
    fwd[:, 0], fwd[:, d // 2] = even, odd
    inv[:, 0], inv[:, d // 2] = 2 * even / d, 2 * odd / d
    sigma = np.ones((P, 1))
    sigma[0] = -1
    return {
        "identity": np.eye(P, dtype=np.float32),
        "upper": np.triu(np.ones((P, P), np.float32), 1),
        "dft": fwd.astype(np.float32),
        "idft_t": inv.astype(np.float32),
        "sigma": sigma.astype(np.float32),
    }


def lay_out(inputs):
    import numpy as np
    a = {k: np.asarray(v) for k, v in inputs.items()}
    rel = a["L1_gnn_loop_rel"][0]
    out = {
        "x": a["x"], "src": a["src"], "dst": a["dst"], "edge_attr": a["edge_attr_256"],
        "theta_t": a["L0_gnn_theta_w"].T, "theta_b": a["L0_gnn_theta_b"],
        "phi_t": a["L0_gnn_phi_w"].T, "phi_b": a["L0_gnn_phi_b"],
        "w_loop": a["L1_gnn_w_loop"], "w_in": a["L1_gnn_w_in"], "loop_rel2": np.concatenate([rel, rel]),
        "w_bias": a["L1_gnn_w_bias"], "bn_gamma": a["L1_gnn_bn_gamma"], "bn_beta": a["L1_gnn_bn_beta"],
    }
    out.update(constants(rel.shape[0]))
    return {k: np.ascontiguousarray(v) for k, v in out.items()}


def build(nc, arrays):
    args = [nc.dram_tensor(f"in_{k}", v.shape, mybir.dt.from_np(v.dtype), kind="ExternalInput").ap()
            for k, v in arrays.items()]
    out = nc.dram_tensor("out_0", arrays["x"].shape, F32, kind="ExternalOutput").ap()
    gnn_kernel(nc, *args, out)


def kernel(**inputs):
    import concourse.bacc as _bacc
    from concourse.bass_utils import run_bass_kernel_spmd as _run

    nc = _bacc.Bacc("TRN2", target_bir_lowering=False, num_devices=1)
    arrays = lay_out(inputs)
    build(nc, arrays)
    r = _run(nc, [{f"in_{k}": v for k, v in arrays.items()}], core_ids=[0])
    return r.results[0]["out_0"]
```

```python
import concourse.bass as bass
from concourse import mybir
from concourse.bass import ds
from contextlib import ExitStack

F32 = mybir.dt.float32
BF16 = mybir.dt.bfloat16
I32 = mybir.dt.int32
ALU = mybir.AluOpType
ACT = mybir.ActivationFunctionType
AX = mybir.AxisListType

P = 128
UNROLL = 4
J = 4
TILE = P * J
HUGE = 3.38e38
MISSING = 1 << 20
EPS = 1e-5


def need(eng, sem, value):
    if isinstance(value, int) and value <= 0:
        return
    eng.wait_ge(sem, value)


class Step:

    def __init__(self, base, k, last):
        self.base, self.k, self.last = base, k, last
        self.t = k if base is None else base * UNROLL + k

    def slot(self, n):
        return self.k % n

    def turn(self, n):
        return self.k // n if self.base is None else base_plus(self.base, UNROLL // n, self.k // n)


def base_plus(base, times, more):
    return (base if times == 1 else base * times) + more


def pipelined(eng, tiles, stages):
    depth = max(lag for lag, _ in stages)
    first = -(-(depth + UNROLL) // UNROLL) * UNROLL
    rounds = max(0, (tiles - 1 - first) // UNROLL)

    def straight(t):
        for lag, step in stages:
            if 0 <= t - lag < tiles:
                step(Step(None, t - lag, t - lag == tiles - 1))

    if rounds == 0:
        first = 0
    for t in range(first):
        straight(t)
    if rounds:
        with eng.Fori(0, rounds) as i:
            for u in range(UNROLL):
                for lag, step in stages:
                    step(Step(i, first + u - lag, False))
    for t in range(first + UNROLL * rounds, tiles + depth):
        straight(t)


def gnn_kernel(nc, x, src, dst, edge_attr, theta_t, theta_b, phi_t, phi_b, w_loop, w_in, loop_rel2,
               w_bias, bn_gamma, bn_beta, identity, upper, dft, idft_t, sigma, out):
    N, D = x.shape
    E = src.shape[0]
    C = D // P
    H = P // 2
    assert D == 256 and N % J == 0
    NT = -(-N // TILE)
    TP = (N - (NT - 1) * TILE) // J
    ET = -(-E // TILE)
    EP = ET * TILE
    EC = EP // P
    ER = EP // D
    HC = EC // 2
    assert EC % 2 == 0 and HC <= P and ER <= P
    NQ = NT * J
    PAD_DST = (NT + 16) * TILE

    dst_pad = nc.dram_tensor("dst_pad", (1 + EP,), I32, kind="Internal").ap()
    src_pad = nc.dram_tensor("src_pad", (EP,), I32, kind="Internal").ap()
    edge_pad = nc.dram_tensor("edge_pad", (EP,), I32, kind="Internal").ap()
    cap_row = nc.dram_tensor("cap_row", (EP,), BF16, kind="Internal").ap()
    keep_row = nc.dram_tensor("keep_row", (EP,), BF16, kind="Internal").ap()
    max_rows = nc.dram_tensor("max_rows", (EP, D), F32, kind="Internal").ap()
    agg_rows = nc.dram_tensor("agg_rows", (EP, D), F32, kind="Internal").ap()
    x1 = nc.dram_tensor("x1", (N, D), F32, kind="Internal").ap()
    h_t = nc.dram_tensor("h_t", (NT, P, C * TILE), F32, kind="Internal").ap()

    def node_rows(table, t, last):
        rows = TP * J if last else TILE
        return table[ds(t * TILE, rows), :].rearrange("(p j) c -> p j c", j=J)

    def edge_rows(table, t):
        return table[ds(t * TILE, TILE), :].rearrange("(p j) c -> p j c", j=J)

    ctx = ExitStack()
    with ctx:
        def sb(name, shape, dt=F32, at=ctx):
            return at.enter_context(nc.sbuf_tensor(name, shape, dt))

        def ps(name, shape, at):
            return at.enter_context(nc.psum_tensor(name, shape, F32))

        def sem(name):
            return ctx.enter_context(nc.semaphore(name))

        ident = sb("ident", [P, P])
        up = sb("up", [P, P])
        ones = sb("ones", [P, P])
        sig = sb("sig", [P, 1])
        w_dst = sb("w_dst", [P, C, D])
        w_src = sb("w_src", [P, C, D])
        dft_sb = sb("dft_sb", [P, 2, P])
        w_h = sb("w_h", [P, C, D])
        w_msg = sb("w_msg", [P, C, D])
        bias_col = sb("bias_col", [P, C])
        wb_col = sb("wb_col", [P, C])
        gam_col = sb("gam_col", [P, C])
        bet_col = sb("bet_col", [P, C])
        eps_col = sb("eps_col", [P, 1])
        src_cols = sb("src_cols", [P, EC], I32)
        edge_cols = sb("edge_cols", [P, EC], I32)
        dst_p = sb("dst_p", [P, EC])
        dst_q = sb("dst_q", [P, EC])
        deg = sb("deg", [P, NQ])
        ptr = sb("ptr", [P, NQ], I32)
        cap_node = sb("cap_node", [P, NQ])
        norm_node = sb("norm_node", [P, NQ])
        h_stats = sb("h_stats", [P, C, NT * 6])
        bn_scale = sb("bn_scale", [P, C])
        bn_shift = sb("bn_shift", [P, C])
        idx = sb("idx", [P, 2, 4, J], I32)

        loaded = sem("loaded")
        loaded_w = sem("loaded_w")
        dst_written = sem("dst_written")
        idx_loaded = sem("idx_loaded")
        prep_v = sem("prep_v")
        prep_t = sem("prep_t")
        pads_ready = sem("pads_ready")
        masks_ready = sem("masks_ready")
        masks_stored = sem("masks_stored")
        prev_loaded = sem("prev_loaded")
        prep_done = sem("prep_done")
        small = ExitStack()
        with small, nc.Block() as block:
            raw_phi = sb("raw_phi", [P, C, D], at=small)
            hankel = sb("hankel", [P, C, D], at=small)
            wl = sb("wl", [P, C, D], at=small)
            wi = sb("wi", [P, C, D], at=small)
            idft_sb = sb("idft_sb", [P, C, D], at=small)
            b_col = sb("b_col", [P, 2, C], at=small)
            first_d = sb("first_d", [1, 1], I32, at=small)
            pad_d = sb("pad_d", [1, EP - E], I32, at=small)
            pad_s = sb("pad_s", [1, EP - E], I32, at=small)
            e_iota = sb("e_iota", [ER, D], I32, at=small)
            e_idx = sb("e_idx", [ER, D], I32, at=small)
            d_now = sb("d_now", [ER, D], I32, at=small)
            d_before = sb("d_before", [ER, D], I32, at=small)
            keep = sb("keep", [ER, D], BF16, at=small)
            cap = sb("cap", [ER, D], BF16, at=small)
            ints = sb("ints", [HC, 3, 2, P], I32, at=small)
            floats = sb("floats", [HC, 3, 2, P], at=small)
            dst_cols = sb("dst_cols", [P, EC], I32, at=small)
            t_a = sb("t_a", [P, EC], I32, at=small)
            t_b = sb("t_b", [P, EC], I32, at=small)
            ps_w = ps("ps_w", [P, 2, C, D], small)
            ps_i = ps("ps_i", [P, 3, 512], small)

            @block.sync
            def _(sp):
                def chunks(w):
                    return w.rearrange("(c p) n -> p c n", p=P)

                sp.dma_start(dst_pad[1:1 + E], dst).then_inc(dst_written, 16)
                sp.dma_start(src_pad[0:E], src).then_inc(dst_written, 16)
                sp.wait_ge(pads_ready, 1)
                sp.dma_start(dst_pad[0:1], first_d[0:1, 0:1]).then_inc(dst_written, 16)
                sp.dma_start(dst_pad[1 + E:], pad_d[0:1, :]).then_inc(dst_written, 16)
                sp.dma_start(src_pad[E:], pad_s[0:1, :]).then_inc(dst_written, 16)
                sp.dma_start(edge_pad.rearrange("(r c) -> r c", c=D), e_idx[:, :]).then_inc(dst_written, 16)
                for dest, w in ((w_dst, theta_t), (raw_phi, phi_t), (wl, w_loop), (wi, w_in),
                                (idft_sb, idft_t)):
                    sp.dma_start(dest[:, :, :], chunks(w)).then_inc(loaded_w, 16)
                sp.dma_start(dft_sb[:, :, :], dft).then_inc(loaded, 16)
                sp.dma_start(ident[:, :], identity).then_inc(loaded, 16)
                sp.dma_start(up[:, :], upper).then_inc(loaded, 16)
                sp.dma_start(sig[:, :], sigma).then_inc(loaded, 16)
                for dest, v in ((b_col[:, 0, :], theta_b), (b_col[:, 1, :], phi_b), (wb_col[:, :], w_bias),
                                (gam_col[:, :], bn_gamma), (bet_col[:, :], bn_beta)):
                    for c in range(C):
                        sp.dma_start(dest[:, c:c + 1], v[c * P:(c + 1) * P].rearrange("(p o) -> p o", o=1)
                                     ).then_inc(loaded, 16)
                for c in range(C):
                    win = bass.AP(loop_rel2.tensor, c * P, [[1, P], [1, D]])
                    sp.dma_start(hankel[:, c, :], win).then_inc(loaded_w, 16)
                sp.wait_ge(dst_written, 6 * 16)
                sp.dma_start(d_now[:, :], dst_pad[1:1 + EP].rearrange("(r c) -> r c", c=D)).then_inc(prev_loaded, 16)
                sp.dma_start(d_before[:, :], dst_pad[0:EP].rearrange("(r c) -> r c", c=D)).then_inc(prev_loaded, 16)
                for n, v in enumerate((src_pad, edge_pad, dst_pad[1:1 + EP])):
                    sp.dma_start(ints[:, n, :, :], v.rearrange("(h r c) -> r h c", h=2, c=P)).then_inc(idx_loaded, 16)
                sp.wait_ge(masks_ready, 1)
                sp.dma_start(keep_row.rearrange("(r c) -> r c", c=D), keep[:, :]).then_inc(masks_stored, 16)
                sp.dma_start(cap_row.rearrange("(r c) -> r c", c=D), cap[:, :]).then_inc(masks_stored, 16)
                sp.wait_ge(masks_stored, 32)

            @block.gpsimd
            def _(pool):
                nc.gpsimd.iota(e_iota[:, :], [[1, D]], base=0, channel_multiplier=D).then_inc(prep_done, 1)

            @block.vector
            def _(dve):
                v = nc.vector
                v.memset(first_d[:, :], -1)
                v.memset(pad_d[:, :], PAD_DST)
                v.memset(pad_s[:, :], 0)
                dve.wait_ge(prep_done, 1)
                v.tensor_scalar(out=e_idx[:, :], in0=e_iota[:, :], scalar1=float(E - 1), scalar2=None,
                                op0=ALU.min).then_inc(pads_ready, 1)
                v.memset(ones[:, :], 1.0)
                v.memset(eps_col[:, :], EPS)
                v.memset(idx[:, :, :, :], 0)
                dve.wait_ge(loaded_w, 16 * (5 + C))
                v.tensor_tensor(out=w_src[:, :, :], in0=raw_phi[:, :, :], in1=w_dst[:, :, :],
                                op=ALU.subtract)
                dve.wait_ge(loaded, 16 * (4 + 5 * C))
                v.tensor_tensor(out=bias_col[:, :], in0=b_col[:, 0, :], in1=b_col[:, 1, :], op=ALU.add)
                dve.wait_ge(prev_loaded, 32)
                v.tensor_tensor(out=keep[:, :], in0=d_now[:, :], in1=d_before[:, :],
                                op=ALU.is_equal).then_inc(prep_v, 1)
                dve.wait_ge(prep_v, 1)
                v.tensor_scalar(out=cap[:, :], in0=keep[:, :], scalar1=2.0, scalar2=1.0, op0=ALU.mult,
                                op1=ALU.subtract).then_inc(prep_v, 1)
                dve.wait_ge(prep_v, 2)
                v.tensor_scalar(out=cap[:, :], in0=cap[:, :], scalar1=HUGE, scalar2=None,
                                op0=ALU.mult).then_inc(masks_ready, 1)
                dve.wait_ge(idx_loaded, 48)
                v.tensor_copy(out=floats[:, :, :, :], in_=ints[:, :, :, :]).then_inc(prep_v, 1)
                dve.wait_ge(prep_t, 1)
                v.tensor_copy(out=src_cols[:, :], in_=ps_i[:, 0, 0:EC])
                v.tensor_copy(out=edge_cols[:, :], in_=ps_i[:, 1, 0:EC])
                v.tensor_copy(out=dst_cols[:, :], in_=ps_i[:, 2, 0:EC]).then_inc(prep_v, 1)
                dve.wait_ge(prep_v, 4)
                v.tensor_scalar(out=t_a[:, :], in0=dst_cols[:, :], scalar1=2, scalar2=P - 1,
                                op0=ALU.logical_shift_right, op1=ALU.bitwise_and).then_inc(prep_v, 1)
                dve.wait_ge(prep_v, 5)
                v.tensor_copy(out=dst_p[:, :], in_=t_a[:, :]).then_inc(prep_v, 1)
                dve.wait_ge(prep_v, 6)
                v.tensor_scalar(out=t_a[:, :], in0=dst_cols[:, :], scalar1=9, scalar2=2,
                                op0=ALU.logical_shift_right, op1=ALU.logical_shift_left)
                v.tensor_scalar(out=t_b[:, :], in0=dst_cols[:, :], scalar1=J - 1, scalar2=None,
                                op0=ALU.bitwise_and).then_inc(prep_v, 1)
                dve.wait_ge(prep_v, 7)
                v.tensor_tensor(out=t_a[:, :], in0=t_a[:, :], in1=t_b[:, :], op=ALU.bitwise_or).then_inc(prep_v, 1)
                dve.wait_ge(prep_v, 8)
                v.tensor_copy(out=dst_q[:, :], in_=t_a[:, :])
                dve.wait_ge(prep_t, 3)
                v.tensor_copy(out=w_h[:, :, :], in_=ps_w[:, 0, :, :])
                v.tensor_copy(out=w_msg[:, :, :], in_=ps_w[:, 1, :, :])

            @block.tensor
            def _(pe):
                pe.wait_ge(loaded, 16 * (4 + 5 * C))
                pe.wait_ge(prep_v, 3)
                for n in range(3):
                    for half in range(2):
                        last = nc.tensor.transpose(ps_i[:, n, half * HC:(half + 1) * HC],
                                                   floats[:, n, half, :], ident[0:HC, 0:HC])
                last.then_inc(prep_t, 1)
                pe.wait_ge(loaded_w, 16 * (5 + C))
                for n, (left, right) in enumerate(((hankel, wl), (idft_sb, wi))):
                    for m in range(C):
                        for c in range(C):
                            last = nc.tensor.matmul(ps_w[:, n, m, :], left[:, c, m * P:(m + 1) * P],
                                                    right[:, c, :], start=(c == 0), stop=(c == C - 1))
                    last.then_inc(prep_t, 1)

        gathers_begun = sem("gathers_begun")

        def stage_indices(pool, cols, w, ring, staged, count):
            nc.gpsimd.tensor_copy(out=idx[:, ring, w.slot(4), :], in_=cols[:, ds(w.t * J, J)]).then_inc(staged, 1)
            pool.wait_ge(staged, count)
            pool.sem_inc(gathers_begun, 1)

        def gather(table, bound, dest, w, ring, done):
            for j in range(J):
                nc.gpsimd.indirect_dma_start(
                    out=dest[:, w.slot(4), j, :], out_offset=None, in_=table,
                    in_offset=bass.IndirectOffsetOnAxis(ap=idx[:, ring, w.slot(4), j:j + 1], axis=0),
                    bounds_check=bound, oob_is_err=False).then_inc(done[w.slot(4)], 16)

        def landed(eng, done, w, transfers=1, extra=0):
            eng.wait_ge(done[w.slot(4)], (w.turn(4) + 1) * (16 * transfers) + extra)

        def slot_free(eng, done, w, transfers=1):
            need(eng, done[w.slot(4)], w.turn(4) * (16 * transfers))

        def all_stored(eng, done, tiles, extra=0):
            for s in range(4):
                more = extra if (tiles - 1) % 4 == s else 0
                eng.wait_ge(done[s], ((tiles + 3 - s) // 4) * 16 + more)

        def transpose_rows(rows, dest, c, n):
            for j in range(J):
                last = nc.tensor.transpose(dest[:, c, j * P:j * P + n], rows[0:n, j, c * P:(c + 1) * P],
                                           ident[0:n, 0:n])
            return last

        def transpose_back(cols, dest, c, n):
            for j in range(J):
                last = nc.tensor.transpose(dest[0:n, j, c * P:(c + 1) * P], cols[:, c, j * P:j * P + n],
                                           ident[:, :])
            return last

        def part(cols, c, n):
            if n == P:
                return cols[:, c, :]
            return cols[:, c, :].rearrange("p (j n) -> p j n", j=J)[:, :, 0:n]

        def ring_sems(name):
            return [sem(f"{name}{s}") for s in range(4)]

        a_idx = sem("a_idx")
        a_src = ring_sems("a_src")
        a_cap = ring_sems("a_cap")
        a_st = ring_sems("a_st")
        a_iota = sem("a_iota")
        a_xt = sem("a_xt")
        a_xtc = sem("a_xtc")
        a_b = sem("a_b")
        a_bc = sem("a_bc")
        a_scan = sem("a_scan")
        a_back = sem("a_back")
        a_rows = sem("a_rows")
        a_hot = sem("a_hot")
        a_cnt = sem("a_cnt")
        a_init = sem("a_init")
        c_v = sem("c_v")
        c_t = sem("c_t")
        c_s = sem("c_s")
        mem = ExitStack()
        with mem, nc.Block() as block:
            iota_q = sb("iota_q", [P, NQ], at=mem)
            iota_p = sb("iota_p", [P, P], at=mem)
            xs = sb("xs", [P, 4, J, D], at=mem)
            xt = sb("xt", [P, 2, C, TILE], at=mem)
            bt = sb("bt", [P, 2, C, TILE], at=mem)
            caps = sb("caps", [P, 4, TILE], BF16, at=mem)
            mx = sb("mx", [P, 2, C, TILE], at=mem)
            rows = sb("rows", [P, 4, J, D], at=mem)
            hot_q = sb("hot_q", [P, 2, J, NQ], BF16, at=mem)
            hot_p = sb("hot_p", [P, 2, J, P], BF16, at=mem)
            ps_x = ps("ps_x", [P, C, TILE], mem)
            ps_b = ps("ps_b", [P, C, TILE], mem)
            ps_r = ps("ps_r", [P, J, D], mem)
            ps_n = ps("ps_n", [P, 512], mem)

            @block.gpsimd
            def _(pool):
                nc.gpsimd.iota(iota_q[:, :], [[1, NQ]], base=0, channel_multiplier=0,
                               allow_small_or_imprecise_dtypes=True)
                nc.gpsimd.iota(iota_p[:, :], [[1, P]], base=0, channel_multiplier=0,
                               allow_small_or_imprecise_dtypes=True).then_inc(a_iota, 1)
                b_x = nc.gpsimd.to_reg(N - 1)

                def gather_src(w):
                    slot_free(pool, a_src, w, J)
                    need(pool, a_xt, (w.t - 3) * C)
                    stage_indices(pool, src_cols, w, 0, a_idx, w.t + 1)
                    gather(x, b_x, xs, w, 0, a_src)

                pipelined(pool, ET, [(0, gather_src)])

            @block.sync
            def _(sp):
                def load_caps(w):
                    need(sp, a_scan, (w.t - 3) * C)
                    sp.dma_start(caps[:, w.slot(4), :], cap_row[ds(w.t * TILE, TILE)].partition_broadcast(P)
                                 ).then_inc(a_cap[w.slot(4)], 16)

                pipelined(sp, ET, [(0, load_caps)])

            @block.tensor
            def _(pe):
                def turn(w):
                    landed(pe, a_src, w, J)
                    need(pe, a_xtc, w.t * C)
                    for c in range(C):
                        transpose_rows(xs[:, w.slot(4), :, :], ps_x, c, P).then_inc(a_xt, 1)

                def project(w):
                    for m in range(C):
                        need(pe, a_bc, (w.t - 1) * C + m + 1)
                        for c in range(C):
                            if m == 0:
                                pe.wait_ge(a_xtc, w.t * C + c + 1)
                            mm = nc.tensor.matmul(ps_b[:, m, :], w_src[:, c, m * P:(m + 1) * P],
                                                  xt[:, w.slot(2), c, :], start=(c == 0), stop=(c == C - 1))
                        mm.then_inc(a_b, 1)

                def count(w):
                    pe.wait_ge(a_hot, w.t + 1)
                    for j in range(J):
                        mm = nc.tensor.matmul(ps_n[:, 0:NQ], hot_p[:, w.slot(2), j, :], hot_q[:, w.slot(2), j, :],
                                              start=(w.base is None and w.k == 0 and j == 0),
                                              stop=(w.last and j == J - 1))
                    mm.then_inc(a_cnt, 1)

                def back(w):
                    need(pe, a_rows, w.t * 2)
                    pe.wait_ge(a_scan, (w.t + 1) * C)
                    for c in range(C):
                        mm = transpose_back(mx[:, w.slot(2), :, :], ps_r, c, P)
                    mm.then_inc(a_back, 1)

                pipelined(pe, ET, [(0, turn), (1, project), (1, count), (3, back)])
                pe.wait_ge(c_v, 2)
                nc.tensor.matmul(ps_x[:, 0, 0:NT], ones[:, :], mx[:, 0, 0, 0:NT], start=True, stop=True)
                nc.tensor.matmul(ps_x[:, 1, 0:NT], up[:, :], mx[:, 0, 0, 0:NT], start=True,
                                 stop=True).then_inc(c_t, 1)

            @block.scalar
            def _(act):
                def copy_xt(w):
                    need(act, a_b, (w.t - 1) * C)
                    for c in range(C):
                        act.wait_ge(a_xt, w.t * C + c + 1)
                        nc.scalar.activation(xt[:, w.slot(2), c, :], ps_x[:, c, :], ACT.Copy).then_inc(a_xtc, 1)

                def add_bias(w):
                    need(act, a_scan, (w.t - 1) * C)
                    for m in range(C):
                        act.wait_ge(a_b, w.t * C + m + 1)
                        nc.scalar.activation(bt[:, w.slot(2), m, :], ps_b[:, m, :], ACT.Identity,
                                             bias=bias_col[:, m:m + 1]).then_inc(a_bc, 1)

                def copy_rows(w):
                    slot_free(act, a_st, w)
                    act.wait_ge(a_back, w.t + 1)
                    for k in range(2):
                        nc.scalar.activation(rows[:, w.slot(4), 2 * k:2 * k + 2, :], ps_r[:, 2 * k:2 * k + 2, :],
                                             ACT.Copy).then_inc(a_rows, 1)

                def store_rows(w):
                    act.wait_ge(a_rows, (w.t + 1) * 2)
                    act.dma_start(edge_rows(max_rows, w.t), rows[:, w.slot(4), :, :]).then_inc(a_st[w.slot(4)], 16)

                pipelined(act, ET, [(0, copy_xt), (1, add_bias), (3, copy_rows), (4, store_rows)])
                act.wait_ge(c_v, 4)
                nc.scalar.activation(norm_node[:, :], norm_node[:, :], ACT.Sqrt).then_inc(c_s, 1)
                all_stored(act, a_st, ET)

            @block.vector
            def _(dve):
                v = nc.vector
                v.memset(mx[:, 1, :, TILE - 1:TILE], -HUGE).then_inc(a_init, 1)
                dve.wait_ge(a_init, 1)
                dve.wait_ge(a_iota, 1)

                def one_hots(w):
                    need(dve, a_cnt, w.t - 1)
                    for j in range(J):
                        col = w.t * J + j
                        v.tensor_scalar(out=hot_q[:, w.slot(2), j, :], in0=iota_q[:, :],
                                        scalar1=dst_q[:, ds(col, 1)], scalar2=None, op0=ALU.is_equal)
                        a = v.tensor_scalar(out=hot_p[:, w.slot(2), j, :], in0=iota_p[:, :],
                                            scalar1=dst_p[:, ds(col, 1)], scalar2=None, op0=ALU.is_equal)
                    a.then_inc(a_hot, 1)

                def running_max(w):
                    need(dve, a_back, w.t - 1)
                    need(dve, a_scan, w.t * C)
                    landed(dve, a_cap, w)
                    for m in range(C):
                        dve.wait_ge(a_bc, w.t * C + m + 1)
                        v.tensor_tensor_scan(out=mx[:, w.slot(2), m, :], data0=caps[:, w.slot(4), :],
                                             data1=bt[:, w.slot(2), m, :],
                                             initial=mx[:, 1 - w.slot(2), m, TILE - 1:TILE], op0=ALU.min,
                                             op1=ALU.max).then_inc(a_scan, 1)

                pipelined(dve, ET, [(0, one_hots), (2, running_max)])

                done = [0]

                def link(ins):
                    done[0] += 1
                    ins.then_inc(c_v, 1)
                    dve.wait_ge(c_v, done[0])

                tot = mx[:, 0, 0, 0:NT]
                every = mx[:, 0, 1, 0:NT]
                base = mx[:, 1, 0, 0:NT]
                ends = xt[:, 0, :, :].rearrange("p c n -> p (c n)")[:, 0:NQ]
                e4 = ends.rearrange("p (i j) -> p i j", j=J)
                d4 = deg[:, :].rearrange("p (i j) -> p i j", j=J)
                i_a = bt[:, 0, :, :].rearrange("p c n -> p (c n)")[:, 0:NQ].bitcast(I32)
                i_b = bt[:, 1, :, :].rearrange("p c n -> p (c n)")[:, 0:NQ].bitcast(I32)
                i_c = xs[:, 0, :, :].rearrange("p c n -> p (c n)")[:, 0:NQ].bitcast(I32)
                dve.wait_ge(a_back, ET)
                dve.wait_ge(a_cnt, ET)
                link(v.tensor_copy(out=deg[:, :], in_=ps_n[:, 0:NQ]))
                link(v.tensor_reduce(out=tot, in_=d4, axis=AX.X, op=ALU.add))
                link(v.tensor_scalar(out=cap_node[:, :], in0=deg[:, :], scalar1=1.0, scalar2=None, op0=ALU.min))
                link(v.tensor_scalar(out=norm_node[:, :], in0=deg[:, :], scalar1=1.0, scalar2=None, op0=ALU.max))
                dve.wait_ge(c_t, 1)
                link(v.tensor_tensor_scan(out=every, data0=ones[:, 0:NT], data1=ps_x[:, 0, 0:NT], initial=0.0,
                                          op0=ALU.mult, op1=ALU.add))
                link(v.tensor_tensor(out=every, in0=every, in1=ps_x[:, 0, 0:NT], op=ALU.subtract))
                link(v.tensor_tensor(out=base, in0=every, in1=ps_x[:, 1, 0:NT], op=ALU.add))
                link(v.tensor_scalar(out=base, in0=base, scalar1=1.0, scalar2=None, op0=ALU.subtract))
                link(v.tensor_tensor(out=e4[:, :, 0], in0=base, in1=d4[:, :, 0], op=ALU.add))
                for j in range(1, J):
                    link(v.tensor_tensor(out=e4[:, :, j], in0=e4[:, :, j - 1], in1=d4[:, :, j], op=ALU.add))
                link(v.tensor_scalar(out=i_a, in0=ends, scalar1=0.0, scalar2=None, op0=ALU.max))
                link(v.tensor_scalar(out=i_b, in0=i_a, scalar1=9, scalar2=9, op0=ALU.logical_shift_right,
                                     op1=ALU.logical_shift_left))
                link(v.tensor_scalar(out=i_c, in0=i_a, scalar1=P - 1, scalar2=2, op0=ALU.bitwise_and,
                                     op1=ALU.logical_shift_left))
                link(v.tensor_tensor(out=i_b, in0=i_b, in1=i_c, op=ALU.bitwise_or))
                link(v.tensor_scalar(out=i_c, in0=i_a, scalar1=7, scalar2=J - 1, op0=ALU.logical_shift_right,
                                     op1=ALU.bitwise_and))
                link(v.tensor_tensor(out=i_b, in0=i_b, in1=i_c, op=ALU.bitwise_or))
                link(v.tensor_scalar(out=i_c, in0=deg[:, :], scalar1=0.0, scalar2=float(MISSING),
                                     op0=ALU.is_equal, op1=ALU.mult))
                link(v.tensor_tensor(out=ptr[:, :], in0=i_b, in1=i_c, op=ALU.bitwise_or))
                dve.wait_ge(c_s, 1)
                link(v.reciprocal(out=norm_node[:, :], in_=norm_node[:, :]))
                link(v.tensor_tensor(out=norm_node[:, :], in0=norm_node[:, :], in1=cap_node[:, :], op=ALU.mult))
                link(v.tensor_scalar(out=cap_node[:, :], in0=cap_node[:, :], scalar1=2.0, scalar2=1.0,
                                     op0=ALU.mult, op1=ALU.subtract))
                link(v.tensor_scalar(out=cap_node[:, :], in0=cap_node[:, :], scalar1=HUGE, scalar2=None,
                                     op0=ALU.mult))

        def half_statistics(y, s6, n):
            for j in range(J):
                ins = nc.vector.bn_stats(out=s6[0:n, j, :], in_=y[0:n, j, :])
            return ins

        def join_halves(dve, s6, ms, tmp, n, step, first):
            v = nc.vector
            v.tensor_tensor(out=ms[0:n, 0, :], in0=s6[0:n, :, 1], in1=s6[0:n, :, 4], op=ALU.add)
            v.tensor_tensor(out=tmp[0:n, 0, :], in0=s6[0:n, :, 1], in1=s6[0:n, :, 4], op=ALU.subtract)
            v.tensor_tensor(out=tmp[0:n, 1, :], in0=s6[0:n, :, 2], in1=s6[0:n, :, 5],
                            op=ALU.add).then_inc(step, 1)
            dve.wait_ge(step, first)
            v.scalar_tensor_tensor(out=tmp[0:n, 2, :], in0=tmp[0:n, 0, :], scalar=0.25, in1=tmp[0:n, 0, :],
                                   op0=ALU.mult, op1=ALU.mult).then_inc(step, 1)
            dve.wait_ge(step, first + 1)
            return v.scalar_tensor_tensor(out=ms[0:n, 1, :], in0=tmp[0:n, 1, :], scalar=1.0 / D,
                                          in1=tmp[0:n, 2, :], op0=ALU.mult, op1=ALU.add)

        p_idx = sem("p_idx")
        p_mg = ring_sems("p_mg")
        p_x = ring_sems("p_x")
        p_st = ring_sems("p_st")
        p_xt = sem("p_xt")
        p_xtc = sem("p_xtc")
        p_a = sem("p_a")
        p_sum = sem("p_sum")
        p_res = sem("p_res")
        p_s6 = sem("p_s6")
        p_join = sem("p_join")
        p_var = sem("p_var")
        p_sd = sem("p_sd")
        p_rs = sem("p_rs")
        p_nb = sem("p_nb")
        p_y = sem("p_y")
        p_init = sem("p_init")
        mem = ExitStack()
        with mem, nc.Block() as block:
            mg = sb("mg", [P, 4, J, D], at=mem)
            xr = sb("xr", [P, 4, J, D], at=mem)
            xt = sb("p_xt_sb", [P, 2, C, TILE], at=mem)
            total = sb("total", [P, 2, J, D], at=mem)
            res = sb("res", [P, 4, J, D], at=mem)
            yo = sb("yo", [P, 4, J, D], at=mem)
            s6 = sb("s6", [P, 2, J, 6], at=mem)
            ms = sb("ms", [P, 4, 2, J], at=mem)
            tmp = sb("tmp", [P, 2, 3, J], at=mem)
            sd = sb("sd", [P, 2, J], at=mem)
            rs = sb("rs", [P, 2, J], at=mem)
            nb = sb("nb", [P, 2, J], at=mem)
            ps_x = ps("p_ps_x", [P, 2, C, TILE], mem)
            ps_a = ps("p_ps_a", [P, 2, J, D], mem)

            @block.gpsimd
            def _(pool):
                pool.wait_ge(p_init, 1)
                b_max = nc.gpsimd.to_reg(EP - 1)

                def gather_max(w):
                    slot_free(pool, p_mg, w, J)
                    need(pool, p_sum, w.t - 3)
                    stage_indices(pool, ptr, w, 0, p_idx, w.t + 1)
                    gather(max_rows, b_max, mg, w, 0, p_mg)

                pipelined(pool, NT, [(0, gather_max)])

            @block.sync
            def _(sp):
                def load_x(w):
                    n = TP if w.last else P
                    need(sp, p_res, w.t - 3)
                    sp.dma_start(xr[0:n, w.slot(4), :, :], node_rows(x, w.t, w.last)).then_inc(p_x[w.slot(4)], 16)

                pipelined(sp, NT, [(0, load_x)])

            @block.tensor
            def _(pe):
                def turn(w):
                    n = TP if w.last else P
                    landed(pe, p_x, w)
                    need(pe, p_xtc, (w.t - 1) * C)
                    for c in range(C):
                        transpose_rows(xr[:, w.slot(4), :, :], ps_x[:, w.slot(2), :, :], c, n).then_inc(p_xt, 1)

                def project(w):
                    n = TP if w.last else P
                    need(pe, p_sum, w.t - 1)
                    pe.wait_ge(p_xtc, (w.t + 1) * C)
                    for j in range(J):
                        for c in range(C):
                            mm = nc.tensor.matmul(ps_a[0:n, w.slot(2), j, :], xt[:, w.slot(2), c, j * P:j * P + n],
                                                  w_dst[:, c, :], start=(c == 0), stop=(c == C - 1))
                    mm.then_inc(p_a, 1)

                pipelined(pe, NT, [(0, turn), (1, project)])

            @block.scalar
            def _(act):
                def copy_xt(w):
                    n = TP if w.last else P
                    need(act, p_a, w.t - 1)
                    for c in range(C):
                        act.wait_ge(p_xt, w.t * C + c + 1)
                        nc.scalar.activation(part(xt[:, w.slot(2), :, :], c, n),
                                             part(ps_x[:, w.slot(2), :, :], c, n), ACT.Copy).then_inc(p_xtc, 1)

                def root(w):
                    n = TP if w.last else P
                    act.wait_ge(p_var, w.t + 1)
                    need(act, p_rs, w.t - 1)
                    nc.scalar.activation(sd[0:n, w.slot(2), :], ms[0:n, w.slot(4), 1, :], ACT.Sqrt,
                                         bias=eps_col[0:n, :]).then_inc(p_sd, 1)

                def normalise(w):
                    n = TP if w.last else P
                    s = w.slot(2)
                    slot_free(act, p_st, w)
                    act.wait_ge(p_nb, w.t + 1)
                    for j in range(J):
                        a = nc.scalar.activation(yo[0:n, w.slot(4), j, :], res[0:n, w.slot(4), j, :], ACT.Identity,
                                                 bias=nb[0:n, s, j:j + 1], scale=rs[0:n, s, j:j + 1])
                    a.then_inc(p_y, 1)

                def store_x1(w):
                    n = TP if w.last else P
                    act.wait_ge(p_y, w.t + 1)
                    act.dma_start(node_rows(x1, w.t, w.last), yo[0:n, w.slot(4), :, :]).then_inc(p_st[w.slot(4)], 16)

                pipelined(act, NT, [(0, copy_xt), (3, root), (4, normalise), (5, store_x1)])
                all_stored(act, p_st, NT)

            @block.vector
            def _(dve):
                v = nc.vector
                v.memset(mg[:, :, :, :], 0.0).then_inc(p_init, 1)

                def add_max(w):
                    n = TP if w.last else P
                    landed(dve, p_mg, w, J)
                    dve.wait_ge(p_a, w.t + 1)
                    need(dve, p_res, w.t - 1)
                    for j in range(J):
                        a = v.scalar_tensor_tensor(out=total[0:n, w.slot(2), j, :], in0=mg[0:n, w.slot(4), j, :],
                                                   scalar=cap_node[0:n, ds(w.t * J + j, 1)],
                                                   in1=ps_a[0:n, w.slot(2), j, :], op0=ALU.min, op1=ALU.add)
                    a.then_inc(p_sum, 1)

                def relu_add(w):
                    n = TP if w.last else P
                    dve.wait_ge(p_sum, w.t + 1)
                    need(dve, p_y, w.t - 3)
                    v.scalar_tensor_tensor(out=res[0:n, w.slot(4), :, :], in0=total[0:n, w.slot(2), :, :], scalar=0.0,
                                           in1=xr[0:n, w.slot(4), :, :], op0=ALU.max, op1=ALU.add).then_inc(p_res, 1)

                def statistics(w):
                    n = TP if w.last else P
                    dve.wait_ge(p_res, w.t + 1)
                    need(dve, p_var, w.t - 1)
                    half_statistics(res[:, w.slot(4), :, :], s6[:, w.slot(2), :, :], n).then_inc(p_s6, 1)

                def variance(w):
                    n = TP if w.last else P
                    dve.wait_ge(p_s6, w.t + 1)
                    need(dve, p_nb, w.t - 3)
                    join_halves(dve, s6[:, w.slot(2), :, :], ms[:, w.slot(4), :, :], tmp[:, w.slot(2), :, :], n,
                                p_join, w.t * 2 + 1).then_inc(p_var, 1)

                def scales(w):
                    n = TP if w.last else P
                    dve.wait_ge(p_sd, w.t + 1)
                    need(dve, p_y, w.t - 1)
                    v.reciprocal(out=rs[0:n, w.slot(2), :], in_=sd[0:n, w.slot(2), :]).then_inc(p_rs, 1)
                    dve.wait_ge(p_rs, w.t + 1)
                    v.scalar_tensor_tensor(out=nb[0:n, w.slot(2), :], in0=ms[0:n, w.slot(4), 0, :], scalar=-0.5,
                                           in1=rs[0:n, w.slot(2), :], op0=ALU.mult, op1=ALU.mult).then_inc(p_nb, 1)

                pipelined(dve, NT, [(3, scales), (1, add_max), (2, statistics), (1, relu_add), (2, variance)])

        b_idx = sem("b_idx")
        b_xs = ring_sems("b_xs")
        b_es = ring_sems("b_es")
        b_kp = ring_sems("b_kp")
        b_st = ring_sems("b_st")
        b_xt = sem("b_xt")
        b_et = sem("b_et")
        b_xh = sem("b_xh")
        b_eh = sem("b_eh")
        b_xf = sem("b_xf")
        b_ef = sem("b_ef")
        b_fx = sem("b_fx")
        b_fe = sem("b_fe")
        b_fxc = sem("b_fxc")
        b_fec = sem("b_fec")
        b_prod = sem("b_prod")
        b_z = sem("b_z")
        b_sc = sem("b_sc")
        b_msg = sem("b_msg")
        b_rows = sem("b_rows")
        b_init = sem("b_init")
        mem = ExitStack()
        with mem, nc.Block() as block:
            xs = sb("b_xs_sb", [P, 4, J, D], at=mem)
            es = sb("b_es_sb", [P, 4, J, D], at=mem)
            upper_x = sb("upper_x", [P, TILE], at=mem)
            upper_e = sb("upper_e", [P, TILE], at=mem)
            fold_x = sb("fold_x", [P, 2, 2, TILE], at=mem)
            fold_e = sb("fold_e", [P, 2, 2, TILE], at=mem)
            fx = sb("fx", [P, 2, 2, TILE], at=mem)
            fe = sb("fe", [P, 2, 2, TILE], at=mem)
            prod = sb("prod", [P, 4, TILE], at=mem)
            z = sb("z", [P, C, TILE], at=mem)
            zs = sb("zs", [P, 2, C, TILE], at=mem)
            keeps = sb("keeps", [P, 4, TILE], BF16, at=mem)
            rows = sb("b_rows_sb", [P, 4, J, D], at=mem)
            ps_t = ps("b_ps_t", [P, C, TILE], mem)
            ps_fx = ps("ps_fx", [P, 2, TILE], mem)
            ps_fe = ps("ps_fe", [P, 2, TILE], mem)
            ps_m = ps("ps_m", [P, J, D], mem)

            @block.gpsimd
            def _(pool):
                b_x1 = nc.gpsimd.to_reg(N - 1)
                b_edge = nc.gpsimd.to_reg(E - 1)

                def gather_both(w):
                    slot_free(pool, b_xs, w, J)
                    need(pool, b_xt, w.t - 3)
                    stage_indices(pool, src_cols, w, 0, b_idx, w.t * 2 + 1)
                    gather(x1, b_x1, xs, w, 0, b_xs)
                    slot_free(pool, b_es, w, J)
                    need(pool, b_et, w.t - 3)
                    stage_indices(pool, edge_cols, w, 1, b_idx, w.t * 2 + 2)
                    gather(edge_attr, b_edge, es, w, 1, b_es)

                pipelined(pool, ET, [(0, gather_both)])

            @block.sync
            def _(sp):
                def load_keep(w):
                    need(sp, b_sc, (w.t - 3) * C)
                    sp.dma_start(keeps[:, w.slot(4), :], keep_row[ds(w.t * TILE, TILE)].partition_broadcast(P)
                                 ).then_inc(b_kp[w.slot(4)], 16)

                pipelined(sp, ET, [(0, load_keep)])

            @block.tensor
            def _(pe):
                def turn_x(w):
                    landed(pe, b_xs, w, J)
                    need(pe, b_ef, w.t)
                    for c in range(C):
                        mm = transpose_rows(xs[:, w.slot(4), :, :], ps_t, 1 - c, P)
                    mm.then_inc(b_xt, 1)

                def turn_e(w):
                    landed(pe, b_es, w, J)
                    pe.wait_ge(b_xf, w.t + 1)
                    for c in range(C):
                        mm = transpose_rows(es[:, w.slot(4), :, :], ps_t, 1 - c, P)
                    mm.then_inc(b_et, 1)

                def transform(w, folded, fold, copied, dest, done):
                    pe.wait_ge(fold, w.t + 1)
                    need(pe, copied, w.t)
                    for m in range(2):
                        mm = nc.tensor.matmul(dest[:, m, :], dft_sb[:, m, :], folded[:, w.slot(2), m, :],
                                              start=True, stop=True)
                    mm.then_inc(done, 1)

                def dft_x(w):
                    transform(w, fold_x, b_xf, b_fxc, ps_fx, b_fx)

                def dft_e(w):
                    transform(w, fold_e, b_ef, b_fec, ps_fe, b_fe)

                def message(w):
                    need(pe, b_rows, w.t * 2)
                    pe.wait_ge(b_sc, (w.t + 1) * C)
                    for j in range(J):
                        for c in range(C):
                            mm = nc.tensor.matmul(ps_m[:, j, :], zs[:, w.slot(2), c, j * P:(j + 1) * P],
                                                  w_msg[:, c, :], start=(c == 0), stop=(c == C - 1))
                    mm.then_inc(b_msg, 1)

                pipelined(pe, ET, [(0, turn_x), (1, dft_x), (1, dft_e), (0, turn_e), (3, message)])

            @block.scalar
            def _(act):
                def upper_half(w, turned, dest, folded, done):
                    act.wait_ge(turned, w.t + 1)
                    need(act, folded, w.t)
                    nc.scalar.activation(dest[:, :], ps_t[:, 1, :], ACT.Copy).then_inc(done, 1)

                def upper_of_x(w):
                    upper_half(w, b_xt, upper_x, b_xf, b_xh)

                def upper_of_e(w):
                    upper_half(w, b_et, upper_e, b_ef, b_eh)

                def spectrum(w, source, transformed, dest, done):
                    act.wait_ge(transformed, w.t + 1)
                    need(act, b_prod, w.t - 1)
                    for part_of in range(2):
                        for m in range(2):
                            a = nc.scalar.activation(dest[m * H:(m + 1) * H, w.slot(2), part_of, :],
                                                     source[part_of * H:(part_of + 1) * H, m, :], ACT.Copy)
                    a.then_inc(done, 1)

                def spectrum_x(w):
                    spectrum(w, ps_fx, b_fx, fx, b_fxc)

                def spectrum_e(w):
                    spectrum(w, ps_fe, b_fe, fe, b_fec)

                def copy_rows(w):
                    slot_free(act, b_st, w)
                    act.wait_ge(b_msg, w.t + 1)
                    for k in range(2):
                        nc.scalar.activation(rows[:, w.slot(4), 2 * k:2 * k + 2, :], ps_m[:, 2 * k:2 * k + 2, :],
                                             ACT.Copy).then_inc(b_rows, 1)

                def store_rows(w):
                    act.wait_ge(b_rows, (w.t + 1) * 2)
                    act.dma_start(edge_rows(agg_rows, w.t), rows[:, w.slot(4), :, :]).then_inc(b_st[w.slot(4)], 16)

                pipelined(act, ET, [(0, upper_of_x), (1, spectrum_x), (1, spectrum_e), (0, upper_of_e),
                                    (3, copy_rows), (4, store_rows)])
                all_stored(act, b_st, ET)

            @block.vector
            def _(dve):
                v = nc.vector
                v.memset(zs[:, 1, :, TILE - 1:TILE], 0.0).then_inc(b_init, 1)
                dve.wait_ge(b_init, 1)

                def fold(w, copied, upper_sb, dest, used, done):
                    dve.wait_ge(copied, w.t + 1)
                    need(dve, used, w.t - 1)
                    v.tensor_tensor(out=dest[:, w.slot(2), 0, :], in0=ps_t[:, 0, :], in1=upper_sb[:, :], op=ALU.add)
                    v.tensor_tensor(out=dest[:, w.slot(2), 1, :], in0=ps_t[:, 0, :], in1=upper_sb[:, :],
                                    op=ALU.subtract).then_inc(done, 1)

                def fold_nodes(w):
                    fold(w, b_xh, upper_x, fold_x, b_fx, b_xf)

                def fold_edges(w):
                    fold(w, b_eh, upper_e, fold_e, b_fe, b_ef)

                def multiply(w):
                    s = w.slot(2)
                    dve.wait_ge(b_fxc, w.t + 1)
                    dve.wait_ge(b_fec, w.t + 1)
                    need(dve, b_z, w.t * C)
                    v.tensor_tensor(out=prod[:, 0, :], in0=fx[:, s, 0, :], in1=fe[:, s, 0, :], op=ALU.mult)
                    v.tensor_tensor(out=prod[:, 1, :], in0=fx[:, s, 1, :], in1=fe[:, s, 1, :], op=ALU.mult)
                    v.tensor_tensor(out=prod[:, 2, :], in0=fx[:, s, 1, :], in1=fe[:, s, 0, :], op=ALU.mult)
                    v.scalar_tensor_tensor(out=prod[:, 3, :], in0=fx[:, s, 0, :], scalar=sig[:, 0:1],
                                           in1=fe[:, s, 1, :], op0=ALU.mult, op1=ALU.mult).then_inc(b_prod, 1)

                def combine(w):
                    dve.wait_ge(b_prod, w.t + 1)
                    need(dve, b_sc, w.t * C)
                    v.tensor_tensor(out=z[:, 0, :], in0=prod[:, 0, :], in1=prod[:, 1, :], op=ALU.add).then_inc(b_z, 1)
                    v.tensor_tensor(out=z[:, 1, :], in0=prod[:, 2, :], in1=prod[:, 3, :],
                                    op=ALU.subtract).then_inc(b_z, 1)

                def running_sum(w):
                    landed(dve, b_kp, w)
                    need(dve, b_msg, w.t - 1)
                    for m in range(C):
                        dve.wait_ge(b_z, w.t * C + m + 1)
                        v.tensor_tensor_scan(out=zs[:, w.slot(2), m, :], data0=keeps[:, w.slot(4), :],
                                             data1=z[:, m, :], initial=zs[:, 1 - w.slot(2), m, TILE - 1:TILE],
                                             op0=ALU.mult, op1=ALU.add).then_inc(b_sc, 1)

                pipelined(dve, ET, [(0, fold_nodes), (2, multiply), (0, fold_edges), (2, combine), (2, running_sum)])

        q_idx = sem("q_idx")
        q_ag = ring_sems("q_ag")
        q_x = ring_sems("q_x")
        q_st = ring_sems("q_st")
        q_xt = sem("q_xt")
        q_xtc = sem("q_xtc")
        q_nrm = sem("q_nrm")
        q_h = sem("q_h")
        q_hc = sem("q_hc")
        q_bn = sem("q_bn")
        q_init = sem("q_init")
        f_v = sem("f_v")
        f_s = sem("f_s")
        mem = ExitStack()
        with mem, nc.Block() as block:
            ag = sb("ag", [P, 4, J, D], at=mem)
            an = sb("an", [P, 2, J, D], at=mem)
            xr = sb("q_xr", [P, 4, J, D], at=mem)
            xt = sb("q_xt_sb", [P, 2, C, TILE], at=mem)
            hs = sb("hs", [P, 4, C, TILE], at=mem)
            mv = sb("q_mv", [P, C, 2], at=mem)
            ps_x = ps("q_ps_x", [P, 2, C, TILE], mem)
            ps_h = ps("q_ps_h", [P, 2, C, TILE], mem)

            @block.gpsimd
            def _(pool):
                pool.wait_ge(q_init, 1)
                b_agg = nc.gpsimd.to_reg(EP - 1)

                def gather_agg(w):
                    slot_free(pool, q_ag, w, J)
                    need(pool, q_nrm, w.t - 3)
                    stage_indices(pool, ptr, w, 0, q_idx, w.t + 1)
                    gather(agg_rows, b_agg, ag, w, 0, q_ag)

                pipelined(pool, NT, [(0, gather_agg)])

            @block.sync
            def _(sp):
                def load_x1(w):
                    n = TP if w.last else P
                    need(sp, q_xt, (w.t - 3) * C)
                    sp.dma_start(xr[0:n, w.slot(4), :, :], node_rows(x1, w.t, w.last)).then_inc(q_x[w.slot(4)], 16)

                pipelined(sp, NT, [(0, load_x1)])

            @block.tensor
            def _(pe):
                def turn(w):
                    n = TP if w.last else P
                    landed(pe, q_x, w)
                    need(pe, q_xtc, (w.t - 1) * C)
                    for c in range(C):
                        transpose_rows(xr[:, w.slot(4), :, :], ps_x[:, w.slot(2), :, :], c, n).then_inc(q_xt, 1)

                def project(w):
                    n = TP if w.last else P
                    s = w.slot(2)
                    need(pe, q_hc, (w.t - 1) * C)
                    pe.wait_ge(q_xtc, (w.t + 1) * C)
                    pe.wait_ge(q_nrm, w.t + 1)
                    for m in range(C):
                        for c in range(C):
                            nc.tensor.matmul(part(ps_h[:, s, :, :], m, n), w_h[:, c, m * P:(m + 1) * P],
                                             part(xt[:, s, :, :], c, n), start=(c == 0), stop=False)
                        for j in range(J):
                            mm = nc.tensor.matmul(ps_h[:, s, m, j * P:j * P + n],
                                                  an[0:n, s, j, m * P:(m + 1) * P], ident[0:n, 0:n],
                                                  is_transpose=True, start=False, stop=(j == J - 1))
                        mm.then_inc(q_h, 1)

                pipelined(pe, NT, [(0, turn), (1, project)])

            @block.scalar
            def _(act):
                def copy_xt(w):
                    n = TP if w.last else P
                    need(act, q_h, (w.t - 1) * C)
                    for c in range(C):
                        act.wait_ge(q_xt, w.t * C + c + 1)
                        nc.scalar.activation(part(xt[:, w.slot(2), :, :], c, n),
                                             part(ps_x[:, w.slot(2), :, :], c, n), ACT.Copy).then_inc(q_xtc, 1)

                def add_bias(w):
                    n = TP if w.last else P
                    slot_free(act, q_st, w)
                    need(act, q_bn, (w.t - 3) * C)
                    for m in range(C):
                        act.wait_ge(q_h, w.t * C + m + 1)
                        nc.scalar.activation(part(hs[:, w.slot(4), :, :], m, n),
                                             part(ps_h[:, w.slot(2), :, :], m, n),
                                             ACT.Identity, bias=wb_col[:, m:m + 1]).then_inc(q_hc, 1)

                def store_h(w):
                    act.wait_ge(q_hc, (w.t + 1) * C)
                    source = hs[:, w.slot(4), :, :]
                    dest = h_t[ds(w.t, 1), :, :].rearrange("o p n -> (o p) n")
                    if w.last:
                        for c in range(C):
                            act.dma_start(part(dest.rearrange("p (c n) -> p c n", c=C), c, TP),
                                          part(source, c, TP)).then_inc(q_st[w.slot(4)], 16)
                    else:
                        act.dma_start(dest, source.rearrange("p c n -> p (c n)")).then_inc(q_st[w.slot(4)], 16)

                pipelined(act, NT, [(0, copy_xt), (1, add_bias), (2, store_h)])
                all_stored(act, q_st, NT, (C - 1) * 16)
                act.wait_ge(f_v, 1)
                nc.scalar.activation(bn_scale[:, :], mv[:, :, 1], ACT.Sqrt, bias=eps_col[:, :]).then_inc(f_s, 1)

            @block.vector
            def _(dve):
                v = nc.vector
                v.memset(ag[:, :, :, :], 0.0).then_inc(q_init, 1)

                def scale_sum(w):
                    n = TP if w.last else P
                    landed(dve, q_ag, w, J)
                    need(dve, q_h, (w.t - 1) * C)
                    for j in range(J):
                        a = v.tensor_scalar(out=an[0:n, w.slot(2), j, :], in0=ag[0:n, w.slot(4), j, :],
                                            scalar1=norm_node[0:n, ds(w.t * J + j, 1)], scalar2=None, op0=ALU.mult)
                    a.then_inc(q_nrm, 1)

                def statistics(w):
                    n = TP if w.last else P
                    for m in range(C):
                        dve.wait_ge(q_hc, w.t * C + m + 1)
                        v.bn_stats(out=h_stats[:, m, ds(w.t * 6, 6)], in_=part(hs[:, w.slot(4), :, :], m, n)
                                   ).then_inc(q_bn, 1)

                pipelined(dve, NT, [(0, scale_sum), (2, statistics)])
                dve.wait_ge(q_bn, NT * C)
                for m in range(C):
                    a = v.bn_aggr(out=mv[:, m, :], in_=h_stats[:, m, :])
                a.then_inc(f_v, 1)
                dve.wait_ge(f_s, 1)
                v.reciprocal(out=bn_scale[:, :], in_=bn_scale[:, :]).then_inc(f_v, 1)
                dve.wait_ge(f_v, 2)
                v.tensor_tensor(out=bn_scale[:, :], in0=bn_scale[:, :], in1=gam_col[:, :], op=ALU.mult).then_inc(f_v, 1)
                dve.wait_ge(f_v, 3)
                v.tensor_tensor(out=bn_shift[:, :], in0=mv[:, :, 0], in1=bn_scale[:, :], op=ALU.mult).then_inc(f_v, 1)
                dve.wait_ge(f_v, 4)
                v.tensor_tensor(out=bn_shift[:, :], in0=bet_col[:, :], in1=bn_shift[:, :], op=ALU.subtract)

        r_h = ring_sems("r_h")
        r_x = ring_sems("r_x")
        r_st = ring_sems("r_st")
        r_th = sem("r_th")
        r_bk = sem("r_bk")
        r_sum = sem("r_sum")
        r_s6 = sem("r_s6")
        r_join = sem("r_join")
        r_var = sem("r_var")
        r_ve = sem("r_ve")
        r_rs = sem("r_rs")
        r_nb = sem("r_nb")
        r_y = sem("r_y")
        r_init = sem("r_init")
        mem = ExitStack()
        with mem, nc.Block() as block:
            ht = sb("ht", [P, 4, C, TILE], at=mem)
            th = sb("th", [P, 2, C, TILE], at=mem)
            xr = sb("r_xr", [P, 4, J, D], at=mem)
            res = sb("r_res", [P, 4, J, D], at=mem)
            yo = sb("r_yo", [P, 4, J, D], at=mem)
            s6 = sb("r_s6_sb", [P, 2, J, 6], at=mem)
            ms = sb("r_ms", [P, 4, 2, J], at=mem)
            tmp = sb("r_tmp", [P, 2, 3, J], at=mem)
            ve = sb("ve", [P, 2, J], at=mem)
            rs = sb("r_rs_sb", [P, 2, J], at=mem)
            nb = sb("r_nb_sb", [P, 2, J], at=mem)
            mhalf = sb("mhalf", [P, J], at=mem)
            eps4 = sb("eps4", [P, J], at=mem)
            ps_y = ps("ps_y", [P, 2, J, D], mem)

            @block.sync
            def _(sp):
                def load(w):
                    n = TP if w.last else P
                    s = w.slot(4)
                    need(sp, r_th, w.t - 3)
                    source = h_t[ds(w.t, 1), :, :].rearrange("o p n -> (o p) n")
                    if w.last:
                        for c in range(C):
                            sp.dma_start(part(ht[:, s, :, :], c, TP),
                                         part(source.rearrange("p (c n) -> p c n", c=C), c, TP)
                                         ).then_inc(r_h[s], 16)
                    else:
                        sp.dma_start(ht[:, s, :, :].rearrange("p c n -> p (c n)"), source).then_inc(r_h[s], 16)
                    need(sp, r_sum, (w.t - 3) * 2)
                    sp.dma_start(xr[0:n, s, :, :], node_rows(x1, w.t, w.last)).then_inc(r_x[s], 16)

                pipelined(sp, NT, [(0, load)])

            @block.scalar
            def _(act):
                def squash(w):
                    n = TP if w.last else P
                    landed(act, r_h, w, extra=16 * (C - 1) if w.last else 0)
                    need(act, r_bk, w.t - 1)
                    for m in range(C):
                        a = nc.scalar.activation(part(th[:, w.slot(2), :, :], m, n), part(ht[:, w.slot(4), :, :], m, n),
                                                 ACT.Tanh, bias=bn_shift[:, m:m + 1], scale=bn_scale[:, m:m + 1])
                    a.then_inc(r_th, 1)

                def normalise(w):
                    n = TP if w.last else P
                    s = w.slot(2)
                    slot_free(act, r_st, w)
                    act.wait_ge(r_nb, w.t + 1)
                    for j in range(J):
                        a = nc.scalar.activation(yo[0:n, w.slot(4), j, :], res[0:n, w.slot(4), j, :], ACT.Identity,
                                                 bias=nb[0:n, s, j:j + 1], scale=rs[0:n, s, j:j + 1])
                    a.then_inc(r_y, 1)

                def store(w):
                    n = TP if w.last else P
                    act.wait_ge(r_y, w.t + 1)
                    act.dma_start(node_rows(out, w.t, w.last), yo[0:n, w.slot(4), :, :]).then_inc(r_st[w.slot(4)], 16)

                pipelined(act, NT, [(0, squash), (4, normalise), (5, store)])
                all_stored(act, r_st, NT)

            @block.tensor
            def _(pe):
                def back(w):
                    n = TP if w.last else P
                    pe.wait_ge(r_th, w.t + 1)
                    need(pe, r_sum, (w.t - 1) * 2)
                    for c in range(C):
                        mm = transpose_back(th[:, w.slot(2), :, :], ps_y[:, w.slot(2), :, :], c, n)
                    mm.then_inc(r_bk, 1)

                pipelined(pe, NT, [(0, back)])

            @block.vector
            def _(dve):
                v = nc.vector
                v.memset(eps4[:, :], EPS)
                v.memset(mhalf[:, :], -0.5).then_inc(r_init, 1)

                def add(w):
                    n = TP if w.last else P
                    s = w.slot(4)
                    dve.wait_ge(r_bk, w.t + 1)
                    landed(dve, r_x, w)
                    need(dve, r_y, w.t - 3)
                    for k in range(2):
                        v.tensor_tensor(out=res[0:n, s, 2 * k:2 * k + 2, :], in0=xr[0:n, s, 2 * k:2 * k + 2, :],
                                        in1=ps_y[0:n, w.slot(2), 2 * k:2 * k + 2, :], op=ALU.add).then_inc(r_sum, 1)

                def statistics(w):
                    n = TP if w.last else P
                    dve.wait_ge(r_sum, (w.t + 1) * 2)
                    need(dve, r_var, w.t - 1)
                    half_statistics(res[:, w.slot(4), :, :], s6[:, w.slot(2), :, :], n).then_inc(r_s6, 1)

                def variance(w):
                    n = TP if w.last else P
                    dve.wait_ge(r_s6, w.t + 1)
                    need(dve, r_nb, w.t - 3)
                    join_halves(dve, s6[:, w.slot(2), :, :], ms[:, w.slot(4), :, :], tmp[:, w.slot(2), :, :], n,
                                r_join, w.t * 2 + 1).then_inc(r_var, 1)

                def shift(w):
                    n = TP if w.last else P
                    dve.wait_ge(r_rs, w.t + 1)
                    need(dve, r_y, w.t - 1)
                    v.scalar_tensor_tensor(out=nb[0:n, w.slot(2), :], in0=ms[0:n, w.slot(4), 0, :], scalar=-0.5,
                                           in1=rs[0:n, w.slot(2), :], op0=ALU.mult, op1=ALU.mult).then_inc(r_nb, 1)

                pipelined(dve, NT, [(3, shift), (1, add), (2, statistics), (2, variance)])

            @block.gpsimd
            def _(pool):
                pool.wait_ge(r_init, 1)

                def rsqrt(w):
                    n = TP if w.last else P
                    s = w.slot(2)
                    pool.wait_ge(r_var, w.t + 1)
                    need(pool, r_rs, w.t - 1)
                    nc.gpsimd.tensor_tensor(out=ve[0:n, s, :], in0=ms[0:n, w.slot(4), 1, :], in1=eps4[0:n, :],
                                            op=ALU.add).then_inc(r_ve, 1)
                    pool.wait_ge(r_ve, w.t + 1)
                    need(pool, r_y, w.t - 1)
                    nc.gpsimd.tensor_tensor(out=rs[0:n, s, :], in0=ve[0:n, s, :], in1=mhalf[0:n, :],
                                            op=ALU.pow).then_inc(r_rs, 1)

                pipelined(pool, NT, [(0, rsqrt)])


def constants(d):
    import numpy as np
    n = np.arange(d)
    m = np.arange(d // 4)
    even, odd = (n % 2 == 0) * 1.0, (n % 2 == 1) * 1.0
    fwd = np.zeros((d // 2, 2, d // 2))
    cosines, sines = [], []
    for k in range(2):
        angle = 2 * np.pi * np.outer(n, 2 * m + k) / d
        cos, sin = np.cos(angle), np.sin(angle)
        if k == 0:
            cos[:, 0], sin[:, 0] = even, odd
        fwd[:, k, :] = np.concatenate([cos, sin], 1)[:d // 2]
        inv_cos, inv_sin = 2 * cos / d, -2 * sin / d
        if k == 0:
            inv_sin[:, 0] *= -1
        cosines.append(inv_cos)
        sines.append(inv_sin)
    sigma = np.ones((P, 1))
    sigma[0] = -1
    return {
        "identity": np.eye(P, dtype=np.float32),
        "upper": np.triu(np.ones((P, P), np.float32), 1),
        "dft": fwd.astype(np.float32),
        "idft_t": np.concatenate(cosines + sines, 1).astype(np.float32),
        "sigma": sigma.astype(np.float32),
    }


def lay_out(inputs):
    import numpy as np
    a = {k: np.asarray(v) for k, v in inputs.items()}
    rel = a["L1_gnn_loop_rel"][0]
    out = {
        "x": a["x"], "src": a["src"], "dst": a["dst"], "edge_attr": a["edge_attr_256"],
        "theta_t": a["L0_gnn_theta_w"].T, "theta_b": a["L0_gnn_theta_b"],
        "phi_t": a["L0_gnn_phi_w"].T, "phi_b": a["L0_gnn_phi_b"],
        "w_loop": a["L1_gnn_w_loop"], "w_in": a["L1_gnn_w_in"], "loop_rel2": np.concatenate([rel, rel]),
        "w_bias": a["L1_gnn_w_bias"], "bn_gamma": a["L1_gnn_bn_gamma"], "bn_beta": a["L1_gnn_bn_beta"],
    }
    out.update(constants(rel.shape[0]))
    return {k: np.ascontiguousarray(v) for k, v in out.items()}


def build(nc, arrays):
    args = [nc.dram_tensor(f"in_{k}", v.shape, mybir.dt.from_np(v.dtype), kind="ExternalInput").ap()
            for k, v in arrays.items()]
    out = nc.dram_tensor("out_0", arrays["x"].shape, F32, kind="ExternalOutput").ap()
    gnn_kernel(nc, *args, out)


def kernel(**inputs):
    import concourse.bacc as _bacc
    from concourse.bass_utils import run_bass_kernel_spmd as _run

    nc = _bacc.Bacc("TRN2", target_bir_lowering=False, num_devices=1)
    arrays = lay_out(inputs)
    build(nc, arrays)
    r = _run(nc, [{f"in_{k}": v for k, v in arrays.items()}], core_ids=[0])
    return r.results[0]["out_0"]
```

```python
import concourse.bass as bass
from concourse import mybir
from concourse.bass import ds
from contextlib import ExitStack

F32 = mybir.dt.float32
F32R = mybir.dt.float32r
BF16 = mybir.dt.bfloat16
I32 = mybir.dt.int32
ALU = mybir.AluOpType
ACT = mybir.ActivationFunctionType
AX = mybir.AxisListType

P = 128
UNROLL = 4
J = 4
GROUP = 2
TILE = P * J
HUGE = 3.38e38
SHARE = 3136
MISSING = 1 << 20
EPS = 1e-5


def need(eng, sem, value):
    if isinstance(value, int) and value <= 0:
        return
    eng.wait_ge(sem, value)


class Step:

    def __init__(self, base, k, last):
        self.base, self.k, self.last = base, k, last
        self.t = k if base is None else base * UNROLL + k

    def slot(self, n):
        return self.k % n

    def turn(self, n):
        return self.k // n if self.base is None else base_plus(self.base, UNROLL // n, self.k // n)


def base_plus(base, times, more):
    return (base if times == 1 else base * times) + more


def pipelined(eng, tiles, stages):
    depth = max(lag for lag, _ in stages)
    first = -(-(depth + UNROLL) // UNROLL) * UNROLL
    rounds = max(0, (tiles - 1 - first) // UNROLL)

    def straight(t):
        for lag, step in stages:
            if 0 <= t - lag < tiles:
                step(Step(None, t - lag, t - lag == tiles - 1))

    if rounds == 0:
        first = 0
    for t in range(first):
        straight(t)
    if rounds:
        with eng.Fori(0, rounds) as i:
            for u in range(UNROLL):
                for lag, step in stages:
                    step(Step(i, first + u - lag, False))
    for t in range(first + UNROLL * rounds, tiles + depth):
        straight(t)


def gnn_kernel(nc, x, src, dst, edge_attr, theta_t, theta_b, phi_t, phi_b, w_loop, w_in, loop_rel2,
               w_bias, bn_gamma, bn_beta, identity, upper, dft, idft_t, sigma, out):
    N, D = x.shape
    E = src.shape[0]
    C = D // P
    H = P // 2
    assert D == 256 and N % J == 0
    NT = -(-N // TILE)
    TP = (N - (NT - 1) * TILE) // J
    ET = -(-E // TILE)
    EP = ET * TILE
    EC = EP // P
    ER = EP // D
    HC = EC // 2
    assert EC % 2 == 0 and HC <= P and ER <= P
    NQ = NT * J
    PAD_DST = (NT + 16) * TILE

    sorted_lists = [nc.dram_tensor(f"{n}_sorted", (1 + EP, 1), I32, kind="Internal").ap()
                    for n in ("src", "dst", "edge")]
    cap_row = nc.dram_tensor("cap_row", (EP,), BF16, kind="Internal").ap()
    keep_row = nc.dram_tensor("keep_row", (EP,), BF16, kind="Internal").ap()
    max_rows = nc.dram_tensor("max_rows", (EP, D), F32, kind="Internal").ap()
    agg_rows = nc.dram_tensor("agg_rows", (EP, D), F32, kind="Internal").ap()
    x1 = nc.dram_tensor("x1", (N, D), F32, kind="Internal").ap()
    h_t = nc.dram_tensor("h_t", (NT, P, C * TILE), F32, kind="Internal").ap()

    def node_rows(table, t, last):
        rows = TP * J if last else TILE
        return table[ds(t * TILE, rows), :].rearrange("(p j) c -> p j c", j=J)

    def edge_rows(table, t):
        return table[ds(t * TILE, TILE), :].rearrange("(p j) c -> p j c", j=J)

    ctx = ExitStack()
    with ctx:
        def sb(name, shape, dt=F32, at=ctx):
            return at.enter_context(nc.sbuf_tensor(name, shape, dt))

        def ps(name, shape, at):
            return at.enter_context(nc.psum_tensor(name, shape, F32))

        def sem(name):
            return ctx.enter_context(nc.semaphore(name))

        ident = sb("ident", [P, P])
        ones = sb("ones", [P, P])
        sig = sb("sig", [P, 1])
        w_h = [sb(f"w_h{k}", [P, C, D], F32R) for k in range(2)]
        bias_col = sb("bias_col", [P, C])
        wb_col = sb("wb_col", [P, C])
        gam_col = sb("gam_col", [P, C])
        bet_col = sb("bet_col", [P, C])
        eps_col = sb("eps_col", [P, 1])
        deg = sb("deg", [P, NQ])
        ptr = sb("ptr", [P, NQ], I32)
        has_edges = sb("has_edges", [P, NQ])
        norm_node = sb("norm_node", [P, NQ])
        h_stats = sb("h_stats", [P, C, NT * 6])
        bn_scale = sb("bn_scale", [P, C])
        bn_shift = sb("bn_shift", [P, C])
        idx = sb("idx", [P, 2, 2 * GROUP * J], I32)
        unsorted = sb("unsorted", [P, 1], I32)

        early = ExitStack()
        up = sb("up", [P, P], at=early)
        w_dst = sb("w_dst", [P, C, D], at=early)
        w_src = [sb(f"w_src{k}", [P, C, D], F32R, at=early) for k in range(2)]
        dft_sb = sb("dft_sb", [P, 2, P], at=early)
        w_msg = [sb(f"w_msg{k}", [P, C, D], F32R, at=early) for k in range(2)]
        src_cols = sb("src_cols", [P, EC], I32, at=early)
        edge_cols = sb("edge_cols", [P, EC], I32, at=early)
        dst_p = sb("dst_p", [P, EC], at=early)
        dst_q = sb("dst_q", [P, EC], at=early)
        hankel = sb("hankel", [P, C, D], at=early)
        wl = sb("wl", [P, C, D], at=early)
        wi = sb("wi", [P, C, D], at=early)
        idft_sb = sb("idft_sb", [P, C, D], at=early)

        small = ExitStack()
        w_diff = sb("w_diff", [P, C, D], at=small)
        raw_phi = sb("raw_phi", [P, C, D], at=small)
        b_col = sb("b_col", [P, 2, C], at=small)
        d_now = sb("d_now", [ER, D], I32, at=small)
        d_before = sb("d_before", [ER, D], I32, at=small)
        keep = sb("keep", [ER, D], BF16, at=small)
        cap = sb("cap", [ER, D], BF16, at=small)
        falls = sb("falls", [ER, D], at=small)
        fall_sum = sb("fall_sum", [ER, 1], at=small)
        ints = sb("ints", [HC, 3, 2, P], I32, at=small)
        floats = sb("floats", [HC, 3, 2, P], at=small)
        dst_cols = sb("dst_cols", [P, EC], I32, at=small)
        t_a = sb("t_a", [P, EC], I32, at=small)
        t_b = sb("t_b", [P, EC], I32, at=small)
        t_c = sb("t_c", [P, EC], I32, at=small)
        n_shares = -(-E // SHARE)
        own_edge = sb("own_edge", [P, n_shares, EC], at=small)
        every_edge = sb("every_edge", [P, SHARE], at=small)
        every_dst = sb("every_dst", [P, SHARE], I32, at=small)
        earlier = sb("earlier", [P, SHARE], at=small)
        precedes = sb("precedes", [P, SHARE], at=small)
        dst_f = sb("dst_f", [P, EC], at=small)
        part_rank = sb("part_rank", [P, EC, n_shares], at=small)
        rank = sb("rank", [P, EC], at=small)
        rank_pad = sb("rank_pad", [P, EC], at=small)
        rank_int = sb("rank_int", [P, EC], I32, at=small)
        moved = sb("moved", [P, 4], I32, at=small)
        ps_i = ps("ps_i", [P, 3, 512], small)
        ps_f = ps("ps_f", [P, 512], small)

        def chunks(w):
            return w.rearrange("(c p) n -> p c n", p=P)

        def load_column(eng, dest, v, done):
            for c in range(C):
                eng.dma_start(dest[:, c:c + 1], v[c * P:(c + 1) * P].rearrange("(p o) -> p o", o=1)).then_inc(done, 16)

        def list_masks(dve, step, first, ready):
            v = nc.vector
            v.tensor_tensor(out=keep[:, :], in0=d_now[:, :], in1=d_before[:, :], op=ALU.is_equal).then_inc(step, 1)
            dve.wait_ge(step, first)
            v.tensor_scalar(out=cap[:, :], in0=keep[:, :], scalar1=2.0, scalar2=1.0, op0=ALU.mult,
                            op1=ALU.subtract).then_inc(step, 1)
            dve.wait_ge(step, first + 1)
            v.tensor_scalar(out=cap[:, :], in0=cap[:, :], scalar1=HUGE, scalar2=None, op0=ALU.mult).then_inc(ready, 1)

        def dst_places(dve, step, first):
            v = nc.vector
            v.tensor_scalar(out=t_a[:, :], in0=dst_cols[:, :], scalar1=2, scalar2=P - 1,
                            op0=ALU.logical_shift_right, op1=ALU.bitwise_and)
            v.tensor_scalar(out=t_b[:, :], in0=dst_cols[:, :], scalar1=9, scalar2=2,
                            op0=ALU.logical_shift_right, op1=ALU.logical_shift_left)
            v.tensor_scalar(out=t_c[:, :], in0=dst_cols[:, :], scalar1=J - 1, scalar2=None,
                            op0=ALU.bitwise_and).then_inc(step, 1)
            dve.wait_ge(step, first)
            v.tensor_copy(out=dst_p[:, :], in_=t_a[:, :])
            v.tensor_tensor(out=t_b[:, :], in0=t_b[:, :], in1=t_c[:, :], op=ALU.bitwise_or).then_inc(step, 1)
            dve.wait_ge(step, first + 1)
            v.tensor_copy(out=dst_q[:, :], in_=t_b[:, :])

        def store_masks(sp, ready, stored, times):
            sp.wait_ge(ready, times)
            sp.dma_start(cap_row.rearrange("(r c) -> r c", c=D), cap[:, :]).then_inc(stored, 16)
            sp.dma_start(keep_row.rearrange("(r c) -> r c", c=D), keep[:, :]).then_inc(stored, 16)
            sp.wait_ge(stored, times * 2 * 16)

        def turn_lists(numbers):
            for n in numbers:
                for half in range(2):
                    last = nc.tensor.transpose(ps_i[:, n, half * HC:(half + 1) * HC], floats[:, n, half, :],
                                               ident[0:HC, 0:HC])
            return last

        carrier = sem("carrier")
        loaded = sem("loaded")
        loaded_w = sem("loaded_w")
        lists_loaded = sem("lists_loaded")
        nb_loaded = sem("nb_loaded")
        blank = sem("blank")
        edge_iota = sem("edge_iota")
        prep_v = sem("prep_v")
        prep_t = sem("prep_t")
        masks_ready = sem("masks_ready")
        masks_stored = sem("masks_stored")
        with nc.Block() as block:
            @block.sync
            def _(sp):
                full, rest = divmod(E, P)
                sp.wait_ge(blank, 1)
                for n, v in ((0, src), (1, dst)):
                    sp.dma_start(ints[:, n, 0, :],
                                 v[0:HC * P].rearrange("(r c) -> r c", c=P)).then_inc(lists_loaded, 16)
                    sp.dma_start(ints[0:full - HC, n, 1, :],
                                 v[HC * P:full * P].rearrange("(r c) -> r c", c=P)).then_inc(lists_loaded, 16)
                    sp.dma_start(ints[full - HC:full - HC + 1, n, 1, 0:rest],
                                 v[full * P:E].rearrange("(r c) -> r c", r=1)).then_inc(lists_loaded, 16)
                full, rest = divmod(E, D)
                sp.dma_start(d_now[0:full, :], dst[0:full * D].rearrange("(r c) -> r c", c=D)).then_inc(nb_loaded, 16)
                sp.dma_start(d_now[full:full + 1, 0:rest],
                             dst[full * D:E].rearrange("(r c) -> r c", r=1)).then_inc(nb_loaded, 16)
                sp.dma_start(d_before[0:1, 1:D], dst[0:D - 1].rearrange("(r c) -> r c", r=1)).then_inc(nb_loaded, 16)
                sp.dma_start(d_before[1:full, :],
                             dst[D - 1:full * D - 1].rearrange("(r c) -> r c", c=D)).then_inc(nb_loaded, 16)
                sp.dma_start(d_before[full:full + 1, 0:rest + 1],
                             dst[full * D - 1:E].rearrange("(r c) -> r c", r=1)).then_inc(nb_loaded, 16)
                store_masks(sp, masks_ready, masks_stored, 1)

            @block.scalar
            def _(act):
                act.dma_start(ident[:, :], identity).then_inc(loaded, 16)
                act.wait_ge(loaded, 16)
                for dest, w in ((w_dst, theta_t), (raw_phi, phi_t)):
                    act.dma_start(dest[:, :, :], chunks(w)).then_inc(loaded_w, 16)
                act.dma_start(up[:, :], upper).then_inc(loaded, 16)
                for dest, v in ((b_col[:, 0, :], theta_b), (b_col[:, 1, :], phi_b)):
                    load_column(act, dest, v, loaded)

            @block.gpsimd
            def _(pool):
                nc.gpsimd.iota(edge_cols[:, :], [[P, EC]], base=0, channel_multiplier=1).then_inc(edge_iota, 1)

            @block.vector
            def _(dve):
                v = nc.vector
                v.memset(ints[:, 0, :, :], 0)
                v.memset(ints[:, 1, :, :], PAD_DST)
                v.memset(d_now[:, :], PAD_DST)
                v.memset(d_before[:, :], PAD_DST).then_inc(prep_v, 1)
                dve.wait_ge(prep_v, 1)
                v.memset(d_before[0:1, 0:1], -1).then_inc(blank, 1)
                v.memset(ones[:, :], 1.0)
                v.memset(eps_col[:, :], EPS)
                v.memset(idx[:, :, :], 0)
                dve.wait_ge(lists_loaded, 6 * 16)
                v.tensor_copy(out=floats[:, 0:2, :, :], in_=ints[:, 0:2, :, :]).then_inc(prep_v, 1)
                dve.wait_ge(nb_loaded, 5 * 16)
                list_masks(dve, prep_v, 3, masks_ready)
                v.tensor_tensor(out=falls[:, :], in0=d_now[:, :], in1=d_before[:, :], op=ALU.is_lt).then_inc(prep_v, 1)
                dve.wait_ge(prep_v, 5)
                v.tensor_reduce(out=fall_sum[:, :], in_=falls[:, :], axis=AX.X, op=ALU.add).then_inc(prep_v, 1)
                dve.wait_ge(prep_t, 1)
                v.tensor_copy(out=src_cols[:, :], in_=ps_i[:, 0, 0:EC])
                v.tensor_copy(out=dst_cols[:, :], in_=ps_i[:, 1, 0:EC])
                dve.wait_ge(edge_iota, 1)
                v.tensor_scalar(out=edge_cols[:, :], in0=edge_cols[:, :], scalar1=float(E - 1), scalar2=None,
                                op0=ALU.min).then_inc(prep_v, 1)
                dve.wait_ge(prep_t, 2)
                v.tensor_copy(out=unsorted[:, :], in_=ps_f[:, 0:1])
                dve.wait_ge(prep_v, 7)
                dst_places(dve, prep_v, 8)
                dve.wait_ge(loaded_w, 16 * 2)
                v.tensor_tensor(out=w_diff[:, :, :], in0=raw_phi[:, :, :], in1=w_dst[:, :, :],
                                op=ALU.subtract).then_inc(prep_v, 1)
                dve.wait_ge(prep_v, 10)
                v.tensor_copy(out=w_src[0][:, :, :], in_=w_diff[:, :, :]).then_inc(prep_v, 1)
                dve.wait_ge(prep_v, 11)
                v.tensor_tensor(out=w_src[1][:, :, :], in0=w_diff[:, :, :], in1=w_src[0][:, :, :].bitcast(F32),
                                op=ALU.subtract)
                dve.wait_ge(loaded, 16 * (2 + 2 * C))
                v.tensor_tensor(out=bias_col[:, :], in0=b_col[:, 0, :], in1=b_col[:, 1, :], op=ALU.add)

            @block.tensor
            def _(pe):
                pe.wait_ge(loaded, 16)
                pe.wait_ge(prep_v, 2)
                turn_lists(range(2)).then_inc(prep_t, 1)
                pe.wait_ge(prep_v, 6)
                nc.tensor.matmul(ps_f[:, 0:1], ones[0:ER, :], fall_sum[:, :], start=True, stop=True).then_inc(prep_t, 1)

        o_iota = sem("o_iota")
        o_dst = sem("o_dst")
        o_early = sem("o_early")
        o_part = sem("o_part")
        o_v = sem("o_v")
        o_rank = sem("o_rank")
        o_stage = sem("o_stage")
        o_moved = sem("o_moved")
        o_near = sem("o_near")
        o_lists = sem("o_lists")
        o_t = sem("o_t")
        shares = [(a, min(E, a + SHARE)) for a in range(0, E, SHARE)]
        with nc.Block() as block:
            @block.sync
            def _(sp):
                with sp.If(sp.value_load(unsorted[0:1, 0:1]) > 0):
                    for q, (a, b) in enumerate(shares):
                        need(sp, o_part, q * EC)
                        sp.dma_start(every_dst[:, 0:b - a], dst[a:b].partition_broadcast(P)).then_inc(o_dst, 16)
                    sp.wait_ge(o_moved, EC * 3 * 16)
                    flat = [t.rearrange("n o -> (n o)") for t in sorted_lists]
                    sp.dma_start(d_now[:, :], flat[1][1:1 + EP].rearrange("(r c) -> r c", c=D)).then_inc(o_near, 16)
                    sp.dma_start(d_before[1:ER, :], flat[1][D:EP].rearrange("(r c) -> r c", c=D)).then_inc(o_near, 16)
                    sp.dma_start(d_before[0:1, 1:D], flat[1][1:D].rearrange("(r c) -> r c", r=1)).then_inc(o_near, 16)
                    for n in range(3):
                        sp.dma_start(ints[:, n, :, :], flat[n][1:1 + EP].rearrange("(h r c) -> r h c", h=2, c=P)
                                     ).then_inc(o_lists, 16)
                    store_masks(sp, masks_ready, masks_stored, 2)

            @block.gpsimd
            def _(pool):
                with pool.If(pool.value_load(unsorted[0:1, 0:1]) > 0):
                    nc.gpsimd.iota(every_edge[:, :], [[1, SHARE]], base=0, channel_multiplier=0,
                                   allow_small_or_imprecise_dtypes=True)
                    for q, (a, b) in enumerate(shares):
                        last = nc.gpsimd.iota(own_edge[:, q, :], [[P, EC]], base=-a, channel_multiplier=1,
                                              allow_small_or_imprecise_dtypes=True)
                    last.then_inc(o_iota, 1)
                    b_all = nc.gpsimd.to_reg(EP)
                    pool.wait_ge(o_rank, 1)
                    with pool.Fori(0, EC) as t:
                        for n, cols in enumerate((rank_int, src_cols, dst_cols, edge_cols)):
                            last = nc.gpsimd.tensor_copy(out=moved[:, n:n + 1], in_=cols[:, ds(t, 1)])
                        last.then_inc(o_stage, 1)
                        pool.wait_ge(o_stage, t + 1)
                        pool.sem_inc(carrier, 1)
                        for n in range(3):
                            nc.gpsimd.indirect_dma_start(
                                out=sorted_lists[n], out_offset=bass.IndirectOffsetOnAxis(ap=moved[:, 0:1], axis=0),
                                in_=moved[:, n + 1:n + 2], in_offset=None, bounds_check=b_all,
                                oob_is_err=False).then_inc(o_moved, 16)
                        pool.wait_ge(o_moved, (t + 1) * (3 * 16))
                        pool.sem_inc(carrier, 1)

            @block.tensor
            def _(pe):
                with pe.If(pe.value_load(unsorted[0:1, 0:1]) > 0):
                    pe.wait_ge(o_t, 1)
                    turn_lists(range(3)).then_inc(o_t, 1)

            @block.vector
            def _(dve):
                v = nc.vector
                with dve.If(dve.value_load(unsorted[0:1, 0:1]) > 0):
                    v.tensor_copy(out=dst_f[:, :], in_=dst_cols[:, :]).then_inc(o_v, 1)
                    dve.wait_ge(o_v, 1)
                    dve.wait_ge(o_iota, 1)
                    for q, (a, b) in enumerate(shares):
                        dve.wait_ge(o_dst, (q + 1) * 16)
                        with dve.Fori(0, EC) as t:
                            v.tensor_scalar(out=earlier[:, 0:b - a], in0=every_edge[:, 0:b - a],
                                            scalar1=own_edge[:, q, ds(t, 1)], scalar2=0.5, op0=ALU.is_lt,
                                            op1=ALU.mult).then_inc(o_early, 1)
                            dve.wait_ge(o_early, t + (q * EC + 1))
                            v.scalar_tensor_tensor(out=precedes[:, 0:b - a], in0=every_dst[:, 0:b - a],
                                                   scalar=dst_f[:, ds(t, 1)], in1=earlier[:, 0:b - a],
                                                   op0=ALU.subtract, op1=ALU.is_lt,
                                                   accum_out=part_rank[:, ds(t, 1), q]).then_inc(o_part, 1)
                            dve.wait_ge(o_part, t + (q * EC + 1))
                    v.tensor_scalar(out=rank_pad[:, :], in0=own_edge[:, 0, :], scalar1=float(E), scalar2=None,
                                    op0=ALU.is_ge).then_inc(o_v, 1)
                    dve.wait_ge(o_v, 2)
                    v.tensor_tensor(out=rank_pad[:, :], in0=rank_pad[:, :], in1=own_edge[:, 0, :], op=ALU.mult)
                    v.tensor_reduce(out=rank[:, :], in_=part_rank[:, :, :], axis=AX.X, op=ALU.add).then_inc(o_v, 1)
                    dve.wait_ge(o_v, 3)
                    v.tensor_tensor(out=rank[:, :], in0=rank[:, :], in1=rank_pad[:, :], op=ALU.max).then_inc(o_v, 1)
                    dve.wait_ge(o_v, 4)
                    v.tensor_scalar(out=rank_int[:, :], in0=rank[:, :], scalar1=1.0, scalar2=None,
                                    op0=ALU.add).then_inc(o_rank, 1)
                    dve.wait_ge(o_lists, 3 * 16)
                    v.tensor_copy(out=floats[:, :, :, :], in_=ints[:, :, :, :]).then_inc(o_t, 1)
                    dve.wait_ge(o_near, 3 * 16)
                    list_masks(dve, o_v, 5, masks_ready)
                    dve.wait_ge(o_t, 2)
                    v.tensor_copy(out=src_cols[:, :], in_=ps_i[:, 0, 0:EC])
                    v.tensor_copy(out=edge_cols[:, :], in_=ps_i[:, 2, 0:EC])
                    v.tensor_copy(out=dst_cols[:, :], in_=ps_i[:, 1, 0:EC]).then_inc(o_v, 1)
                    dve.wait_ge(o_v, 7)
                    dst_places(dve, o_v, 8)
        small.close()

        phase_init = sem("phase_init")

        def stage_indices(pool, cols, w, tiles, ring, done, staged, rings=1):
            if w.k % GROUP == 0:
                n = min(GROUP, tiles - w.k) if w.base is None else GROUP
                at = w.slot(2 * GROUP)
                for g in range(n):
                    need(pool, done[(w.k + g) % 4], (w.turn(4) + (1 - GROUP // 2)) * (16 * J))
                nc.gpsimd.tensor_copy(out=idx[:, ring, at * J:(at + n) * J], in_=cols[:, ds(w.t * J, n * J)]
                                      ).then_inc(staged, 1)
                pool.wait_ge(staged, w.turn(GROUP) * rings + (ring + 1))
            pool.sem_inc(carrier, 1)

        def gather(table, bound, dest, w, ring, done):
            for j in range(J):
                at = w.slot(2 * GROUP) * J + j
                nc.gpsimd.indirect_dma_start(
                    out=dest[:, w.slot(4), j, :], out_offset=None, in_=table,
                    in_offset=bass.IndirectOffsetOnAxis(ap=idx[:, ring, at:at + 1], axis=0),
                    bounds_check=bound, oob_is_err=False).then_inc(done[w.slot(4)], 16)

        def landed(eng, done, w, transfers=1, extra=0):
            eng.wait_ge(done[w.slot(4)], (w.turn(4) + 1) * (16 * transfers) + extra)

        def slot_free(eng, done, w):
            need(eng, done[w.slot(4)], w.turn(4) * 16)

        def all_stored(eng, done, tiles, extra=0, slots=4):
            for s in range(slots):
                more = extra if (tiles - 1) % 4 == s else 0
                eng.wait_ge(done[s], ((tiles + 3 - s) // 4) * 16 + more)

        def transpose_rows(rows, dest, c, n):
            for j in range(J):
                last = nc.tensor.transpose(dest[:, c, j * P:j * P + n], rows[0:n, j, c * P:(c + 1) * P],
                                           ident[0:n, 0:n])
            return last

        def transpose_back(cols, dest, c, n):
            for j in range(J):
                last = nc.tensor.transpose(dest[0:n, j, c * P:(c + 1) * P], cols[:, c, j * P:j * P + n],
                                           ident[:, :])
            return last

        def low_part(dest, whole, high):
            return nc.vector.tensor_tensor(out=dest, in0=whole, in1=high.bitcast(F32), op=ALU.subtract)

        PRODUCTS = ((0, 0), (0, 1), (1, 0))

        def part(cols, c, n):
            if n == P:
                return cols[:, c, :]
            return cols[:, c, :].rearrange("p (j n) -> p j n", j=J)[:, :, 0:n]

        def ring_sems(name):
            return [sem(f"{name}{s}") for s in range(4)]

        p_x = ring_sems("p_x")
        p1_mem = ExitStack()
        p1_x = sb("p1_x", [P, 4, J, D], at=p1_mem)
        a_idx = sem("a_idx")
        a_src = ring_sems("a_src")
        a_cap = ring_sems("a_cap")
        a_st = ring_sems("a_st")
        a_iota = sem("a_iota")
        a_xt = sem("a_xt")
        a_xtc = sem("a_xtc")
        a_xlo = sem("a_xlo")
        a_b = sem("a_b")
        a_bc = sem("a_bc")
        a_scan = sem("a_scan")
        a_back = sem("a_back")
        a_rows = sem("a_rows")
        a_hot = sem("a_hot")
        a_cnt = sem("a_cnt")
        c_v = sem("c_v")
        c_t = sem("c_t")
        mem = ExitStack()
        with mem, nc.Block() as block:
            iota_q = sb("iota_q", [P, NQ], at=mem)
            iota_p = sb("iota_p", [P, P], at=mem)
            xs = sb("xs", [P, 4, J, D], at=mem)
            xt = [sb(f"xt{k}", [P, 2, C, TILE], F32R, at=mem) for k in range(2)]
            bt = sb("bt", [P, 2, C, TILE], at=mem)
            caps = sb("caps", [P, 4, TILE], BF16, at=mem)
            mx = sb("mx", [P, 2, C, TILE], at=mem)
            rows = sb("rows", [P, 4, J, D], at=mem)
            hot_q = sb("hot_q", [P, 2, J, NQ], BF16, at=mem)
            hot_p = sb("hot_p", [P, 2, J, P], BF16, at=mem)
            sums = sb("sums", [P, 3, NT], at=mem)
            ends = sb("ends", [P, NQ], at=mem)
            places = sb("places", [P, 3, NQ], I32, at=mem)
            ps_x = ps("ps_x", [P, C, TILE], mem)
            ps_b = ps("ps_b", [P, C, TILE], mem)
            ps_r = ps("ps_r", [P, J, D], mem)
            ps_n = ps("ps_n", [P, 512], mem)

            @block.gpsimd
            def _(pool):
                nc.gpsimd.iota(iota_q[:, :], [[1, NQ]], base=0, channel_multiplier=0,
                               allow_small_or_imprecise_dtypes=True)
                nc.gpsimd.iota(iota_p[:, :], [[1, P]], base=0, channel_multiplier=0,
                               allow_small_or_imprecise_dtypes=True).then_inc(a_iota, 1)
                b_x = nc.gpsimd.to_reg(N - 1)

                def gather_src(w):
                    need(pool, a_xt, (w.t - 3) * C)
                    stage_indices(pool, src_cols, w, ET, 0, a_src, a_idx)
                    gather(x, b_x, xs, w, 0, a_src)

                pipelined(pool, ET, [(0, gather_src)])

            @block.sync
            def _(sp):
                def load_caps(w):
                    need(sp, a_scan, (w.t - 3) * C)
                    sp.dma_start(caps[:, w.slot(4), :], cap_row[ds(w.t * TILE, TILE)].partition_broadcast(P)
                                 ).then_inc(a_cap[w.slot(4)], 16)

                pipelined(sp, ET, [(0, load_caps)])

                for t in range(4):
                    sp.dma_start(p1_x[:, t, :, :], node_rows(x, t, False)).then_inc(p_x[t], 16)
                for dest, w in ((wl, w_loop), (wi, w_in), (idft_sb, idft_t)):
                    sp.dma_start(dest[:, :, :], chunks(w)).then_inc(loaded_w, 16)
                for c in range(C):
                    win = bass.AP(loop_rel2.tensor, c * P, [[1, P], [1, D]])
                    sp.dma_start(hankel[:, c, :], win).then_inc(loaded_w, 16)
                sp.dma_start(dft_sb[:, :, :], dft).then_inc(loaded_w, 16)
                sp.dma_start(sig[:, :], sigma).then_inc(loaded_w, 16)
                for dest, v in ((wb_col, w_bias), (gam_col, bn_gamma), (bet_col, bn_beta)):
                    load_column(sp, dest, v, loaded_w)

            @block.tensor
            def _(pe):
                def turn(w):
                    landed(pe, a_src, w, J)
                    need(pe, a_xlo, w.t * C)
                    for c in range(C):
                        transpose_rows(xs[:, w.slot(4), :, :], ps_x, c, P).then_inc(a_xt, 1)

                def project(w):
                    for m in range(C):
                        need(pe, a_bc, (w.t - 1) * C + m + 1)
                        pe.wait_ge(a_xlo, (w.t + 1) * C)
                        for k, (kw, kx) in enumerate(PRODUCTS):
                            for c in range(C):
                                mm = nc.tensor.matmul(ps_b[:, m, :], w_src[kw][:, c, m * P:(m + 1) * P],
                                                      xt[kx][:, w.slot(2), c, :], start=(k + c == 0),
                                                      stop=(k == 2 and c == C - 1))
                        mm.then_inc(a_b, 1)

                def count(w):
                    pe.wait_ge(a_hot, w.t + 1)
                    for j in range(J):
                        mm = nc.tensor.matmul(ps_n[:, 0:NQ], hot_p[:, w.slot(2), j, :], hot_q[:, w.slot(2), j, :],
                                              start=(w.base is None and w.k == 0 and j == 0),
                                              stop=(w.last and j == J - 1))
                    mm.then_inc(a_cnt, 1)

                def back(w):
                    need(pe, a_rows, w.t * 2)
                    pe.wait_ge(a_scan, (w.t + 1) * C)
                    for c in range(C):
                        mm = transpose_back(mx[:, w.slot(2), :, :], ps_r, c, P)
                    mm.then_inc(a_back, 1)

                pipelined(pe, ET, [(0, turn), (1, project), (1, count), (3, back)])
                pe.wait_ge(c_v, 2)
                nc.tensor.matmul(ps_x[:, 0, 0:NT], ones[:, :], sums[:, 0, :], start=True, stop=True)
                nc.tensor.matmul(ps_x[:, 1, 0:NT], up[:, :], sums[:, 0, :], start=True,
                                 stop=True).then_inc(c_t, 1)

            @block.scalar
            def _(act):
                def copy_xt(w):
                    need(act, a_b, (w.t - 1) * C)
                    for c in range(C):
                        act.wait_ge(a_xt, w.t * C + c + 1)
                        nc.scalar.activation(xt[0][:, w.slot(2), c, :], ps_x[:, c, :], ACT.Copy).then_inc(a_xtc, 1)

                def add_bias(w):
                    need(act, a_scan, (w.t - 1) * C)
                    for m in range(C):
                        act.wait_ge(a_b, w.t * C + m + 1)
                        nc.scalar.activation(bt[:, w.slot(2), m, :], ps_b[:, m, :], ACT.Identity,
                                             bias=bias_col[:, m:m + 1]).then_inc(a_bc, 1)

                def copy_rows(w):
                    slot_free(act, a_st, w)
                    act.wait_ge(a_back, w.t + 1)
                    for k in range(2):
                        nc.scalar.activation(rows[:, w.slot(4), 2 * k:2 * k + 2, :], ps_r[:, 2 * k:2 * k + 2, :],
                                             ACT.Copy).then_inc(a_rows, 1)

                def store_rows(w):
                    act.wait_ge(a_rows, (w.t + 1) * 2)
                    act.dma_start(edge_rows(max_rows, w.t), rows[:, w.slot(4), :, :]).then_inc(a_st[w.slot(4)], 16)

                pipelined(act, ET, [(0, copy_xt), (1, add_bias), (3, copy_rows), (4, store_rows)])
                all_stored(act, a_st, ET)

            @block.vector
            def _(dve):
                v = nc.vector
                v.memset(mx[:, 1, :, TILE - 1:TILE], -HUGE).then_inc(phase_init, 1)
                dve.wait_ge(phase_init, 1)
                dve.wait_ge(a_iota, 1)

                def one_hots(w):
                    need(dve, a_cnt, w.t - 1)
                    for j in range(J):
                        col = w.t * J + j
                        v.tensor_scalar(out=hot_q[:, w.slot(2), j, :], in0=iota_q[:, :],
                                        scalar1=dst_q[:, ds(col, 1)], scalar2=None, op0=ALU.is_equal)
                        a = v.tensor_scalar(out=hot_p[:, w.slot(2), j, :], in0=iota_p[:, :],
                                            scalar1=dst_p[:, ds(col, 1)], scalar2=None, op0=ALU.is_equal)
                    a.then_inc(a_hot, 1)

                def low_xt(w):
                    need(dve, a_b, (w.t - 1) * C)
                    for c in range(C):
                        dve.wait_ge(a_xtc, w.t * C + c + 1)
                        low_part(xt[1][:, w.slot(2), c, :], ps_x[:, c, :], xt[0][:, w.slot(2), c, :]).then_inc(a_xlo, 1)

                def running_max(w):
                    need(dve, a_back, w.t - 1)
                    need(dve, a_scan, w.t * C)
                    landed(dve, a_cap, w)
                    for m in range(C):
                        dve.wait_ge(a_bc, w.t * C + m + 1)
                        v.tensor_tensor_scan(out=mx[:, w.slot(2), m, :], data0=caps[:, w.slot(4), :],
                                             data1=bt[:, w.slot(2), m, :],
                                             initial=mx[:, 1 - w.slot(2), m, TILE - 1:TILE], op0=ALU.min,
                                             op1=ALU.max).then_inc(a_scan, 1)

                pipelined(dve, ET, [(0, low_xt), (2, running_max), (0, one_hots)])

                done = [0]

                def link(ins):
                    done[0] += 1
                    ins.then_inc(c_v, 1)
                    dve.wait_ge(c_v, done[0])

                tot, every, base = (sums[:, k, :] for k in range(3))
                e4 = ends[:, :].rearrange("p (i j) -> p i j", j=J)
                d4 = deg[:, :].rearrange("p (i j) -> p i j", j=J)
                i_a, i_b, i_c = (places[:, k, :] for k in range(3))
                dve.wait_ge(a_cnt, ET)
                link(v.tensor_copy(out=deg[:, :], in_=ps_n[:, 0:NQ]))
                link(v.tensor_reduce(out=tot, in_=d4, axis=AX.X, op=ALU.add))
                dve.wait_ge(c_t, 1)
                link(v.tensor_tensor_scan(out=every, data0=ones[:, 0:NT], data1=ps_x[:, 0, 0:NT], initial=0.0,
                                          op0=ALU.mult, op1=ALU.add))
                link(v.tensor_tensor(out=every, in0=every, in1=ps_x[:, 0, 0:NT], op=ALU.subtract))
                link(v.tensor_tensor(out=base, in0=every, in1=ps_x[:, 1, 0:NT], op=ALU.add))
                link(v.tensor_scalar(out=base, in0=base, scalar1=1.0, scalar2=None, op0=ALU.subtract))
                link(v.tensor_tensor(out=e4[:, :, 0], in0=base, in1=d4[:, :, 0], op=ALU.add))
                for j in range(1, J):
                    link(v.tensor_tensor(out=e4[:, :, j], in0=e4[:, :, j - 1], in1=d4[:, :, j], op=ALU.add))
                link(v.tensor_scalar(out=i_a, in0=ends[:, :], scalar1=0.0, scalar2=None, op0=ALU.max))
                link(v.tensor_scalar(out=i_b, in0=i_a, scalar1=9, scalar2=9, op0=ALU.logical_shift_right,
                                     op1=ALU.logical_shift_left))
                link(v.tensor_scalar(out=i_c, in0=i_a, scalar1=P - 1, scalar2=2, op0=ALU.bitwise_and,
                                     op1=ALU.logical_shift_left))
                link(v.tensor_tensor(out=i_b, in0=i_b, in1=i_c, op=ALU.bitwise_or))
                link(v.tensor_scalar(out=i_c, in0=i_a, scalar1=7, scalar2=J - 1, op0=ALU.logical_shift_right,
                                     op1=ALU.bitwise_and))
                link(v.tensor_tensor(out=i_b, in0=i_b, in1=i_c, op=ALU.bitwise_or))
                link(v.tensor_scalar(out=i_c, in0=deg[:, :], scalar1=0.0, scalar2=float(MISSING),
                                     op0=ALU.is_equal, op1=ALU.mult))
                link(v.tensor_tensor(out=ptr[:, :], in0=i_b, in1=i_c, op=ALU.bitwise_or))

        def half_statistics(y, s6, n):
            for j in range(J):
                ins = nc.vector.bn_stats(out=s6[0:n, j, :], in_=y[0:n, j, :])
            return ins

        def moments(s6, ms, n):
            for j in range(J):
                ins = nc.vector.bn_aggr(out=ms[0:n, j, :], in_=s6[0:n, j, :])
            return ins

        p_idx = sem("p_idx")
        p_clear = sem("p_clear")
        p_mg = ring_sems("p_mg")
        p_st = ring_sems("p_st")
        p_xt = sem("p_xt")
        p_xtc = sem("p_xtc")
        p_a = sem("p_a")
        p_sum = sem("p_sum")
        p_res = sem("p_res")
        p_s6 = sem("p_s6")
        p_var = sem("p_var")
        p_sd = sem("p_sd")
        p_rs = sem("p_rs")
        p_nb = sem("p_nb")
        p_y = sem("p_y")
        mem = ExitStack()
        with mem, nc.Block() as block:
            mg = sb("mg", [P, 4, J, D], at=mem)
            no_edges = sb("no_edges", [P, J, D], at=mem)
            xt = sb("p_xt_sb", [P, 2, C, TILE], at=mem)
            total = sb("total", [P, 2, J, D], at=mem)
            res = sb("res", [P, 4, J, D], at=mem)
            yo = sb("yo", [P, 4, J, D], at=mem)
            s6 = sb("s6", [P, 2, J, 6], at=mem)
            ms = sb("ms", [P, 4, J, 2], at=mem)
            sd = sb("sd", [P, 2, J], at=mem)
            rs = sb("rs", [P, 2, J], at=mem)
            nb = sb("nb", [P, 2, J], at=mem)
            ps_x = ps("p_ps_x", [P, 2, C, TILE], mem)
            ps_a = ps("p_ps_a", [P, 2, J, D], mem)

            @block.gpsimd
            def _(pool):
                b_max = nc.gpsimd.to_reg(EP - 1)

                def gather_max(w):
                    pool.wait_ge(p_clear, w.t + 1)
                    stage_indices(pool, ptr, w, NT, 0, p_mg, p_idx)
                    gather(max_rows, b_max, mg, w, 0, p_mg)

                pipelined(pool, NT, [(0, gather_max)])

            @block.sync
            def _(sp):
                def load_x(w):
                    if w.base is None and w.t < 4:
                        return
                    n = TP if w.last else P
                    need(sp, p_res, w.t - 3)
                    sp.dma_start(p1_x[0:n, w.slot(4), :, :], node_rows(x, w.t, w.last)).then_inc(p_x[w.slot(4)], 16)

                pipelined(sp, NT, [(0, load_x)])

            @block.tensor
            def _(pe):
                def turn(w):
                    n = TP if w.last else P
                    landed(pe, p_x, w)
                    need(pe, p_xtc, (w.t - 1) * C)
                    for c in range(C):
                        transpose_rows(p1_x[:, w.slot(4), :, :], ps_x[:, w.slot(2), :, :], c, n).then_inc(p_xt, 1)

                def project(w):
                    n = TP if w.last else P
                    need(pe, p_sum, w.t - 1)
                    pe.wait_ge(p_xtc, (w.t + 1) * C)
                    for j in range(J):
                        for c in range(C):
                            mm = nc.tensor.matmul(ps_a[0:n, w.slot(2), j, :], xt[:, w.slot(2), c, j * P:j * P + n],
                                                  w_dst[:, c, :], start=(c == 0), stop=(c == C - 1))
                    mm.then_inc(p_a, 1)

                pipelined(pe, NT, [(0, turn), (1, project)])

            @block.scalar
            def _(act):
                act.wait_ge(phase_init, 2)

                def clear(w):
                    need(act, p_sum, w.t - 3)
                    nc.scalar.activation(mg[:, w.slot(4), :, :], no_edges[:, :, :], ACT.Copy).then_inc(p_clear, 1)

                def copy_xt(w):
                    n = TP if w.last else P
                    need(act, p_a, w.t - 1)
                    for c in range(C):
                        act.wait_ge(p_xt, w.t * C + c + 1)
                        nc.scalar.activation(part(xt[:, w.slot(2), :, :], c, n),
                                             part(ps_x[:, w.slot(2), :, :], c, n), ACT.Copy).then_inc(p_xtc, 1)

                def root(w):
                    n = TP if w.last else P
                    act.wait_ge(p_var, w.t + 1)
                    need(act, p_rs, w.t - 1)
                    nc.scalar.activation(sd[0:n, w.slot(2), :], ms[0:n, w.slot(4), :, 1], ACT.Sqrt,
                                         bias=eps_col[0:n, :]).then_inc(p_sd, 1)

                def normalise(w):
                    n = TP if w.last else P
                    s = w.slot(2)
                    slot_free(act, p_st, w)
                    act.wait_ge(p_nb, w.t + 1)
                    for j in range(J):
                        a = nc.scalar.activation(yo[0:n, w.slot(4), j, :], res[0:n, w.slot(4), j, :], ACT.Identity,
                                                 bias=nb[0:n, s, j:j + 1], scale=rs[0:n, s, j:j + 1])
                    a.then_inc(p_y, 1)

                def store_x1(w):
                    n = TP if w.last else P
                    act.wait_ge(p_y, w.t + 1)
                    act.dma_start(node_rows(x1, w.t, w.last), yo[0:n, w.slot(4), :, :]).then_inc(p_st[w.slot(4)], 16)

                pipelined(act, NT, [(0, clear), (2, copy_xt), (5, root), (6, normalise), (7, store_x1)])
                all_stored(act, p_st, NT)

            @block.vector
            def _(dve):
                v = nc.vector
                v.memset(no_edges[:, :, :], -HUGE).then_inc(phase_init, 1)

                def add_max(w):
                    n = TP if w.last else P
                    landed(dve, p_mg, w, J)
                    dve.wait_ge(p_a, w.t + 1)
                    need(dve, p_res, w.t - 1)
                    v.tensor_tensor(out=total[0:n, w.slot(2), :, :], in0=mg[0:n, w.slot(4), :, :],
                                    in1=ps_a[0:n, w.slot(2), :, :], op=ALU.add).then_inc(p_sum, 1)

                def relu_add(w):
                    n = TP if w.last else P
                    dve.wait_ge(p_sum, w.t + 1)
                    need(dve, p_y, w.t - 3)
                    v.scalar_tensor_tensor(out=res[0:n, w.slot(4), :, :], in0=total[0:n, w.slot(2), :, :], scalar=0.0,
                                           in1=p1_x[0:n, w.slot(4), :, :], op0=ALU.max, op1=ALU.add).then_inc(p_res, 1)

                def statistics(w):
                    n = TP if w.last else P
                    dve.wait_ge(p_res, w.t + 1)
                    need(dve, p_var, w.t - 1)
                    half_statistics(res[:, w.slot(4), :, :], s6[:, w.slot(2), :, :], n).then_inc(p_s6, 1)

                def variance(w):
                    n = TP if w.last else P
                    dve.wait_ge(p_s6, w.t + 1)
                    need(dve, p_nb, w.t - 3)
                    dve.sem_inc(carrier, 1)
                    moments(s6[:, w.slot(2), :, :], ms[:, w.slot(4), :, :], n).then_inc(p_var, 1)

                def scales(w):
                    n = TP if w.last else P
                    dve.wait_ge(p_sd, w.t + 1)
                    need(dve, p_y, w.t - 1)
                    v.reciprocal(out=rs[0:n, w.slot(2), :], in_=sd[0:n, w.slot(2), :]).then_inc(p_rs, 1)
                    dve.wait_ge(p_rs, w.t + 1)
                    v.scalar_tensor_tensor(out=nb[0:n, w.slot(2), :], in0=ms[0:n, w.slot(4), :, 0], scalar=-1.0,
                                           in1=rs[0:n, w.slot(2), :], op0=ALU.mult, op1=ALU.mult).then_inc(p_nb, 1)

                pipelined(dve, NT, [(1, add_max), (2, variance), (1, relu_add), (3, scales), (1, statistics)])

        p1_mem.close()

        b_idx = sem("b_idx")
        b_w = sem("b_w")
        b_ws = sem("b_ws")
        b_xs = ring_sems("b_xs")
        b_es = ring_sems("b_es")
        b_kp = ring_sems("b_kp")
        b_st = ring_sems("b_st")
        b_xt = sem("b_xt")
        b_et = sem("b_et")
        b_xh = sem("b_xh")
        b_eh = sem("b_eh")
        b_xf = sem("b_xf")
        b_ef = sem("b_ef")
        b_fx = sem("b_fx")
        b_fe = sem("b_fe")
        b_fxc = sem("b_fxc")
        b_fec = sem("b_fec")
        b_prod = sem("b_prod")
        b_z = sem("b_z")
        b_sc = sem("b_sc")
        b_zh = sem("b_zh")
        b_zl = sem("b_zl")
        b_msg = sem("b_msg")
        b_rows = sem("b_rows")
        mem = ExitStack()
        with mem, nc.Block() as block:
            xs = sb("b_xs_sb", [P, 4, J, D], at=mem)
            es = sb("b_es_sb", [P, 4, J, D], at=mem)
            upper_x = sb("upper_x", [P, TILE], at=mem)
            upper_e = sb("upper_e", [P, TILE], at=mem)
            fold_x = sb("fold_x", [P, 2, 2, TILE], at=mem)
            fold_e = sb("fold_e", [P, 2, 2, TILE], at=mem)
            fx = sb("fx", [P, 2, 2, TILE], at=mem)
            fe = sb("fe", [P, 2, 2, TILE], at=mem)
            prod = sb("prod", [P, 2, 4, TILE], at=mem)
            z = sb("z", [P, 2, C, TILE], at=mem)
            zs = sb("zs", [P, 2, C, TILE], at=mem)
            zp = [sb(f"zs{k}", [P, 2, C, TILE], F32R, at=mem) for k in range(2)]
            keeps = sb("keeps", [P, 4, TILE], BF16, at=mem)
            rows = sb("b_rows_sb", [P, 4, J, D], at=mem)
            ps_x = ps("b_ps_x", [P, C, TILE], mem)
            ps_e = ps("b_ps_e", [P, C, TILE], mem)
            ps_f = ps("b_ps_f", [P, 2, TILE], mem)
            ps_m = ps("ps_m", [P, J, D], mem)

            @block.gpsimd
            def _(pool):
                b_x1 = nc.gpsimd.to_reg(N - 1)
                b_edge = nc.gpsimd.to_reg(E - 1)

                def gather_nodes(w, rings):
                    need(pool, b_xt, w.t - 3)
                    stage_indices(pool, src_cols, w, ET, 0, b_xs, b_idx, rings)
                    gather(x1, b_x1, xs, w, 0, b_xs)

                def gather_both(w):
                    gather_nodes(w, 2)
                    need(pool, b_et, w.t - 3)
                    stage_indices(pool, edge_cols, w, ET, 1, b_es, b_idx, 2)
                    gather(edge_attr, b_edge, es, w, 1, b_es)

                def combine(w):
                    s = w.slot(2)
                    pool.wait_ge(b_prod, w.t + 1)
                    need(pool, b_sc, (w.t - 1) * C)
                    for m, sign in ((0, ALU.add), (1, ALU.subtract)):
                        nc.gpsimd.tensor_tensor(out=z[:, s, m, :], in0=prod[:, s, 2 * m, :],
                                                in1=prod[:, s, 2 * m + 1, :], op=sign).then_inc(b_z, 1)

                with pool.If(pool.value_load(unsorted[0:1, 0:1]) > 0):
                    pipelined(pool, ET, [(6, combine), (0, gather_both)])
                with pool.Else():
                    pipelined(pool, ET, [(6, combine), (0, lambda w: gather_nodes(w, 1))])

            @block.sync
            def _(sp):
                def load_edges(w):
                    need(sp, b_et, w.t - 3)
                    for j in range(J):
                        n = max(1, min(P, E - ((ET - 1) * TILE + j * P))) if w.last else P
                        at = min(E - 1, w.t * TILE + j * P) if w.last else w.t * TILE + j * P
                        sp.dma_start(es[0:n, w.slot(4), j, :], edge_attr[ds(at, n), :]).then_inc(b_es[w.slot(4)], 16)

                with sp.If(sp.value_load(unsorted[0:1, 0:1]) < 1):
                    pipelined(sp, ET, [(0, load_edges)])

            @block.tensor
            def _(pe):
                pe.wait_ge(loaded_w, 16 * (7 + 4 * C))
                for n, (left, right) in enumerate(((hankel, wl), (idft_sb, wi))):
                    for m in range(C):
                        for c in range(C):
                            last = nc.tensor.matmul(ps_m[:, n * C + m, :], left[:, c, m * P:(m + 1) * P],
                                                    right[:, c, :], start=(c == 0), stop=(c == C - 1))
                    last.then_inc(b_w, 1)

                def turn_x(w):
                    landed(pe, b_xs, w, J)
                    need(pe, b_xf, w.t)
                    for c in range(C):
                        mm = transpose_rows(xs[:, w.slot(4), :, :], ps_x, 1 - c, P)
                    mm.then_inc(b_xt, 1)

                def turn_e(w):
                    landed(pe, b_es, w, J)
                    need(pe, b_ef, w.t)
                    for c in range(C):
                        mm = transpose_rows(es[:, w.slot(4), :, :], ps_e, 1 - c, P)
                    mm.then_inc(b_et, 1)

                def dft_x(w):
                    pe.wait_ge(b_xf, w.t + 1)
                    for m in range(2):
                        need(pe, b_fec, w.t * 2 + m - 1)
                        nc.tensor.matmul(ps_f[:, m, :], dft_sb[:, m, :], fold_x[:, w.slot(2), m, :],
                                         start=True, stop=True).then_inc(b_fx, 1)

                def dft_e(w):
                    pe.wait_ge(b_ef, w.t + 1)
                    for m in range(2):
                        pe.wait_ge(b_fxc, w.t * 2 + m + 1)
                        nc.tensor.matmul(ps_f[:, m, :], dft_sb[:, m, :], fold_e[:, w.slot(2), m, :],
                                         start=True, stop=True).then_inc(b_fe, 1)

                def message(w):
                    if w.base is None and w.k == 0:
                        pe.wait_ge(b_ws, 4)
                    need(pe, b_rows, w.t * 2)
                    pe.wait_ge(b_zl, (w.t + 1) * C)
                    for j in range(J):
                        for k, (kw, kz) in enumerate(PRODUCTS):
                            for c in range(C):
                                mm = nc.tensor.matmul(ps_m[:, j, :], zp[kz][:, w.slot(2), c, j * P:(j + 1) * P],
                                                      w_msg[kw][:, c, :], start=(k + c == 0),
                                                      stop=(k == 2 and c == C - 1))
                    mm.then_inc(b_msg, 1)

                pipelined(pe, ET, [(0, turn_x), (1, dft_x), (0, turn_e), (5, message), (1, dft_e)])

            @block.scalar
            def _(act):
                def upper_half(w, source, turned, dest, folded, done):
                    act.wait_ge(turned, w.t + 1)
                    need(act, folded, w.t)
                    nc.scalar.activation(dest[:, :], source[:, 1, :], ACT.Copy).then_inc(done, 1)

                def upper_of_x(w):
                    upper_half(w, ps_x, b_xt, upper_x, b_xf, b_xh)

                def upper_of_e(w):
                    upper_half(w, ps_e, b_et, upper_e, b_ef, b_eh)

                def spectrum(w, transformed, dest, done):
                    need(act, b_prod, w.t - 1)
                    for m in range(2):
                        act.wait_ge(transformed, w.t * 2 + m + 1)
                        for part_of in range(2):
                            a = nc.scalar.activation(dest[m * H:(m + 1) * H, w.slot(2), part_of, :],
                                                     ps_f[part_of * H:(part_of + 1) * H, m, :], ACT.Copy)
                        a.then_inc(done, 1)

                def spectrum_x(w):
                    spectrum(w, b_fx, fx, b_fxc)

                def spectrum_e(w):
                    spectrum(w, b_fe, fe, b_fec)

                def load_keep(w):
                    need(act, b_sc, (w.t - 3) * C)
                    act.dma_start(keeps[:, w.slot(4), :], keep_row[ds(w.t * TILE, TILE)].partition_broadcast(P)
                                 ).then_inc(b_kp[w.slot(4)], 16)

                def high_sums(w):
                    need(act, b_msg, w.t - 1)
                    for m in range(C):
                        act.wait_ge(b_sc, w.t * C + m + 1)
                        nc.scalar.activation(zp[0][:, w.slot(2), m, :], zs[:, w.slot(2), m, :],
                                             ACT.Copy).then_inc(b_zh, 1)

                def copy_rows(w):
                    slot_free(act, b_st, w)
                    act.wait_ge(b_msg, w.t + 1)
                    for k in range(2):
                        nc.scalar.activation(rows[:, w.slot(4), 2 * k:2 * k + 2, :], ps_m[:, 2 * k:2 * k + 2, :],
                                             ACT.Copy).then_inc(b_rows, 1)

                def store_rows(w):
                    act.wait_ge(b_rows, (w.t + 1) * 2)
                    act.dma_start(edge_rows(agg_rows, w.t), rows[:, w.slot(4), :, :]).then_inc(b_st[w.slot(4)], 16)

                pipelined(act, ET, [(0, upper_of_x), (1, spectrum_x), (0, upper_of_e), (4, high_sums), (2, load_keep),
                                    (5, copy_rows), (1, spectrum_e), (6, store_rows)])
                all_stored(act, b_st, ET)

            @block.vector
            def _(dve):
                v = nc.vector
                v.memset(zs[:, 1, :, TILE - 1:TILE], 0.0).then_inc(phase_init, 1)
                dve.wait_ge(phase_init, 3)
                for n, w in enumerate((w_h, w_msg)):
                    whole = ps_m[:, n * C:(n + 1) * C, :]
                    dve.wait_ge(b_w, n + 1)
                    v.tensor_copy(out=w[0][:, :, :], in_=whole).then_inc(b_ws, 1)
                    dve.wait_ge(b_ws, 2 * n + 1)
                    low_part(w[1][:, :, :], whole, w[0][:, :, :]).then_inc(b_ws, 1)

                def fold(w, source, copied, upper_sb, dest, used, done):
                    dve.wait_ge(copied, w.t + 1)
                    need(dve, used, (w.t - 1) * 2)
                    v.tensor_tensor(out=dest[:, w.slot(2), 0, :], in0=source[:, 0, :], in1=upper_sb[:, :], op=ALU.add)
                    v.tensor_tensor(out=dest[:, w.slot(2), 1, :], in0=source[:, 0, :], in1=upper_sb[:, :],
                                    op=ALU.subtract).then_inc(done, 1)

                def fold_nodes(w):
                    fold(w, ps_x, b_xh, upper_x, fold_x, b_fx, b_xf)

                def fold_edges(w):
                    fold(w, ps_e, b_eh, upper_e, fold_e, b_fe, b_ef)

                def multiply(w):
                    s = w.slot(2)
                    dve.wait_ge(b_fxc, (w.t + 1) * 2)
                    dve.wait_ge(b_fec, (w.t + 1) * 2)
                    need(dve, b_z, (w.t - 1) * C)
                    v.tensor_tensor(out=prod[:, s, 0, :], in0=fx[:, s, 0, :], in1=fe[:, s, 0, :], op=ALU.mult)
                    v.tensor_tensor(out=prod[:, s, 1, :], in0=fx[:, s, 1, :], in1=fe[:, s, 1, :], op=ALU.mult)
                    v.tensor_tensor(out=prod[:, s, 2, :], in0=fx[:, s, 1, :], in1=fe[:, s, 0, :], op=ALU.mult)
                    v.scalar_tensor_tensor(out=prod[:, s, 3, :], in0=fx[:, s, 0, :], scalar=sig[:, 0:1],
                                           in1=fe[:, s, 1, :], op0=ALU.mult, op1=ALU.mult).then_inc(b_prod, 1)

                def running_sum(w):
                    landed(dve, b_kp, w)
                    need(dve, b_zl, (w.t - 1) * C)
                    for m in range(C):
                        dve.wait_ge(b_z, w.t * C + m + 1)
                        v.tensor_tensor_scan(out=zs[:, w.slot(2), m, :], data0=keeps[:, w.slot(4), :],
                                             data1=z[:, w.slot(2), m, :],
                                             initial=zs[:, 1 - w.slot(2), m, TILE - 1:TILE],
                                             op0=ALU.mult, op1=ALU.add).then_inc(b_sc, 1)

                def low_sums(w):
                    for m in range(C):
                        dve.wait_ge(b_zh, w.t * C + m + 1)
                        low_part(zp[1][:, w.slot(2), m, :], zs[:, w.slot(2), m, :], zp[0][:, w.slot(2), m, :]
                                 ).then_inc(b_zl, 1)

                pipelined(dve, ET, [(5, low_sums), (4, running_sum), (0, fold_nodes), (0, fold_edges), (2, multiply)])

        early.close()

        q_idx = sem("q_idx")
        q_ag = ring_sems("q_ag")
        q_x = ring_sems("q_x")
        q_st = ring_sems("q_st")
        q_xt = sem("q_xt")
        q_xtc = sem("q_xtc")
        q_xlo = sem("q_xlo")
        q_nrm = sem("q_nrm")
        q_h = sem("q_h")
        q_hc = sem("q_hc")
        q_bn = sem("q_bn")
        n_v = sem("n_v")
        n_s = sem("n_s")
        f_v = sem("f_v")
        f_s = sem("f_s")
        r_x = ring_sems("r_x")
        x_ring = sb("x_ring", [P, 4, J, D])
        kept_h = sb("kept_h", [P, (NT + 3) // 4, C, TILE])

        def is_kept(w):
            return w.slot(4) == 3

        def h_tile(ring, w):
            if is_kept(w):
                return kept_h[:, ds(w.turn(4), 1), :, :].rearrange("p o c n -> p (o c) n")
            return ring[:, w.slot(4), :, :]

        mem = ExitStack()
        with mem, nc.Block() as block:
            ag = sb("ag", [P, 4, J, D], at=mem)
            an = sb("an", [P, 2, J, D], at=mem)
            xt = [sb(f"q_xt{k}", [P, 2, C, TILE], F32R, at=mem) for k in range(2)]
            hs = sb("hs", [P, 3, C, TILE], at=mem)
            mv = sb("q_mv", [P, C, 2], at=mem)
            ps_x = ps("q_ps_x", [P, 2, C, TILE], mem)
            ps_h = ps("q_ps_h", [P, 2, C, TILE], mem)

            @block.gpsimd
            def _(pool):
                b_agg = nc.gpsimd.to_reg(EP - 1)

                def gather_agg(w):
                    need(pool, q_nrm, w.t - 3)
                    if w.base is None and w.t < 4:
                        pool.wait_ge(phase_init, 4 + w.t)
                    stage_indices(pool, ptr, w, NT, 0, q_ag, q_idx)
                    gather(agg_rows, b_agg, ag, w, 0, q_ag)

                pipelined(pool, NT, [(0, gather_agg)])

            @block.sync
            def _(sp):
                def load_x1(w):
                    n = TP if w.last else P
                    need(sp, q_xt, (w.t - 3) * C)
                    sp.dma_start(x_ring[0:n, w.slot(4), :, :], node_rows(x1, w.t, w.last)).then_inc(q_x[w.slot(4)], 16)

                pipelined(sp, NT, [(0, load_x1)])
                for t in range(4):
                    sp.wait_ge(q_xt, (NT - (NT - 1 - t) % 4) * C)
                    sp.dma_start(x_ring[:, t, :, :], node_rows(x1, t, False)).then_inc(r_x[t], 16)

            @block.tensor
            def _(pe):
                def turn(w):
                    n = TP if w.last else P
                    landed(pe, q_x, w)
                    need(pe, q_xlo, (w.t - 1) * C)
                    for c in range(C):
                        transpose_rows(x_ring[:, w.slot(4), :, :], ps_x[:, w.slot(2), :, :], c, n).then_inc(q_xt, 1)

                def project(w):
                    n = TP if w.last else P
                    s = w.slot(2)
                    need(pe, q_hc, (w.t - 1) * C)
                    pe.wait_ge(q_xlo, (w.t + 1) * C)
                    pe.wait_ge(q_nrm, w.t + 1)
                    for m in range(C):
                        for k, (kw, kx) in enumerate(PRODUCTS):
                            for c in range(C):
                                nc.tensor.matmul(part(ps_h[:, s, :, :], m, n), w_h[kw][:, c, m * P:(m + 1) * P],
                                                 part(xt[kx][:, s, :, :], c, n), start=(k + c == 0), stop=False)
                        for j in range(J):
                            mm = nc.tensor.matmul(ps_h[:, s, m, j * P:j * P + n],
                                                  an[0:n, s, j, m * P:(m + 1) * P], ident[0:n, 0:n],
                                                  is_transpose=True, start=False, stop=(j == J - 1))
                        mm.then_inc(q_h, 1)

                pipelined(pe, NT, [(0, turn), (1, project)])

            @block.scalar
            def _(act):
                act.wait_ge(n_v, 1)
                nc.scalar.activation(norm_node[:, :], norm_node[:, :], ACT.Sqrt).then_inc(n_s, 1)

                def copy_xt(w):
                    n = TP if w.last else P
                    need(act, q_h, (w.t - 1) * C)
                    for c in range(C):
                        act.wait_ge(q_xt, w.t * C + c + 1)
                        nc.scalar.activation(part(xt[0][:, w.slot(2), :, :], c, n),
                                             part(ps_x[:, w.slot(2), :, :], c, n), ACT.Copy).then_inc(q_xtc, 1)

                def add_bias(w):
                    n = TP if w.last else P
                    if not is_kept(w):
                        slot_free(act, q_st, w)
                    need(act, q_bn, (w.t - 3) * C)
                    for m in range(C):
                        act.wait_ge(q_h, w.t * C + m + 1)
                        nc.scalar.activation(part(h_tile(hs, w), m, n),
                                             part(ps_h[:, w.slot(2), :, :], m, n),
                                             ACT.Identity, bias=wb_col[:, m:m + 1]).then_inc(q_hc, 1)

                def store_h(w):
                    if is_kept(w):
                        return
                    act.wait_ge(q_hc, (w.t + 1) * C)
                    source = hs[:, w.slot(4), :, :]
                    dest = h_t[ds(w.t, 1), :, :].rearrange("o p n -> (o p) n")
                    if w.last:
                        for c in range(C):
                            act.dma_start(part(dest.rearrange("p (c n) -> p c n", c=C), c, TP),
                                          part(source, c, TP)).then_inc(q_st[w.slot(4)], 16)
                    else:
                        act.dma_start(dest, source.rearrange("p c n -> p (c n)")).then_inc(q_st[w.slot(4)], 16)

                pipelined(act, NT, [(0, copy_xt), (1, add_bias), (2, store_h)])
                all_stored(act, q_st, NT, (C - 1) * 16, 3)
                act.wait_ge(f_v, 1)
                nc.scalar.activation(bn_scale[:, :], mv[:, :, 1], ACT.Sqrt, bias=eps_col[:, :]).then_inc(f_s, 1)

            @block.vector
            def _(dve):
                v = nc.vector
                for k in range(4):
                    v.memset(ag[:, k, :, :], 0.0).then_inc(phase_init, 1)
                v.tensor_scalar(out=has_edges[:, :], in0=deg[:, :], scalar1=1.0, scalar2=None, op0=ALU.min)
                v.tensor_scalar(out=norm_node[:, :], in0=deg[:, :], scalar1=1.0, scalar2=None,
                                op0=ALU.max).then_inc(n_v, 1)
                dve.wait_ge(n_s, 1)
                v.reciprocal(out=norm_node[:, :], in_=norm_node[:, :]).then_inc(n_v, 1)
                dve.wait_ge(n_v, 2)
                v.tensor_tensor(out=norm_node[:, :], in0=norm_node[:, :], in1=has_edges[:, :],
                                op=ALU.mult).then_inc(n_v, 1)
                dve.wait_ge(n_v, 3)

                def low_xt(w):
                    n = TP if w.last else P
                    s = w.slot(2)
                    need(dve, q_h, (w.t - 1) * C)
                    for c in range(C):
                        dve.wait_ge(q_xtc, w.t * C + c + 1)
                        low_part(part(xt[1][:, s, :, :], c, n), part(ps_x[:, s, :, :], c, n),
                                 part(xt[0][:, s, :, :], c, n)).then_inc(q_xlo, 1)

                def scale_sum(w):
                    n = TP if w.last else P
                    landed(dve, q_ag, w, J)
                    need(dve, q_h, (w.t - 1) * C)
                    for j in range(J):
                        a = v.tensor_scalar(out=an[0:n, w.slot(2), j, :], in0=ag[0:n, w.slot(4), j, :],
                                            scalar1=norm_node[0:n, ds(w.t * J + j, 1)], scalar2=None, op0=ALU.mult)
                    a.then_inc(q_nrm, 1)

                def statistics(w):
                    n = TP if w.last else P
                    for m in range(C):
                        dve.wait_ge(q_hc, w.t * C + m + 1)
                        v.bn_stats(out=h_stats[:, m, ds(w.t * 6, 6)], in_=part(h_tile(hs, w), m, n)
                                   ).then_inc(q_bn, 1)

                pipelined(dve, NT, [(0, low_xt), (0, scale_sum), (2, statistics)])
                dve.wait_ge(q_bn, NT * C)
                for m in range(C):
                    a = v.bn_aggr(out=mv[:, m, :], in_=h_stats[:, m, :])
                a.then_inc(f_v, 1)
                dve.wait_ge(f_s, 1)
                v.reciprocal(out=bn_scale[:, :], in_=bn_scale[:, :]).then_inc(f_v, 1)
                dve.wait_ge(f_v, 2)
                v.tensor_tensor(out=bn_scale[:, :], in0=bn_scale[:, :], in1=gam_col[:, :], op=ALU.mult).then_inc(f_v, 1)
                dve.wait_ge(f_v, 3)
                v.tensor_tensor(out=bn_shift[:, :], in0=mv[:, :, 0], in1=bn_scale[:, :], op=ALU.mult).then_inc(f_v, 1)
                dve.wait_ge(f_v, 4)
                v.tensor_tensor(out=bn_shift[:, :], in0=bet_col[:, :], in1=bn_shift[:, :], op=ALU.subtract)

        r_h = ring_sems("r_h")
        r_st = ring_sems("r_st")
        r_th = sem("r_th")
        r_bk = sem("r_bk")
        r_sum = sem("r_sum")
        r_s6 = sem("r_s6")
        r_var = sem("r_var")
        r_ve = sem("r_ve")
        r_rs = sem("r_rs")
        r_nb = sem("r_nb")
        r_y = sem("r_y")
        mem = ExitStack()
        with mem, nc.Block() as block:
            ht = sb("ht", [P, 3, C, TILE], at=mem)
            th = sb("th", [P, 2, C, TILE], at=mem)
            res = sb("r_res", [P, 4, J, D], at=mem)
            yo = sb("r_yo", [P, 4, J, D], at=mem)
            s6 = sb("r_s6_sb", [P, 2, J, 6], at=mem)
            ms = sb("r_ms", [P, 4, J, 2], at=mem)
            ve = sb("ve", [P, 2, J], at=mem)
            rs = sb("r_rs_sb", [P, 2, J], at=mem)
            nb = sb("r_nb_sb", [P, 2, J], at=mem)
            mhalf = sb("mhalf", [P, J], at=mem)
            eps4 = sb("eps4", [P, J], at=mem)
            ps_y = ps("ps_y", [P, 2, J, D], mem)

            @block.sync
            def _(sp):
                def load(w):
                    n = TP if w.last else P
                    s = w.slot(4)
                    if not is_kept(w):
                        need(sp, r_th, w.t - 3)
                        source = h_t[ds(w.t, 1), :, :].rearrange("o p n -> (o p) n")
                        if w.last:
                            for c in range(C):
                                sp.dma_start(part(ht[:, s, :, :], c, TP),
                                             part(source.rearrange("p (c n) -> p c n", c=C), c, TP)
                                             ).then_inc(r_h[s], 16)
                        else:
                            sp.dma_start(ht[:, s, :, :].rearrange("p c n -> p (c n)"), source).then_inc(r_h[s], 16)
                    if w.base is None and w.t < 4:
                        return
                    need(sp, r_sum, (w.t - 3) * 2)
                    sp.dma_start(x_ring[0:n, s, :, :], node_rows(x1, w.t, w.last)).then_inc(r_x[s], 16)

                pipelined(sp, NT, [(0, load)])

            @block.scalar
            def _(act):
                def squash(w):
                    n = TP if w.last else P
                    if not is_kept(w):
                        landed(act, r_h, w, extra=16 * (C - 1) if w.last else 0)
                    need(act, r_bk, w.t - 1)
                    for m in range(C):
                        a = nc.scalar.activation(part(th[:, w.slot(2), :, :], m, n), part(h_tile(ht, w), m, n),
                                                 ACT.Tanh, bias=bn_shift[:, m:m + 1], scale=bn_scale[:, m:m + 1])
                    a.then_inc(r_th, 1)

                def normalise(w):
                    n = TP if w.last else P
                    s = w.slot(2)
                    slot_free(act, r_st, w)
                    act.wait_ge(r_nb, w.t + 1)
                    for j in range(J):
                        a = nc.scalar.activation(yo[0:n, w.slot(4), j, :], res[0:n, w.slot(4), j, :], ACT.Identity,
                                                 bias=nb[0:n, s, j:j + 1], scale=rs[0:n, s, j:j + 1])
                    a.then_inc(r_y, 1)

                def store(w):
                    n = TP if w.last else P
                    act.wait_ge(r_y, w.t + 1)
                    act.dma_start(node_rows(out, w.t, w.last), yo[0:n, w.slot(4), :, :]).then_inc(r_st[w.slot(4)], 16)

                pipelined(act, NT, [(0, squash), (4, normalise), (5, store)])
                all_stored(act, r_st, NT)

            @block.tensor
            def _(pe):
                def back(w):
                    n = TP if w.last else P
                    pe.wait_ge(r_th, w.t + 1)
                    need(pe, r_sum, (w.t - 1) * 2)
                    for c in range(C):
                        mm = transpose_back(th[:, w.slot(2), :, :], ps_y[:, w.slot(2), :, :], c, n)
                    mm.then_inc(r_bk, 1)

                pipelined(pe, NT, [(0, back)])

            @block.vector
            def _(dve):
                v = nc.vector
                v.memset(eps4[:, :], EPS)
                v.memset(mhalf[:, :], -0.5).then_inc(phase_init, 1)

                def add(w):
                    n = TP if w.last else P
                    s = w.slot(4)
                    dve.wait_ge(r_bk, w.t + 1)
                    landed(dve, r_x, w)
                    need(dve, r_y, w.t - 3)
                    for k in range(2):
                        v.tensor_tensor(out=res[0:n, s, 2 * k:2 * k + 2, :], in0=x_ring[0:n, s, 2 * k:2 * k + 2, :],
                                        in1=ps_y[0:n, w.slot(2), 2 * k:2 * k + 2, :], op=ALU.add).then_inc(r_sum, 1)

                def statistics(w):
                    n = TP if w.last else P
                    dve.wait_ge(r_sum, (w.t + 1) * 2)
                    need(dve, r_var, w.t - 1)
                    half_statistics(res[:, w.slot(4), :, :], s6[:, w.slot(2), :, :], n).then_inc(r_s6, 1)

                def variance(w):
                    n = TP if w.last else P
                    dve.wait_ge(r_s6, w.t + 1)
                    need(dve, r_nb, w.t - 3)
                    dve.sem_inc(carrier, 1)
                    moments(s6[:, w.slot(2), :, :], ms[:, w.slot(4), :, :], n).then_inc(r_var, 1)

                def shift(w):
                    n = TP if w.last else P
                    dve.wait_ge(r_rs, w.t + 1)
                    need(dve, r_y, w.t - 1)
                    v.scalar_tensor_tensor(out=nb[0:n, w.slot(2), :], in0=ms[0:n, w.slot(4), :, 0], scalar=-1.0,
                                           in1=rs[0:n, w.slot(2), :], op0=ALU.mult, op1=ALU.mult).then_inc(r_nb, 1)

                pipelined(dve, NT, [(1, add), (3, shift), (2, statistics), (2, variance)])

            @block.gpsimd
            def _(pool):
                pool.wait_ge(phase_init, 3 + 4 + 1)

                def rsqrt(w):
                    n = TP if w.last else P
                    s = w.slot(2)
                    pool.wait_ge(r_var, w.t + 1)
                    need(pool, r_rs, w.t - 1)
                    nc.gpsimd.tensor_tensor(out=ve[0:n, s, :], in0=ms[0:n, w.slot(4), :, 1], in1=eps4[0:n, :],
                                            op=ALU.add).then_inc(r_ve, 1)
                    pool.wait_ge(r_ve, w.t + 1)
                    need(pool, r_y, w.t - 1)
                    nc.gpsimd.tensor_tensor(out=rs[0:n, s, :], in0=ve[0:n, s, :], in1=mhalf[0:n, :],
                                            op=ALU.pow).then_inc(r_rs, 1)

                pipelined(pool, NT, [(0, rsqrt)])


def constants(d):
    import numpy as np
    n = np.arange(d)
    m = np.arange(d // 4)
    even, odd = (n % 2 == 0) * 1.0, (n % 2 == 1) * 1.0
    fwd = np.zeros((d // 2, 2, d // 2))
    cosines, sines = [], []
    for k in range(2):
        angle = 2 * np.pi * np.outer(n, 2 * m + k) / d
        cos, sin = np.cos(angle), np.sin(angle)
        if k == 0:
            cos[:, 0], sin[:, 0] = even, odd
        fwd[:, k, :] = np.concatenate([cos, sin], 1)[:d // 2]
        inv_cos, inv_sin = 2 * cos / d, -2 * sin / d
        if k == 0:
            inv_sin[:, 0] *= -1
        cosines.append(inv_cos)
        sines.append(inv_sin)
    sigma = np.ones((P, 1))
    sigma[0] = -1
    return {
        "identity": np.eye(P, dtype=np.float32),
        "upper": np.triu(np.ones((P, P), np.float32), 1),
        "dft": fwd.astype(np.float32),
        "idft_t": np.concatenate(cosines + sines, 1).astype(np.float32),
        "sigma": sigma.astype(np.float32),
    }


def lay_out(inputs):
    import numpy as np
    a = {k: np.asarray(v) for k, v in inputs.items()}
    rel = a["L1_gnn_loop_rel"][0]
    out = {
        "x": a["x"], "src": a["src"], "dst": a["dst"], "edge_attr": a["edge_attr_256"],
        "theta_t": a["L0_gnn_theta_w"].T, "theta_b": a["L0_gnn_theta_b"],
        "phi_t": a["L0_gnn_phi_w"].T, "phi_b": a["L0_gnn_phi_b"],
        "w_loop": a["L1_gnn_w_loop"], "w_in": a["L1_gnn_w_in"], "loop_rel2": np.concatenate([rel, rel]),
        "w_bias": a["L1_gnn_w_bias"], "bn_gamma": a["L1_gnn_bn_gamma"], "bn_beta": a["L1_gnn_bn_beta"],
    }
    out.update(constants(rel.shape[0]))
    return {k: np.ascontiguousarray(v) for k, v in out.items()}


def build(nc, arrays):
    args = [nc.dram_tensor(f"in_{k}", v.shape, mybir.dt.from_np(v.dtype), kind="ExternalInput").ap()
            for k, v in arrays.items()]
    out = nc.dram_tensor("out_0", arrays["x"].shape, F32, kind="ExternalOutput").ap()
    gnn_kernel(nc, *args, out)


def kernel(**inputs):
    import concourse.bacc as _bacc
    from concourse.bass_utils import run_bass_kernel_spmd as _run

    nc = _bacc.Bacc("TRN2", target_bir_lowering=False, num_devices=1)
    arrays = lay_out(inputs)
    build(nc, arrays)
    r = _run(nc, [{f"in_{k}": v for k, v in arrays.items()}], core_ids=[0])
    return r.results[0]["out_0"]
```
